# Optimizing a Trainium2 kernel written in Bass

```python
import numpy as np
import jax
import jax.numpy as jnp

def _softmax(x, axis=-1):
    return jax.nn.softmax(x, axis=axis)

def _gelu(x):
    return jax.nn.gelu(x, approximate=True)

def _silu(x):
    return jax.nn.silu(x)

def _sigmoid(x):
    return jax.nn.sigmoid(x)

def _layernorm(x, axis=-1, eps=1e-05):
    m = jnp.mean(x, axis=axis, keepdims=True)
    v = jnp.var(x, axis=axis, keepdims=True)
    return (x - m) / jnp.sqrt(v + eps)

def _scatter_add(tgt, idx, src, axis=0):
    return tgt.at[idx].add(src)

def _segment_sum(src, seg, n):
    return jax.ops.segment_sum(src, seg, n)
kernel_name = 'mk_gnn_preln_d4_gnn_r32_550aa0'

def setup_inputs(seed: int=0):
    np.random.seed(seed)
    _w = jnp.asarray

    def _rec_inputs():
        import jax
        import jax.numpy as jnp
        _gk = jax.random.key(seed)
        x = 0.0001712 + 1 * jax.random.normal(jax.random.fold_in(_gk, 1), (3125, 16), jnp.float32)
        src = jax.random.randint(jax.random.fold_in(_gk, 2), (100000,), 0, 3125, jnp.int32)
        dst = jnp.minimum((3125 * jax.random.uniform(jax.random.fold_in(_gk, 3), (100000,)) ** 2.0).astype(jnp.int32), 99999)
        _o = jnp.argsort(dst, stable=True)
        src = src[_o]
        dst = dst[_o]
        edge_attr_16 = -0.00010739 + 0.99994 * jax.random.normal(jax.random.fold_in(_gk, 12), (100000, 16), jnp.float32)
        edge_weight = jax.random.uniform(jax.random.fold_in(_gk, 14), (100000,), jnp.float32, 0.0, 1)
        return (x, src, dst, edge_attr_16, edge_weight)
    x, src, dst, edge_attr_16, edge_weight = _rec_inputs()

    def _L0_gnn_setup():
        import jax, jax.numpy as jnp
        import numpy as np
        STALK_DIM = 16
        N_NODES = 50000
        N_EDGES = 12500
        HIDDEN = 64
        key = jax.random.key(seed)
        k1, k2, k3, k4 = jax.random.split(key, 4)
        d = STALK_DIM
        x = jax.random.normal(k1, (N_NODES, d), dtype=jnp.float32)
        edge_index = jax.random.randint(k2, (2, N_EDGES), 0, N_NODES, dtype=jnp.int64)
        W1 = jax.random.normal(k3, (HIDDEN, 2 * d), dtype=jnp.float32) * (1.0 / np.sqrt(2 * d))
        b1 = jnp.zeros((HIDDEN,), dtype=jnp.float32)
        W2 = jax.random.normal(k4, (d, HIDDEN), dtype=jnp.float32) * (1.0 / np.sqrt(HIDDEN))
        b2 = jnp.zeros((d,), dtype=jnp.float32)
        return {'x': x, 'edge_index': edge_index, 'W1': W1, 'b1': b1, 'W2': W2, 'b2': b2}
    _L0_gnn_all = _L0_gnn_setup()
    _L0_gnn_in = {k: v for k, v in _L0_gnn_all.items() if k in ('W1', 'b1', 'W2', 'b2')}
    del _L0_gnn_all

    def _L1_gnn_setup():
        import jax, jax.numpy as jnp
        import numpy as np
        N_NODES = 3125
        N_EDGES = 100000
        DIM = 16
        B, K, C, D, E, H = (0.1, 5.0, 1.0, 5.0, 0.9, 0.1)
        E_ = E
        key = jax.random.key(seed)
        k1, k2, k3, k4 = jax.random.split(key, 4)
        x = jax.random.uniform(k1, (N_NODES, DIM), dtype=jnp.float32)
        edge_src = jax.random.randint(k2, (N_EDGES,), 0, N_NODES, dtype=jnp.int32)
        edge_dst = jax.random.randint(k3, (N_EDGES,), 0, N_NODES, dtype=jnp.int32)
        edge_vals = jax.random.uniform(k4, (N_EDGES,), dtype=jnp.float32)
        return {'x': x, 'edge_src': edge_src, 'edge_dst': edge_dst, 'edge_vals': edge_vals}
    _L1_gnn_all = _L1_gnn_setup()
    _L1_gnn_in = {k: v for k, v in _L1_gnn_all.items() if k in ()}
    del _L1_gnn_all

    def _L2_gnn_setup():
        import jax, jax.numpy as jnp
        import numpy as np
        N = 3125
        E = 100000
        C = 16
        PC = 3 * C
        HID = 32

        def gcn_conv(x, edge_index, W):
            h = x @ W.T
            row, col = (edge_index[0], edge_index[1])
            ones = jnp.ones((edge_index.shape[1],), dtype=x.dtype)
            deg = jax.ops.segment_sum(ones, col, num_segments=x.shape[0]) + 1.0
            dis = jax.lax.rsqrt(deg)
            norm = dis[row] * dis[col]
            agg = jax.ops.segment_sum(h[row] * norm[:, None], col, num_segments=x.shape[0])
            agg = agg + h * (dis * dis)[:, None]
            return agg
        key = jax.random.key(seed)
        ks = jax.random.split(key, 8)
        xx = jax.random.normal(ks[0], (N, C), dtype=jnp.float32)
        edge_index = jax.random.randint(ks[1], (2, E), 0, N, dtype=jnp.int64)
        W_gcn = jax.random.normal(ks[2], (PC, C), dtype=jnp.float32) * (1.0 / np.sqrt(C))
        W1 = jax.random.normal(ks[3], (HID, PC), dtype=jnp.float32) * (1.0 / np.sqrt(PC))
        b1 = jax.random.normal(ks[4], (HID,), dtype=jnp.float32) * 0.01
        W2 = jax.random.normal(ks[5], (C, HID), dtype=jnp.float32) * (1.0 / np.sqrt(HID))
        b2 = jax.random.normal(ks[6], (C,), dtype=jnp.float32) * 0.01
        return {'xx': xx, 'edge_index': edge_index, 'parent_index': 0, 'W_gcn': W_gcn, 'W1': W1, 'b1': b1, 'W2': W2, 'b2': b2}
    _L2_gnn_all = _L2_gnn_setup()
    _L2_gnn_in = {k: v for k, v in _L2_gnn_all.items() if k in ('W_gcn', 'W1', 'b1', 'W2', 'b2')}
    del _L2_gnn_all

    def _L3_gnn_setup():
        import jax, jax.numpy as jnp
        import numpy as np
        N_NODES = 50000
        N_EDGES = 25000
        IN_CH = 16
        OUT_CH = 16
        EDGE_DIM = 16
        HIDDEN = 128
        key = jax.random.key(seed)
        ks = jax.random.split(key, 8)
        node_attr = jax.random.normal(ks[0], (N_NODES, IN_CH), dtype=jnp.float32)
        edge_attr = jax.random.normal(ks[1], (N_EDGES, EDGE_DIM), dtype=jnp.float32)
        W1 = jax.random.normal(ks[2], (EDGE_DIM, HIDDEN), dtype=jnp.float32) / np.sqrt(EDGE_DIM)
        b1 = jnp.zeros((HIDDEN,), dtype=jnp.float32)
        W2 = jax.random.normal(ks[3], (HIDDEN, IN_CH * OUT_CH), dtype=jnp.float32) / np.sqrt(HIDDEN)
        b2 = jnp.zeros((IN_CH * OUT_CH,), dtype=jnp.float32)
        bound = 1.0 / np.sqrt(IN_CH)
        root = jax.random.uniform(ks[4], (IN_CH, OUT_CH), dtype=jnp.float32, minval=-bound, maxval=bound)
        edge_index = jax.random.randint(ks[5], (2, N_EDGES), 0, N_NODES, dtype=jnp.int64)
        return {'node_attr': node_attr, 'edge_attr': edge_attr, 'W1': W1, 'b1': b1, 'W2': W2, 'b2': b2, 'root': root, 'edge_index': edge_index}
    _L3_gnn_all = _L3_gnn_setup()
    _L3_gnn_in = {k: v for k, v in _L3_gnn_all.items() if k in ('W1', 'b1', 'W2', 'b2', 'root')}
    del _L3_gnn_all
    return {'x': x, 'src': src, 'dst': dst, 'edge_attr_16': edge_attr_16, 'edge_weight': edge_weight, 'L0_gnn_W1': _L0_gnn_in['W1'], 'L0_gnn_b1': _L0_gnn_in['b1'], 'L0_gnn_W2': _L0_gnn_in['W2'], 'L0_gnn_b2': _L0_gnn_in['b2'], 'L2_gnn_W_gcn': _L2_gnn_in['W_gcn'], 'L2_gnn_W1': _L2_gnn_in['W1'], 'L2_gnn_b1': _L2_gnn_in['b1'], 'L2_gnn_W2': _L2_gnn_in['W2'], 'L2_gnn_b2': _L2_gnn_in['b2'], 'L3_gnn_W1': _L3_gnn_in['W1'], 'L3_gnn_b1': _L3_gnn_in['b1'], 'L3_gnn_W2': _L3_gnn_in['W2'], 'L3_gnn_b2': _L3_gnn_in['b2'], 'L3_gnn_root': _L3_gnn_in['root']}

def reference(x, src, dst, edge_attr_16, edge_weight, L0_gnn_W1, L0_gnn_b1, L0_gnn_W2, L0_gnn_b2, L2_gnn_W_gcn, L2_gnn_W1, L2_gnn_b1, L2_gnn_W2, L2_gnn_b2, L3_gnn_W1, L3_gnn_b1, L3_gnn_W2, L3_gnn_b2, L3_gnn_root):
    import jax
    import jax.numpy as jnp

    def _L0_gnn_ref(x, edge_index, W1, b1, W2, b2):
        import jax, jax.numpy as jnp
        import numpy as np
        STALK_DIM = 16
        N_NODES = 50000
        N_EDGES = 12500
        HIDDEN = 64
        d = x.shape[1]
        n = x.shape[0]
        src, dst = (edge_index[0], edge_index[1])
        xs, xd = (x[src], x[dst])

        def reflection(a, b):
            h = jax.nn.relu(jnp.concatenate([a, b], axis=1) @ W1.T + b1)
            return h @ W2.T + b2

        def householder(v):
            vn = v / jnp.maximum(jnp.linalg.norm(v, axis=1, keepdims=True), 1e-12)
            return jnp.eye(d, dtype=v.dtype)[None] - 2.0 * vn[:, :, None] * vn[:, None, :]
        F_s = householder(reflection(xs, xd))
        F_d = householder(reflection(xd, xs))
        L_sd = -jnp.einsum('eki,ekj->eij', F_s, F_d)
        ones_e = jnp.ones(src.shape[0], dtype=x.dtype)
        deg = jnp.zeros(n, dtype=x.dtype).at[src].add(ones_e).at[dst].add(ones_e)
        deg_inv_sqrt = 1.0 / jnp.sqrt(jnp.maximum(deg, 1e-05))
        coef = deg_inv_sqrt[src] * deg_inv_sqrt[dst]
        msg_s = coef[:, None] * jnp.einsum('eij,ej->ei', L_sd, xd)
        msg_d = coef[:, None] * jnp.einsum('eji,ej->ei', L_sd, xs)
        out = x - jnp.zeros_like(x).at[src].add(msg_s) - jnp.zeros_like(x).at[dst].add(msg_d)
        return jax.nn.relu(out)

    def _L1_gnn_ref(x, edge_src, edge_dst, edge_vals):
        import jax, jax.numpy as jnp
        import numpy as np
        N_NODES = 3125
        N_EDGES = 100000
        DIM = 16
        B, K, C, D, E, H = (0.1, 5.0, 1.0, 5.0, 0.9, 0.1)
        E_ = E
        n = x.shape[0]
        f = B + x * (1.0 - x / K) * (x / C - 1.0)
        xi = x[edge_src]
        xj = x[edge_dst]
        msg = edge_vals[:, None] * xi * xj / (D + E_ * xi + H * xj)
        f = f + jax.ops.segment_sum(msg, edge_src, num_segments=n)
        return f

    def _L2_gnn_ref(xx, edge_index, parent_index, W_gcn, W1, b1, W2, b2):
        import jax, jax.numpy as jnp
        import numpy as np
        N = 3125
        E = 100000
        C = 16
        PC = 3 * C
        HID = 32

        def gcn_conv(x, edge_index, W):
            h = x @ W.T
            row, col = (edge_index[0], edge_index[1])
            ones = jnp.ones((edge_index.shape[1],), dtype=x.dtype)
            deg = jax.ops.segment_sum(ones, col, num_segments=x.shape[0]) + 1.0
            dis = jax.lax.rsqrt(deg)
            norm = dis[row] * dis[col]
            agg = jax.ops.segment_sum(h[row] * norm[:, None], col, num_segments=x.shape[0])
            agg = agg + h * (dis * dis)[:, None]
            return agg
        features = gcn_conv(xx, edge_index, W_gcn)
        update = jax.nn.relu(features @ W1.T + b1) @ W2.T + b2
        return xx + update

    def _L3_gnn_ref(node_attr, edge_attr, W1, b1, W2, b2, root, edge_index):
        import jax, jax.numpy as jnp
        import numpy as np
        N_NODES = 50000
        N_EDGES = 25000
        IN_CH = 16
        OUT_CH = 16
        EDGE_DIM = 16
        HIDDEN = 128
        n_nodes = node_attr.shape[0]
        h = jax.nn.relu(edge_attr @ W1 + b1)
        weights = (h @ W2 + b2).reshape(-1, IN_CH, OUT_CH)
        src = node_attr[edge_index[0]]
        messages = jnp.einsum('ei,eio->eo', src, weights)
        out = jax.ops.segment_sum(messages, edge_index[1], num_segments=n_nodes)
        out = out + node_attr @ root
        return out
    edge_index = jnp.stack([src, dst])
    h = jnp.maximum(_layernorm(x, axis=-1), 0.0)
    x = x + _L0_gnn_ref(h, edge_index, L0_gnn_W1, L0_gnn_b1, L0_gnn_W2, L0_gnn_b2)
    h = jnp.maximum(_layernorm(x, axis=-1), 0.0)
    x = x + _L1_gnn_ref(h, src, dst, edge_weight)
    h = jnp.maximum(_layernorm(x, axis=-1), 0.0)
    x = x + _L2_gnn_ref(h, edge_index, 0, L2_gnn_W_gcn, L2_gnn_W1, L2_gnn_b1, L2_gnn_W2, L2_gnn_b2)
    h = jnp.maximum(_layernorm(x, axis=-1), 0.0)
    x = x + _L3_gnn_ref(h, edge_attr_16, L3_gnn_W1, L3_gnn_b1, L3_gnn_W2, L3_gnn_b2, L3_gnn_root, edge_index)
    return x

_drawn_inputs = setup_inputs


def setup_inputs(seed=0):
    import zlib

    import numpy as np

    out = dict(_drawn_inputs(seed))
    spreads = {'L0_gnn_b1': (0.0, 2.0),
     'L0_gnn_b2': (0.0, 0.592),
     'L3_gnn_b1': (0.0, 0.1),
     'L3_gnn_b2': (0.0, 0.1)}
    factors = {'edge_weight': 3.513,
     'L2_gnn_b1': 60.679,
     'L2_gnn_b2': 62.759,
     'L3_gnn_root': 5.761,
     'L2_gnn_W1': 2.779}
    for name, (base, spread) in spreads.items():
        noise = np.random.default_rng([zlib.crc32(name.encode()), seed]).standard_normal(out[name].shape)
        drawn = base * np.exp(spread * noise) if base else spread * noise
        out[name] = jnp.asarray(drawn.astype(out[name].dtype))
    for name, factor in factors.items():
        out[name] = (out[name] * factor).astype(out[name].dtype)
    return out
```

```python
from contextlib import ExitStack

import concourse.bass as bass
from concourse import mybir

ALU = mybir.AluOpType
ACT = mybir.ActivationFunctionType
AX_X = mybir.AxisListType.X
F32 = mybir.dt.float32
F16 = mybir.dt.float16
BF16 = mybir.dt.bfloat16
I32 = mybir.dt.int32

N = 3125
C = 16
E = 100000
EP = 125
TILES = E // EP
CT = 16
CHUNKS = TILES // CT
PAIRS = CHUNKS // 2
NP = 112
G = 28
H = 7
LO = NP * G // H
B = LO // NP
FULL = N // NP
TAIL = N - FULL * NP
R0 = 20
OG = 4
HALF = CT // 2
MAGIC = float(3 * 2 ** 22)
SCALE16 = 8192.0
EPS = 1e-5


class Chain:

    def __init__(self, engine, sem, base=0):
        self.engine, self.sem, self.base, self.n = engine, sem, base, 0

    def mark(self, ins):
        self.n += 1
        ins.then_inc(self.sem, 1)

    def link(self, ins):
        self.mark(ins)
        self.engine.wait_ge(self.sem, self.base + self.n)


def gnn_program(nc, x, src, dst, edge_attr, edge_weight, w1_0t, b1_0, w2_0t, b2_0,
                wg_t, w1_2t, b1_2, w2_2t, b2_2, w1_3, b1_3, w2_3, b2_3, root, out):
    H0 = b1_0.shape[0]
    H2 = b1_2.shape[0]
    PC = wg_t.shape[1]
    H3 = b1_3.shape[0]
    OO = C * C

    table0 = nc.dram_tensor("table0", (NP * G, R0), F32, kind="Internal").ap()
    table1 = nc.dram_tensor("table1", (NP * G, C), F32, kind="Internal").ap()
    table2 = nc.dram_tensor("table2", (NP * G, 2 * C), F16, kind="Internal").ap()
    table3 = nc.dram_tensor("table3", (NP * G, 2 * C), F32, kind="Internal").ap()

    with ExitStack() as ctx:
        def sb(name, shape, dt=F32):
            return ctx.enter_context(nc.sbuf_tensor(name, shape, dt))

        def ps(name, shape=(128, 512)):
            return ctx.enter_context(nc.psum_tensor(name, list(shape), F32))

        def sem(name):
            return ctx.enter_context(nc.semaphore(name))

        identity = sb("identity", [128, 128])
        iota_lo_i = sb("iota_lo_i", [128, LO], I32)
        iota_lo = sb("iota_lo", [128, LO], F16)
        zeros = sb("zeros", [128, LO], BF16)
        w1_0 = sb("w1_0", [128, 4, 2 * H0])
        b1c_0 = sb("b1c_0", [128, 1])
        w2_0 = sb("w2_0", [128, 2 * C])
        b2r_0 = sb("b2r_0", [EP, 2, C])
        wg = sb("wg", [C, PC])
        w1_2 = sb("w1_2", [PC, H2])
        b1c_2 = sb("b1c_2", [H2, 1])
        w2_2 = sb("w2_2", [H2, C])
        b2r_2 = sb("b2r_2", [NP, C])
        w1z_3 = sb("w1z_3", [128, 8, H3])
        b1c_3 = sb("b1c_3", [H3, 1])
        w2s_3 = sb("w2s_3", [H3, OO])
        zr_3 = sb("zr_3", [C, 2, C])

        ends = sb("ends", [EP, 2, TILES], I32)
        ew = sb("ew", [EP, TILES])
        n_f = sb("n_f", [EP, 2, TILES])
        t_f = sb("t_f", [EP, 2, TILES])
        lo = sb("lo", [EP, 2, TILES])
        group = sb("group", [EP, 2, TILES], F16)
        place = sb("place", [EP, 2, TILES], F16)
        hmask = sb("hmask", [EP, 2, TILES, H], BF16)

        nx = sb("nx", [NP, G, C])
        nh = sb("nh", [NP, G, C])
        na = sb("na", [NP, G, C])
        nb = sb("nb", [NP, G, C])
        ncc = sb("ncc", [NP, G, C])
        stat = sb("stat", [NP, 4, G])
        degs = sb("degs", [NP, 2, G])
        rdeg = sb("rdeg", [NP, G])
        dis = sb("dis", [NP, G])
        rows0 = sb("rows0", [NP, G, R0])
        rows2 = sb("rows2", [NP, G, 2, C], F16)
        rows3 = sb("rows3", [NP, G, 2, C])
        accs = sb("accs", [NP, LO])

        istage = sb("istage", [EP, 2, 2, CT], I32)
        gat = sb("gat", [EP, 2, CT, 2 * R0])
        lstage = sb("lstage", [EP, 2, 2, CT])
        onehot = sb("onehot", [EP, 2, 2, OG, LO], BF16)
        stat_m = sb("stat_m", [EP, 2, 4, CT, H * C], BF16)
        stat_h = stat_m[:, :, :, :, :].bitcast(F16)
        ab = sb("ab", [EP, CT, 2, C])
        prod = sb("prod", [EP, CT, 7, C])
        dots = sb("dots", [EP, CT, 7])
        inv = sb("inv", [EP, CT, 2])
        co = sb("co", [EP, CT, 2])
        cx = sb("cx", [EP, CT, 2])
        ga = sb("ga", [EP, CT, 2])
        m = sb("m", [EP, CT, 2, C])
        mt = sb("mt", [EP, CT, 2, C])
        part_h = sb("part_h", [EP, 2, CT, 2, C], F16)
        part_b = sb("part_b", [EP, 3, CT, C], BF16)
        packed = sb("packed", [EP, CT, 2, C])
        xt = sb("xt", [128, 4, EP])
        hid = sb("hid", [128, 4, 4 * EP])
        ea = sb("ea", [EP, 2, CT, C])
        pr = sb("pr", [EP, 2, C, C])
        feat = sb("feat", [128, 3, 4 * NP])

        p_acc = ps("p_acc")
        p_xt = ps("p_xt")
        p_a = ps("p_a")
        p_b = ps("p_b")
        p_c = ps("p_c")
        p_d = ps("p_d")
        p_e = ps("p_e")
        p_hid = [p_a, p_b]
        p_ab = [p_c, p_d]
        p_w = [p_c, p_d, p_e]

        s_in = sem("s_in")
        s_w = sem("s_w")
        s_const = sem("s_const")
        s_zero = sem("s_zero")
        s_tab = sem("s_tab")
        s_out = sem("s_out")
        s_dve = sem("s_dve")
        s_sq = sem("s_sq")
        s_rt = sem("s_rt")
        s_rows = sem("s_rows")
        s_cnt_oh = sem("s_cnt_oh")
        s_cnt_mm = sem("s_cnt_mm")
        s_acc0 = sem("s_acc0")
        s_done = sem("s_done")
        s_accs = sem("s_accs")
        s_node = sem("s_node")
        s_feat = sem("s_feat")
        s_stage = sem("s_stage")
        s_pool = sem("s_pool")
        L = range(4)
        s_gat = [[sem(f"s_gat{n}_{s}") for s in range(2)] for n in L]
        s_gfree = [sem(f"s_gfree{n}") for n in L]
        s_chain = [sem(f"s_chain{n}") for n in L]
        s_stat = [sem(f"s_stat{n}") for n in L]
        s_oh = [sem(f"s_oh{n}") for n in L]
        s_ohfree = [sem(f"s_ohfree{n}") for n in L]
        s_sfree = [sem(f"s_sfree{n}") for n in L]
        s_xt = {n: sem(f"s_xt{n}") for n in (0, 3)}
        s_xts = {n: sem(f"s_xts{n}") for n in (0, 3)}
        s_hp = {n: sem(f"s_hp{n}") for n in (0, 3)}
        s_hs = {n: sem(f"s_hs{n}") for n in (0, 3)}
        s_mlp = {n: sem(f"s_mlp{n}") for n in (0, 3)}
        s_mfree = {n: sem(f"s_mfree{n}") for n in (0, 3)}
        s_ea = [sem(f"s_ea{s}") for s in range(2)]
        s_packed = sem("s_packed")
        s_msg = sem("s_msg")
        s_p1 = sem("s_p1")

        x_groups = x[0:FULL * NP, :].rearrange("(g p) c -> p g c", p=NP)
        x_tail = x[FULL * NP:N, :]
        out_groups = out[0:FULL * NP, :].rearrange("(g p) c -> p g c", p=NP)
        out_tail = out[FULL * NP:N, :]
        ea_rows = edge_attr.rearrange("(p t) c -> p (t c)", p=EP)

        def rows_of(table):
            return table.rearrange("(g p) c -> p g c", p=NP)

        block = ctx.enter_context(nc.Block())

        node_step = {}
        count = 0
        for what in ["degrees", "sums0", "sums1", "sums2"]:
            count += 1
            node_step[what] = count
        for q in range(H):
            for what in ("turned", "features", "hidden", "update"):
                count += 1
                node_step[(what, q)] = count
        for q in range(H):
            for what in ("turned3", "rooted"):
                count += 1
                node_step[(what, q)] = count
        count += 1
        node_step["sums3"] = count

        @block.sync
        def _(sp):
            sp.dma_start(ends[:, 0, :], src.rearrange("(p t) -> p t", p=EP)).then_inc(s_in, 16)
            sp.dma_start(ends[:, 1, :], dst.rearrange("(p t) -> p t", p=EP)).then_inc(s_in, 16)
            sp.wait_ge(s_zero, 1)
            sp.dma_start(nx[:, 0:FULL, :], x_groups).then_inc(s_in, 16)
            sp.dma_start(nx[0:TAIL, FULL, :], x_tail).then_inc(s_in, 16)
            sp.dma_start(ew[:, :], edge_weight.rearrange("(p t) -> p t", p=EP)).then_inc(s_w, 16)
            for j in range(4):
                r = 2 * C * j
                sp.dma_start(w1_0[r:r + 2 * C, j, 0:H0], w1_0t).then_inc(s_w, 16)
                sp.dma_start(w1_0[r:r + C, j, H0:2 * H0], w1_0t[C:2 * C, :]).then_inc(s_w, 16)
                sp.dma_start(w1_0[r + C:r + 2 * C, j, H0:2 * H0], w1_0t[0:C, :]).then_inc(s_w, 16)
            for d in range(2):
                sp.dma_start(b1c_0[d * H0:(d + 1) * H0, :], b1_0.rearrange("(k a) -> k a", a=1)).then_inc(s_w, 16)
                sp.dma_start(w2_0[d * H0:(d + 1) * H0, d * C:(d + 1) * C], w2_0t).then_inc(s_w, 16)
                sp.dma_start(b2r_0[:, d, :], b2_0.rearrange("(a c) -> a c", a=1).to_broadcast((EP, C))).then_inc(s_w, 16)
            sp.dma_start(wg[:, :], wg_t).then_inc(s_w, 16)
            sp.dma_start(w1_2[:, :], w1_2t).then_inc(s_w, 16)
            sp.dma_start(b1c_2[:, :], b1_2.rearrange("(k a) -> k a", a=1)).then_inc(s_w, 16)
            sp.dma_start(w2_2[:, :], w2_2t).then_inc(s_w, 16)
            sp.dma_start(b2r_2[:, :], b2_2.rearrange("(a c) -> a c", a=1).to_broadcast((NP, C))).then_inc(s_w, 16)
            for j in range(8):
                sp.dma_start(w1z_3[j * C:(j + 1) * C, j, :], w1_3).then_inc(s_w, 16)
            sp.dma_start(b1c_3[:, :], b1_3.rearrange("(k a) -> k a", a=1)).then_inc(s_w, 16)
            sp.dma_start(w2s_3[:, :], w2_3).then_inc(s_w, 16)
            sp.dma_start(zr_3[:, 0, :], b2_3.rearrange("(i o) -> i o", i=C)).then_inc(s_w, 16)
            sp.dma_start(zr_3[:, 1, :], root).then_inc(s_w, 16)
            for n, (table, rows) in enumerate((
                    (table0, rows0[:, :, :]), (table1, nh[:, :, :]),
                    (table2, rows2[:, :, :, :].rearrange("p g a c -> p g (a c)")),
                    (table3, rows3[:, :, :, :].rearrange("p g a c -> p g (a c)")))):
                sp.wait_ge(s_rows, n + 1)
                sp.dma_start(rows_of(table), rows).then_inc(s_tab, 16)
            with sp.Fori(0, PAIRS) as i:
                for s in range(2):
                    sp.wait_ge(s_xt[3], 2 * i + s + 1)
                    sp.dma_start(ea[:, s, :, :].rearrange("p t c -> p (t c)"),
                                 ea_rows[:, bass.ds(i * (2 * CT * C) + s * CT * C, CT * C)]).then_inc(s_ea[s], 16)
            sp.wait_ge(s_rows, 5)
            sp.dma_start(out_groups, nx[:, 0:FULL, :]).then_inc(s_out, 16)
            sp.dma_start(out_tail, nx[0:TAIL, FULL, :]).then_inc(s_out, 16)
            sp.wait_ge(s_out, 32)

        @block.gpsimd
        def _(pool):
            pool.memset(identity[:, :], 0.0).then_inc(s_const, 1)
            pool.wait_ge(s_const, 1)
            pool.affine_select(out=identity[:, :], in_=identity[:, :], compare_op=ALU.not_equal, fill=1.0,
                               base=0, pattern=[[-1, 128]], channel_multiplier=1).then_inc(s_const, 1)
            pool.iota(iota_lo_i[:, :], [[1, LO]], base=0, channel_multiplier=0).then_inc(s_const, 1)
            pool.wait_ge(s_in, 64)
            staged = 0
            for n, table, ends_of in ((0, table0, (0, 1)), (1, table1, (0, 1)), (2, table2, (0,)), (3, table3, (0,))):
                width = table.shape[1]
                pool.wait_ge(s_tab, 16 * (n + 1))
                with pool.Fori(0, PAIRS) as i:
                    for s in range(2):
                        pool.wait_ge(s_gfree[n], 2 * i + s + 1)
                        pool.sem_inc(s_pool, 1)
                        pool.tensor_copy(istage[:, s, :, :], ends[:, :, bass.ds(i * (2 * CT) + s * CT, CT)]).then_inc(s_stage, 1)
                        pool.wait_ge(s_stage, 2 * i + s + 1 + staged)
                        pool.sem_inc(s_pool, 1)
                        for t in range(CT):
                            for d in ends_of:
                                if n == 2:
                                    to = gat[:, s, t, 0:C].bitcast(F16)
                                elif n == 3:
                                    to = gat[:, s, t, 0:2 * C]
                                else:
                                    to = gat[:, s, t, d * R0:d * R0 + width]
                                pool.indirect_dma_start(to, None, table,
                                                        bass.IndirectOffsetOnAxis(istage[:, s, d, t:t + 1], 0)
                                                        ).then_inc(s_gat[n][s], 16)
                staged += CHUNKS

        @block.scalar
        def _(act):
            def square_root(k, out_ap, in_ap):
                act.wait_ge(s_sq, k)
                nc.scalar.activation(out_ap, in_ap, ACT.Sqrt).then_inc(s_rt, 1)

            square_root(1, stat[:, 2, :], stat[:, 1, :])
            square_root(2, stat[:, 2, :], stat[:, 1, :])
            square_root(3, stat[:, 2, :], stat[:, 1, :])

            def hidden0(i, s, i2):
                act.wait_ge(s_gat[0][s], (i + 1) * (2 * CT * 16))
                nc.scalar.activation(packed[:, :, :, :],
                                     gat[:, s, :, :].rearrange("p t (d f) -> p t d f", d=2)[:, :, :, 0:C],
                                     ACT.Copy).then_inc(s_packed, 1)
                act.wait_ge(s_xt[0], i2 + 1)
                nc.scalar.activation(xt[:, :, :], p_xt[:, 0:4 * EP].rearrange("p (q e) -> p q e", q=4),
                                     ACT.Copy).then_inc(s_xts[0], 1)
                for j in range(4):
                    act.wait_ge(s_hp[0], i2 * 4 + j + 1)
                    nc.scalar.activation(hid[:, j, :], p_hid[j % 2][:, 0:4 * EP], ACT.Relu,
                                         bias=b1c_0[:, 0:1]).then_inc(s_hs[0], 1)

            def first_parts(i2):
                act.wait_ge(s_msg, i2 + 1)
                nc.scalar.activation(part_h[:, 0, :, :, :], m[:, :, :, :], ACT.Copy).then_inc(s_p1, 1)

            hidden0(0, 0, 0)
            with act.Fori(0, PAIRS - 1) as i:
                hidden0(i, 1, 2 * i + 1)
                first_parts(2 * i)
                hidden0(i + 1, 0, 2 * i + 2)
                first_parts(2 * i + 1)
            hidden0(PAIRS - 1, 1, CHUNKS - 1)
            first_parts(CHUNKS - 2)
            first_parts(CHUNKS - 1)

            square_root(4, stat[:, 2, :], stat[:, 1, :])
            square_root(5, stat[:, 2, :], stat[:, 1, :])
            for q in range(H):
                act.wait_ge(s_node, node_step[("hidden", q)])
                nc.scalar.activation(feat[0:H2, 2, :], p_b[0:H2, 0:LO], ACT.Relu,
                                     bias=b1c_2[:, 0:1]).then_inc(s_feat, 1)
            square_root(6, stat[:, 2, :], stat[:, 1, :])

            with act.Fori(0, PAIRS) as i:
                for s in range(2):
                    act.wait_ge(s_xt[3], 2 * i + s + 3)
                    nc.scalar.activation(xt[:, 0:2, :], p_xt[:, 0:2 * EP].rearrange("p (u e) -> p u e", u=2),
                                         ACT.Copy).then_inc(s_xts[3], 1)
                    for j in range(4):
                        act.wait_ge(s_hp[3], (2 * i + s) * 4 + j + 1)
                        nc.scalar.activation(hid[:, j, :], p_hid[j % 2][:, 0:4 * EP], ACT.Relu,
                                             bias=b1c_3[:, 0:1]).then_inc(s_hs[3], 1)

        @block.vector
        def _(dve):
            v = nc.vector
            c = Chain(dve, s_dve)

            v.memset(nx[:, FULL, :], 0.0)
            v.memset(w1_0[:, :, :], 0.0)
            v.memset(w2_0[:, :], 0.0)
            v.memset(w1z_3[:, :, :], 0.0)
            v.memset(rows0[:, :, C:R0], 0.0)
            v.memset(zeros[:, :], 0.0)
            v.memset(rows3[:, :, :, :], 0.0).then_inc(s_zero, 1)
            dve.wait_ge(s_zero, 1)

            dve.wait_ge(s_in, 64)
            dve.wait_ge(s_const, 3)
            v.tensor_copy(iota_lo[:, :], iota_lo_i[:, :])
            c.link(v.tensor_copy(n_f[:, :, :], ends[:, :, :]))
            c.link(v.tensor_scalar(t_f[:, :, :], n_f[:, :, :], -(NP - 1) / 2.0, 1.0 / NP, ALU.add, ALU.mult))
            c.link(v.tensor_scalar(t_f[:, :, :], t_f[:, :, :], MAGIC, None, ALU.add))
            c.link(v.tensor_scalar(t_f[:, :, :], t_f[:, :, :], -MAGIC, None, ALU.add))
            v.tensor_copy(group[:, :, :], t_f[:, :, :])
            c.link(v.scalar_tensor_tensor(place[:, :, :], t_f[:, :, :], -float(NP), n_f[:, :, :], ALU.mult, ALU.add))
            c.link(v.tensor_scalar(t_f[:, :, :], n_f[:, :, :], -(LO - 1) / 2.0, 1.0 / LO, ALU.add, ALU.mult))
            c.link(v.tensor_scalar(t_f[:, :, :], t_f[:, :, :], MAGIC, None, ALU.add))
            c.link(v.tensor_scalar(t_f[:, :, :], t_f[:, :, :], -MAGIC, None, ALU.add))
            v.scalar_tensor_tensor(lo[:, :, :], t_f[:, :, :], -float(LO), n_f[:, :, :], ALU.mult, ALU.add)
            for d in range(2):
                c.link(v.tensor_tensor(hmask[:, d, :, :],
                                       t_f[:, d, :].unsqueeze(2).to_broadcast((EP, TILES, H)),
                                       iota_lo[0:EP, 0:H].unsqueeze(1).to_broadcast((EP, TILES, H)), ALU.is_equal))

            DC = 8
            dig_p = stat_m[:, :, :, :, :].rearrange("p s a t k -> p (s a t k)")
            dig_g = onehot[:, :, :, :, :].rearrange("p r e o k -> p (r e o k)")

            def digits(s, i2):
                a = dig_p[:, s * 2 * DC * NP:(s + 1) * 2 * DC * NP].rearrange("p (d t k) -> p d t k", d=2, t=DC)
                b = dig_g[:, s * 2 * DC * G:(s + 1) * 2 * DC * G].rearrange("p (d t k) -> p d t k", d=2, t=DC)
                return a, b

            dve.sem_inc(s_cnt_mm, 2)
            with dve.Fori(0, TILES // DC // 2) as i:
                for s in range(2):
                    dve.wait_ge(s_cnt_mm, 2 * i + s + 1)
                    a, b = digits(s, i)
                    at = bass.ds(i * (2 * DC) + s * DC, DC)
                    for d in range(2):
                        v.tensor_tensor(a[:, d], place[:, d, at].unsqueeze(2).to_broadcast((EP, DC, NP)),
                                        iota_lo[0:EP, 0:NP].unsqueeze(1).to_broadcast((EP, DC, NP)), ALU.is_equal)
                        last = v.tensor_tensor(b[:, d], group[:, d, at].unsqueeze(2).to_broadcast((EP, DC, G)),
                                               iota_lo[0:EP, 0:G].unsqueeze(1).to_broadcast((EP, DC, G)), ALU.is_equal)
                    last.then_inc(s_cnt_oh, 1)

            roots = [0]

            def inverse_root(out_ap, in_ap):
                c.link(v.tensor_copy(stat[:, 1, :], in_ap))
                roots[0] += 1
                dve.sem_inc(s_sq, 1)
                dve.wait_ge(s_rt, roots[0])
                c.link(v.reciprocal(stat[:, 3, :], stat[:, 2, :]))
                c.link(v.tensor_tensor(stat[:, 2, :], stat[:, 3, :], stat[:, 3, :], ALU.mult))
                c.link(v.scalar_tensor_tensor(stat[:, 2, :], stat[:, 2, :], -0.5, stat[:, 1, :], ALU.mult, ALU.mult))
                c.link(v.scalar_tensor_tensor(out_ap, stat[:, 2, :], 1.5, stat[:, 3, :], ALU.add, ALU.mult))

            def wide(ap):
                return ap.unsqueeze(2).to_broadcast((NP, G, C))

            def layernorm_relu():
                c.link(v.tensor_reduce(stat[:, 0, :], nx[:, :, :], AX_X, ALU.add))
                c.link(v.tensor_scalar(stat[:, 0, :], stat[:, 0, :], 1.0 / C, None, ALU.mult))
                c.link(v.tensor_tensor(na[:, :, :], nx[:, :, :], wide(stat[:, 0, :]), ALU.subtract))
                c.link(v.tensor_tensor(nb[:, :, :], na[:, :, :], na[:, :, :], ALU.mult))
                c.link(v.tensor_reduce(stat[:, 3, :], nb[:, :, :], AX_X, ALU.add))
                c.link(v.tensor_scalar(stat[:, 3, :], stat[:, 3, :], 1.0 / C, EPS, ALU.mult, ALU.add))
                inverse_root(stat[:, 0, :], stat[:, 3, :])
                c.link(v.tensor_tensor(nb[:, :, :], na[:, :, :], wide(stat[:, 0, :]), ALU.mult))
                c.link(v.tensor_scalar(nh[:, :, :], nb[:, :, :], 0.0, None, ALU.max))

            def layer_sums(n, what):
                dve.wait_ge(s_done, n + 1)
                v.tensor_copy(accs[:, :], p_acc[0:NP, 0:LO]).then_inc(s_accs, 1)
                dve.wait_ge(s_node, node_step[what])
                return p_a[0:NP, 0:G * C].rearrange("p (b h c) -> p h b c", b=B, h=H)

            def by_high(t):
                return t[:, :, :].rearrange("p (h b) c -> p h b c", b=B)

            def sums_to(t, n, what):
                c.link(v.tensor_copy(by_high(t), layer_sums(n, what)))

            def onehots(n, chunk, s, g, og, ends_of):
                dve.wait_ge(s_ohfree[n], chunk * (CT // og) + g + 1)
                for k in range(og):
                    for d in ends_of:
                        last = v.tensor_scalar(onehot[:, g % 2, d, k, :], iota_lo[0:EP, :],
                                               lstage[:, s, d, g * og + k:g * og + k + 1], None, ALU.is_equal)
                last.then_inc(s_oh[n], 1)

            def build_onehots(n, chunk, s, ends_of):
                for g in range(CT // OG):
                    onehots(n, chunk, s, g, OG, ends_of)

            def stage_low(i, s):
                return v.tensor_scalar(lstage[:, s, :, :], lo[:, :, bass.ds(i * (2 * CT) + s * CT, CT)],
                                       0.0, None, ALU.add)

            def weigh(out4, part, i, s, d):
                mask = hmask[:, d, bass.ds(i * (2 * CT) + s * CT, CT), :]
                return v.tensor_tensor(out4.rearrange("p t (h c) -> p t h c", h=H),
                                       part.unsqueeze(2).to_broadcast((EP, CT, H, C)),
                                       mask.unsqueeze(3).to_broadcast((EP, CT, H, C)), ALU.mult)

            def split3(link, msg):
                link(v.tensor_copy(part_b[:, 0], msg))
                link(v.tensor_tensor(mt[:, :, 0, :], msg, part_b[:, 0], ALU.subtract))
                link(v.tensor_copy(part_b[:, 1], mt[:, :, 0, :]))
                link(v.tensor_tensor(part_b[:, 2], mt[:, :, 0, :], part_b[:, 1], ALU.subtract))

            layernorm_relu()
            dve.wait_ge(s_node, node_step["degrees"])
            c.link(v.tensor_copy(degs[:, :, :], p_a[0:NP, 0:2 * G].rearrange("p (d g) -> p d g", d=2)))
            c.link(v.tensor_tensor(rdeg[:, :], degs[:, 0, :], degs[:, 1, :], ALU.add))
            c.link(v.tensor_scalar(rdeg[:, :], rdeg[:, :], EPS, None, ALU.max))
            inverse_root(rdeg[:, :], rdeg[:, :])
            c.link(v.tensor_scalar(dis[:, :], degs[:, 1, :], 1.0, None, ALU.add))
            inverse_root(dis[:, :], dis[:, :])
            v.tensor_scalar(rows0[:, :, C], rdeg[:, :], SCALE16, None, ALU.mult)
            v.tensor_copy(rows0[:, :, 0:C], nh[:, :, :]).then_inc(s_rows, 1)

            dve.wait_ge(s_w, 16 * W_LOADS)
            dve.sem_inc(s_gfree[0], 2)
            dve.sem_inc(s_ohfree[0], 2)
            dve.sem_inc(s_sfree[0], 2)
            dve.sem_inc(s_mfree[0], 2)
            STEPS0 = 17
            with dve.Fori(0, PAIRS) as i:
                c0 = Chain(dve, s_chain[0], i * (2 * STEPS0))
                for s in range(2):
                    xs = gat[:, s, :, 0:C]
                    xd = gat[:, s, :, R0:R0 + C]
                    both = gat[:, s, :, :].rearrange("p t (d f) -> p t d f", d=2)[:, :, :, 0:C]
                    dve.wait_ge(s_gat[0][s], (i + 1) * (2 * CT * 16))
                    dve.wait_ge(s_mlp[0], 2 * i + s + 1)
                    ins = v.tensor_tensor(ab[:, :, :, :], p_ab[s][0:EP, :].rearrange("p (t d c) -> p t d c", t=CT, d=2),
                                          b2r_0[:, :, :].unsqueeze(1).to_broadcast((EP, CT, 2, C)), ALU.add)
                    c0.link(ins)
                    dve.sem_inc(s_mfree[0], 1)
                    a, b = ab[:, :, 0, :], ab[:, :, 1, :]
                    v.tensor_tensor(prod[:, :, 0:2, :], ab[:, :, :, :], ab[:, :, :, :], ALU.mult)
                    v.tensor_tensor(prod[:, :, 2:4, :], ab[:, :, :, :], both, ALU.mult)
                    v.tensor_tensor(prod[:, :, 4, :], a, xd, ALU.mult)
                    v.tensor_tensor(prod[:, :, 5, :], b, xs, ALU.mult)
                    c0.link(v.tensor_tensor(prod[:, :, 6, :], a, b, ALU.mult))
                    c0.link(v.tensor_reduce(dots[:, :, :], prod[:, :, :, :], AX_X, ALU.add))
                    c0.link(v.tensor_scalar(inv[:, :, :], dots[:, :, 0:2], 1e-24, 0.5, ALU.max, ALU.mult))
                    c0.link(v.reciprocal(inv[:, :, :], inv[:, :, :]))
                    c0.link(v.tensor_tensor(co[:, :, :], inv[:, :, :], dots[:, :, 2:4], ALU.mult))
                    c0.link(v.tensor_tensor(cx[:, :, :], co[:, :, :],
                                            dots[:, :, 6:7].to_broadcast((EP, CT, 2)), ALU.mult))
                    v.tensor_tensor(ga[:, :, 0], dots[:, :, 4], cx[:, :, 1], ALU.subtract)
                    c0.link(v.tensor_tensor(ga[:, :, 1], dots[:, :, 5], cx[:, :, 0], ALU.subtract))
                    c0.link(v.tensor_tensor(ga[:, :, :], ga[:, :, :], inv[:, :, :], ALU.mult))
                    c0.link(v.tensor_tensor(mt[:, :, :, :], ab[:, :, :, :],
                                            co[:, :, :].unsqueeze(3).to_broadcast((EP, CT, 2, C)), ALU.mult))
                    v.tensor_tensor(m[:, :, 0, :], xd, mt[:, :, 1, :], ALU.subtract)
                    c0.link(v.tensor_tensor(m[:, :, 1, :], xs, mt[:, :, 0, :], ALU.subtract))
                    c0.link(v.tensor_tensor(mt[:, :, :, :], ab[:, :, :, :],
                                            ga[:, :, :].unsqueeze(3).to_broadcast((EP, CT, 2, C)), ALU.mult))
                    c0.link(v.tensor_tensor(m[:, :, :, :], m[:, :, :, :], mt[:, :, :, :], ALU.subtract))
                    v.tensor_tensor(m[:, :, 0, :], m[:, :, 0, :],
                                    gat[:, s, :, R0 + C:R0 + C + 1].to_broadcast((EP, CT, C)), ALU.mult)
                    c0.link(v.tensor_tensor(m[:, :, 1, :], m[:, :, 1, :],
                                            gat[:, s, :, C:C + 1].to_broadcast((EP, CT, C)), ALU.mult))
                    dve.sem_inc(s_msg, 1)
                    dve.sem_inc(s_gfree[0], 1)
                    dve.wait_ge(s_p1, 2 * i + s + 1)
                    c0.link(v.tensor_tensor(part_h[:, 1], m[:, :, :, :], part_h[:, 0], ALU.subtract))
                    dve.wait_ge(s_sfree[0], 2 * i + s + 1)
                    c0.link(stage_low(i, s))
                    for d in range(2):
                        for q in range(2):
                            last = weigh(stat_h[:, s, 2 * d + q], part_h[:, q, :, d, :], i, s, d)
                    c0.link(last)
                    dve.sem_inc(s_stat[0], 1)
                    build_onehots(0, 2 * i + s, s, (0, 1))
                assert c0.n == 2 * STEPS0, c0.n

            sums_to(na, 0, "sums0")
            c.link(v.tensor_tensor(nb[:, :, :], na[:, :, :], wide(rdeg[:, :]), ALU.mult))
            c.link(v.scalar_tensor_tensor(na[:, :, :], nb[:, :, :], 1.0 / SCALE16, nh[:, :, :], ALU.mult, ALU.add))
            c.link(v.scalar_tensor_tensor(nx[:, :, :], na[:, :, :], 0.0, nx[:, :, :], ALU.max, ALU.add))

            layernorm_relu()
            dve.sem_inc(s_rows, 1)
            dve.sem_inc(s_gfree[1], 2)
            dve.sem_inc(s_ohfree[1], 2)
            dve.sem_inc(s_sfree[1], 2)
            STEPS1 = 12
            with dve.Fori(0, PAIRS) as i:
                c1 = Chain(dve, s_chain[1], i * (2 * STEPS1))
                for s in range(2):
                    xs = gat[:, s, :, 0:C]
                    xd = gat[:, s, :, R0:R0 + C]
                    dve.wait_ge(s_gat[1][s], (i + 1) * (2 * CT * 16))
                    c1.link(v.tensor_scalar(mt[:, :, 0, :], xs, 0.9, 5.0, ALU.mult, ALU.add))
                    c1.link(v.scalar_tensor_tensor(mt[:, :, 1, :], xd, 0.1, mt[:, :, 0, :], ALU.mult, ALU.add))
                    c1.link(v.reciprocal(mt[:, :, 0, :], mt[:, :, 1, :]))
                    c1.link(v.tensor_tensor(m[:, :, 0, :], xs, xd, ALU.mult))
                    dve.sem_inc(s_gfree[1], 1)
                    c1.link(v.tensor_tensor(m[:, :, 1, :], m[:, :, 0, :], mt[:, :, 0, :], ALU.mult))
                    c1.link(v.tensor_tensor(m[:, :, 0, :], m[:, :, 1, :],
                                            ew[:, bass.ds(i * (2 * CT) + s * CT, CT)].unsqueeze(2)
                                            .to_broadcast((EP, CT, C)), ALU.mult))
                    split3(c1.link, m[:, :, 0, :])
                    dve.wait_ge(s_sfree[1], 2 * i + s + 1)
                    c1.link(stage_low(i, s))
                    for q in range(3):
                        last = weigh(stat_m[:, s, q], part_b[:, q], i, s, 0)
                    c1.link(last)
                    dve.sem_inc(s_stat[1], 1)
                    build_onehots(1, 2 * i + s, s, (0,))
                assert c1.n == 2 * STEPS1, c1.n

            sums_to(na, 1, "sums1")
            c.link(v.tensor_tensor(nb[:, :, :], na[:, :, :], nx[:, :, :], ALU.add))
            c.link(v.tensor_scalar(na[:, :, :], nh[:, :, :], -0.2, 1.0, ALU.mult, ALU.add))
            c.link(v.tensor_tensor(ncc[:, :, :], na[:, :, :], nh[:, :, :], ALU.mult))
            c.link(v.scalar_tensor_tensor(na[:, :, :], nh[:, :, :], -1.0, ncc[:, :, :], ALU.add, ALU.mult))
            c.link(v.scalar_tensor_tensor(nx[:, :, :], na[:, :, :], 0.1, nb[:, :, :], ALU.add, ALU.add))

            layernorm_relu()
            c.link(v.tensor_tensor(ncc[:, :, :], nh[:, :, :], wide(dis[:, :]), ALU.mult))
            c.link(v.tensor_scalar(rows2[:, :, 0, :], ncc[:, :, :], SCALE16, None, ALU.mult))
            c.link(v.scalar_tensor_tensor(rows2[:, :, 1, :], ncc[:, :, :], SCALE16, rows2[:, :, 0, :],
                                          ALU.mult, ALU.subtract))
            dve.sem_inc(s_rows, 1)
            dve.sem_inc(s_gfree[2], 2)
            dve.sem_inc(s_ohfree[2], 2)
            dve.sem_inc(s_sfree[2], 2)
            STEPS2 = 2
            with dve.Fori(0, PAIRS) as i:
                c2 = Chain(dve, s_chain[2], i * (2 * STEPS2))
                for s in range(2):
                    dve.wait_ge(s_gat[2][s], (i + 1) * (CT * 16))
                    dve.wait_ge(s_sfree[2], 2 * i + s + 1)
                    c2.link(stage_low(i, s))
                    halves = gat[:, s, :, 0:C].bitcast(F16)
                    for q in range(2):
                        last = weigh(stat_h[:, s, q], halves[:, :, q * C:(q + 1) * C], i, s, 1)
                    c2.link(last)
                    dve.sem_inc(s_stat[2], 1)
                    dve.sem_inc(s_gfree[2], 1)
                    build_onehots(2, 2 * i + s, s, (1,))
                assert c2.n == 2 * STEPS2, c2.n

            sums_to(na, 2, "sums2")
            c.link(v.scalar_tensor_tensor(nb[:, :, :], na[:, :, :], 1.0 / SCALE16, ncc[:, :, :], ALU.mult, ALU.add))
            c.link(v.tensor_tensor(na[:, :, :], nb[:, :, :], wide(dis[:, :]), ALU.mult))
            dve.sem_inc(s_feat, 1)
            for q in range(H):
                dve.wait_ge(s_node, node_step[("turned", q)])
                v.tensor_copy(feat[0:C, 0, :], p_xt[0:C, 0:LO]).then_inc(s_feat, 1)
                dve.wait_ge(s_node, node_step[("features", q)])
                v.tensor_copy(feat[0:PC, 1, :], p_a[0:PC, 0:LO]).then_inc(s_feat, 1)
            dve.wait_ge(s_node, node_step[("update", H - 1)])
            c.link(v.tensor_tensor(nb[:, :, :], p_c[0:NP, 0:G * C].rearrange("p (g c) -> p g c", g=G),
                                   b2r_2[:, :].unsqueeze(1).to_broadcast((NP, G, C)), ALU.add))
            c.link(v.tensor_tensor(na[:, :, :], nb[:, :, :], nh[:, :, :], ALU.add))
            c.link(v.tensor_tensor(nx[:, :, :], nx[:, :, :], na[:, :, :], ALU.add))

            layernorm_relu()
            dve.sem_inc(s_feat, 1)
            for q in range(H):
                dve.wait_ge(s_node, node_step[("turned3", q)])
                v.tensor_copy(feat[0:C, 0, :], p_xt[0:C, 0:LO]).then_inc(s_feat, 1)
                dve.wait_ge(s_node, node_step[("rooted", q)])
                both = p_a[0:NP, 0:B * 2 * C].rearrange("p (b r c) -> p b r c", b=B, r=2)
                v.tensor_copy(rows3[:, q * B:(q + 1) * B, 1, :], both[:, :, 0, :])
                v.tensor_copy(ncc[:, q * B:(q + 1) * B, :], both[:, :, 1, :]).then_inc(s_feat, 1)
            v.tensor_copy(rows3[:, :, 0, :], nh[:, :, :]).then_inc(s_rows, 1)
            dve.sem_inc(s_gfree[3], 2)
            dve.sem_inc(s_ohfree[3], 2)
            dve.sem_inc(s_sfree[3], 2)
            dve.sem_inc(s_mfree[3], 2)
            STEPS3 = 2 * HALF + 7

            def use_weights(link, i, s, chunk, j):
                dve.wait_ge(s_mlp[3], chunk * HALF + j + 1)
                rows = gat[:, s, :, :].rearrange("p (u j) f -> p j u f", u=2)
                for u in range(2):
                    last = v.tensor_tensor(pr[:, u], p_w[j % 2][0:EP, u * OO:(u + 1) * OO].rearrange("p (i o) -> p i o", i=C),
                                           rows[:, j, u, 0:C].unsqueeze(2).to_broadcast((EP, C, C)), ALU.mult)
                link(last)
                dve.sem_inc(s_mfree[3], 1)
                link(v.tensor_reduce(m[:, :, 0, :].rearrange("p (u j) c -> p j u c", u=2)[:, j],
                                     pr[:, :, :, :].rearrange("p u i o -> p u o i"), AX_X, ALU.add))

            def weigh_messages(link, i, s, chunk):
                link(v.tensor_tensor(m[:, :, 1, :], m[:, :, 0, :], gat[:, s, :, C:2 * C], ALU.add))
                dve.sem_inc(s_gfree[3], 1)
                split3(link, m[:, :, 1, :])
                dve.wait_ge(s_sfree[3], chunk + 1)
                link(stage_low(i, s))
                for q in range(3):
                    last = weigh(stat_m[:, s, q], part_b[:, q], i, s, 1)
                link(last)
                dve.sem_inc(s_stat[3], 1)

            def finish_and_begin(link, i, s, chunk, i_next):
                weigh_messages(link, i, s, chunk)
                dve.wait_ge(s_gat[3][1 - s], (i_next + 1) * (CT * 16))
                for g in range(HALF):
                    onehots(3, chunk, s, g, 2, (1,))
                    use_weights(link, i_next, 1 - s, chunk + 1, g)

            dve.wait_ge(s_gat[3][0], CT * 16)
            for j in range(HALF):
                use_weights(c.link, 0, 0, 0, j)
            with dve.Fori(0, PAIRS - 1) as i:
                c3 = Chain(dve, s_chain[3], i * (2 * STEPS3))
                finish_and_begin(c3.link, i, 0, 2 * i, i)
                finish_and_begin(c3.link, i, 1, 2 * i + 1, i + 1)
                assert c3.n == 2 * STEPS3, c3.n
            finish_and_begin(c.link, PAIRS - 1, 0, CHUNKS - 2, PAIRS - 1)
            weigh_messages(c.link, PAIRS - 1, 1, CHUNKS - 1)
            for g in range(HALF):
                onehots(3, CHUNKS - 1, 1, g, 2, (1,))

            sums_to(na, 3, "sums3")
            c.link(v.tensor_tensor(nb[:, :, :], na[:, :, :], ncc[:, :, :], ALU.add))
            c.link(v.tensor_tensor(nx[:, :, :], nx[:, :, :], nb[:, :, :], ALU.add))
            dve.sem_inc(s_rows, 1)

        @block.tensor
        def _(pe):
            te = nc.tensor
            acc = p_acc[0:NP, 0:LO]

            def clear(last=False):
                return te.matmul(acc, zeros[0:1, 0:NP], zeros[0:1, :], start=not last, stop=last,
                                 skip_group_check=True)

            def turn_sums(n):
                pe.wait_ge(s_accs, n + 1)
                for b in range(B):
                    last = te.transpose(p_a[0:NP, b * NP:(b + 1) * NP], accs[:, b * NP:(b + 1) * NP],
                                        identity[0:NP, 0:NP])
                last.then_inc(s_node, 1)

            def scatter_group(n, chunk, s, g, og, terms, masks):
                pe.wait_ge(s_oh[n], chunk * (CT // og) + g + 1)
                for k in range(og):
                    for d, q in terms:
                        last = te.matmul(acc, masks[:, s, q, g * og + k, :], onehot[:, g % 2, d, k, :],
                                         start=False, stop=False, skip_group_check=True)
                last.then_inc(s_ohfree[n], 1)

            def masks_used(n):
                te.matmul(acc, zeros[0:1, 0:NP], zeros[0:1, :], start=False, stop=False,
                          skip_group_check=True).then_inc(s_sfree[n], 1)

            def scatter(n, chunk, s, terms, masks):
                pe.wait_ge(s_stat[n], chunk + 1)
                for g in range(CT // OG):
                    scatter_group(n, chunk, s, g, OG, terms, masks)
                masks_used(n)

            pe.wait_ge(s_zero, 1)
            te.matmul(p_a[0:NP, 0:2 * G], zeros[0:1, 0:NP], zeros[0:1, 0:2 * G], start=True, stop=False,
                      skip_group_check=True)
            DC = 8
            dig_p = stat_m[:, :, :, :, :].rearrange("p s a t k -> p (s a t k)")
            dig_g = onehot[:, :, :, :, :].rearrange("p r e o k -> p (r e o k)")
            with pe.Fori(0, TILES // DC // 2) as i:
                for s in range(2):
                    pe.wait_ge(s_cnt_oh, 2 * i + s + 1)
                    a = dig_p[:, s * 2 * DC * NP:(s + 1) * 2 * DC * NP].rearrange("p (d t k) -> p d t k", d=2, t=DC)
                    b = dig_g[:, s * 2 * DC * G:(s + 1) * 2 * DC * G].rearrange("p (d t k) -> p d t k", d=2, t=DC)
                    for d in range(2):
                        for t in range(DC):
                            last = te.matmul(p_a[0:NP, d * G:(d + 1) * G], a[:, d, t, :], b[:, d, t, :],
                                             start=False, stop=False, skip_group_check=True)
                    last.then_inc(s_cnt_mm, 1)
            te.matmul(p_a[0:NP, 0:2 * G], zeros[0:1, 0:NP], zeros[0:1, 0:2 * G], start=False, stop=True,
                      skip_group_check=True).then_inc(s_node, 1)

            clear()
            pe.wait_ge(s_w, 16 * W_LOADS)
            pe.wait_ge(s_const, 2)

            def mlp0(i, s, i2):
                pe.wait_ge(s_packed, i2 + 1)
                for q in range(4):
                    last = te.transpose(p_xt[:, q * EP:(q + 1) * EP],
                                        packed[:, 4 * q:4 * q + 4, :, :].rearrange("p t d c -> p (t d c)"),
                                        identity[0:EP, 0:EP])
                last.then_inc(s_xt[0], 1)
                pe.wait_ge(s_xts[0], i2 + 1)
                for j in range(4):
                    if j >= 2:
                        pe.wait_ge(s_hs[0], i2 * 4 + j - 1)
                    te.matmul(p_hid[j % 2][:, 0:4 * EP], w1_0[:, j, :],
                              xt[:, :, :].rearrange("p q e -> p (q e)"), start=True, stop=True).then_inc(s_hp[0], 1)
                pe.wait_ge(s_mfree[0], i2 + 1)
                for j in range(4):
                    pe.wait_ge(s_hs[0], i2 * 4 + j + 1)
                    for q in range(4):
                        t = 4 * q + j
                        last = te.matmul(p_ab[s][0:EP, t * 2 * C:(t + 1) * 2 * C], hid[:, j, q * EP:(q + 1) * EP],
                                         w2_0[:, :], start=True, stop=True)
                last.then_inc(s_mlp[0], 1)

            terms0 = ((0, 0), (0, 1), (1, 2), (1, 3))
            mlp0(0, 0, 0)
            with pe.Fori(0, PAIRS - 1) as i:
                mlp0(i, 1, 2 * i + 1)
                scatter(0, 2 * i, 0, terms0, stat_h)
                mlp0(i + 1, 0, 2 * i + 2)
                scatter(0, 2 * i + 1, 1, terms0, stat_h)
            mlp0(PAIRS - 1, 1, CHUNKS - 1)
            scatter(0, CHUNKS - 2, 0, terms0, stat_h)
            scatter(0, CHUNKS - 1, 1, terms0, stat_h)
            clear(last=True).then_inc(s_done, 1)
            turn_sums(0)

            for n, terms, masks in ((1, ((0, 0), (0, 1), (0, 2)), stat_m), (2, ((1, 0), (1, 1)), stat_h)):
                clear()
                with pe.Fori(0, PAIRS) as i:
                    for s in range(2):
                        scatter(n, 2 * i + s, s, terms, masks)
                clear(last=True).then_inc(s_done, 1)
                turn_sums(n)

            copied = 1
            pe.wait_ge(s_feat, copied)
            for q in range(H):
                for b in range(B):
                    last = te.transpose(p_xt[0:C, b * NP:(b + 1) * NP], na[:, q * B + b, :], identity[0:NP, 0:NP])
                last.then_inc(s_node, 1)
                copied += 1
                pe.wait_ge(s_feat, copied)
                te.matmul(p_a[0:PC, 0:LO], wg[:, :], feat[0:C, 0, :], start=True, stop=True).then_inc(s_node, 1)
                copied += 1
                pe.wait_ge(s_feat, copied)
                te.matmul(p_b[0:H2, 0:LO], w1_2[:, :], feat[0:PC, 1, :], start=True, stop=True).then_inc(s_node, 1)
                copied += 1
                pe.wait_ge(s_feat, copied)
                for b in range(B):
                    g = q * B + b
                    last = te.matmul(p_c[0:NP, g * C:(g + 1) * C], feat[0:H2, 2, b * NP:(b + 1) * NP], w2_2[:, :],
                                     start=True, stop=True)
                last.then_inc(s_node, 1)

            copied += 1
            pe.wait_ge(s_feat, copied)
            for q in range(H):
                for b in range(B):
                    last = te.transpose(p_xt[0:C, b * NP:(b + 1) * NP], nh[:, q * B + b, :], identity[0:NP, 0:NP])
                last.then_inc(s_node, 1)
                copied += 1
                pe.wait_ge(s_feat, copied)
                for b in range(B):
                    last = te.matmul(p_a[0:NP, b * 2 * C:(b + 1) * 2 * C], feat[0:C, 0, b * NP:(b + 1) * NP],
                                     zr_3[:, :, :].rearrange("i r o -> i (r o)"), start=True, stop=True)
                last.then_inc(s_node, 1)
                copied += 1
                pe.wait_ge(s_feat, copied)

            clear()

            def hidden3(i, s, i2):
                pe.wait_ge(s_ea[s], (i + 1) * 16)
                for u in range(2):
                    last = te.transpose(p_xt[:, u * EP:(u + 1) * EP],
                                        ea[:, s, u * HALF:(u + 1) * HALF, :].rearrange("p t c -> p (t c)"),
                                        identity[0:EP, 0:EP])
                last.then_inc(s_xt[3], 1)
                pe.wait_ge(s_xts[3], i2 + 1)
                for jj in range(4):
                    if jj >= 2:
                        pe.wait_ge(s_hs[3], i2 * 4 + jj - 1)
                    for k in range(2):
                        last = te.matmul(p_hid[jj % 2][:, k * 2 * EP:(k + 1) * 2 * EP], w1z_3[:, 2 * jj + k, :],
                                         xt[:, 0:2, :].rearrange("p u e -> p (u e)"), start=True, stop=True)
                    last.then_inc(s_hp[3], 1)

            def weights3(s, i2, j):
                pe.wait_ge(s_hs[3], i2 * 4 + j // 2 + 1)
                pe.wait_ge(s_mfree[3], i2 * HALF + j + 1)
                for u in range(2):
                    at = ((j % 2) * 2 + u) * EP
                    last = te.matmul(p_w[j % 2][0:EP, u * OO:(u + 1) * OO], hid[:, j // 2, at:at + EP],
                                     w2s_3[:, :], start=True, stop=True)
                last.then_inc(s_mlp[3], 1)

            def scatter_and_weights(chunk, s, i_next):
                hidden3(i_next, 1 - s, chunk + 1)
                pe.wait_ge(s_stat[3], chunk + 1)
                for g in range(HALF):
                    scatter_group(3, chunk, s, g, 2, terms3, stat_m)
                    weights3(1 - s, chunk + 1, g)
                masks_used(3)

            terms3 = ((1, 0), (1, 1), (1, 2))
            pe.sem_inc(s_xt[3], 2)
            hidden3(0, 0, 0)
            for j in range(HALF):
                weights3(0, 0, j)
            with pe.Fori(0, PAIRS - 1) as i:
                scatter_and_weights(2 * i, 0, i)
                scatter_and_weights(2 * i + 1, 1, i + 1)
            scatter_and_weights(CHUNKS - 2, 0, PAIRS - 1)
            pe.wait_ge(s_stat[3], CHUNKS)
            for g in range(HALF):
                scatter_group(3, CHUNKS - 1, 1, g, 2, terms3, stat_m)
            masks_used(3)
            clear(last=True).then_inc(s_done, 1)
            turn_sums(3)


W_LOADS = 1 + 4 * 3 + 2 * 3 + 5 + 8 + 4


_INS = ["x", "src", "dst", "edge_attr_16", "edge_weight", "L0_gnn_W1", "L0_gnn_b1", "L0_gnn_W2", "L0_gnn_b2",
        "L2_gnn_W_gcn", "L2_gnn_W1", "L2_gnn_b1", "L2_gnn_W2", "L2_gnn_b2",
        "L3_gnn_W1", "L3_gnn_b1", "L3_gnn_W2", "L3_gnn_b2", "L3_gnn_root"]
_TURNED = {"L0_gnn_W1", "L0_gnn_W2", "L2_gnn_W_gcn", "L2_gnn_W1", "L2_gnn_W2"}


def kernel(**inputs):
    import numpy as _np
    import concourse.bacc as _bacc
    from concourse import mybir as _mybir
    from concourse.bass_utils import run_bass_kernel_spmd as _run

    nc = _bacc.Bacc("TRN2", target_bir_lowering=False, num_devices=1)
    arrays, args = {}, []
    for name in _INS:
        a = _np.asarray(inputs[name])
        a = _np.ascontiguousarray(a.T if name in _TURNED else a)
        arrays[f"in_{name}_dram"] = a
        args.append(nc.dram_tensor(f"in_{name}_dram", a.shape, _mybir.dt.from_np(a.dtype), kind="ExternalInput").ap())
    args.append(nc.dram_tensor("out_0_dram", (N, C), F32, kind="ExternalOutput").ap())
    gnn_program(nc, *args)
    r = _run(nc, [arrays], core_ids=[0])
    return r.results[0]["out_0_dram"]
```

```python
from contextlib import ExitStack

import concourse.bass as bass
from concourse import mybir

ALU = mybir.AluOpType
ACT = mybir.ActivationFunctionType
AX_X = mybir.AxisListType.X
F32 = mybir.dt.float32
F16 = mybir.dt.float16
BF16 = mybir.dt.bfloat16
I32 = mybir.dt.int32

N = 3125
C = 16
E = 100000
EP = 125
TILES = E // EP
CT = 16
CHUNKS = TILES // CT
PAIRS = CHUNKS // 2
NP = 112
G = 28
H = 7
LO = NP * G // H
B = LO // NP
FULL = N // NP
TAIL = N - FULL * NP
R0 = 20
OG = 4
HALF = CT // 2
DC = 8
BT = 160
BLOCKS = TILES // BT
BP = BT // (2 * CT)
BZ = 32
MAGIC = float(3 * 2 ** 22)
SCALE16 = 8192.0
EPS = 1e-5


class Chain:

    def __init__(self, engine, sem, base=0):
        self.engine, self.sem, self.base, self.n = engine, sem, base, 0

    def mark(self, ins):
        self.n += 1
        ins.then_inc(self.sem, 1)

    def link(self, ins):
        self.mark(ins)
        self.engine.wait_ge(self.sem, self.base + self.n)


def gnn_program(nc, x, src, dst, edge_attr, edge_weight, w1_0t, b1_0, w2_0t, b2_0,
                wg_t, w1_2t, b1_2, w2_2t, b2_2, w1_3, b1_3, w2_3, b2_3, root, out):
    H0 = b1_0.shape[0]
    H2 = b1_2.shape[0]
    PC = wg_t.shape[1]
    H3 = b1_3.shape[0]
    OO = C * C

    table0 = nc.dram_tensor("table0", (NP * G, R0), F32, kind="Internal").ap()
    table1 = nc.dram_tensor("table1", (NP * G, C), F32, kind="Internal").ap()
    table2 = nc.dram_tensor("table2", (NP * G, 2 * C), F16, kind="Internal").ap()
    table2f = nc.dram_tensor("table2f", (NP * G, C), F32, kind="Internal").ap()
    starts = nc.dram_tensor("starts", (E + NP * G, R0), F32, kind="Internal").ap()
    running = nc.dram_tensor("running", (E, C), F32, kind="Internal").ap()
    table3 = nc.dram_tensor("table3", (NP * G, 2 * C), F32, kind="Internal").ap()

    with ExitStack() as ctx:
        def sb(name, shape, dt=F32):
            return ctx.enter_context(nc.sbuf_tensor(name, shape, dt))

        def ps(name, shape=(128, 512)):
            return ctx.enter_context(nc.psum_tensor(name, list(shape), F32))

        def sem(name):
            return ctx.enter_context(nc.semaphore(name))

        identity = sb("identity", [128, 128])
        iota_lo_i = sb("iota_lo_i", [128, LO], I32)
        iota_lo = sb("iota_lo", [128, LO], F16)
        zeros = sb("zeros", [128, LO], BF16)
        w1_0 = sb("w1_0", [128, 4, 2 * H0])
        b1c_0 = sb("b1c_0", [128, 1])
        w2_0 = sb("w2_0", [128, 2 * C])
        b2r_0 = sb("b2r_0", [EP, 2, C])
        wg = sb("wg", [C, PC])
        w1_2 = sb("w1_2", [PC, H2])
        b1c_2 = sb("b1c_2", [H2, 1])
        w2_2 = sb("w2_2", [H2, C])
        b2r_2 = sb("b2r_2", [NP, C])
        w1z_3 = sb("w1z_3", [128, 8, H3])
        b1c_3 = sb("b1c_3", [H3, 1])
        w2s_3 = sb("w2s_3", [H3, OO])
        zr_3 = sb("zr_3", [C, 2, C])

        ends = sb("ends", [EP, 2, TILES], I32)
        ew = sb("ew", [EP, TILES])
        lo_s = sb("lo_s", [EP, TILES])
        hmask_s = sb("hmask_s", [EP, H, TILES], BF16)
        same = sb("same", [EP, TILES])
        nxt = sb("nxt", [EP, 1], I32)
        nxt_f = sb("nxt_f", [EP, 1])
        cont = sb("cont", [EP, 1])
        viol = sb("viol", [EP, 2])
        viol_f = sb("viol_f", [EP, 1])
        flag = sb("flag", [1, 1], I32)
        dig_l = sb("dig_l", [EP, 2])

        wide = sb("wide", [EP, TILES, C])
        flat = wide[:, :, :].rearrange("p t c -> p (t c)")
        W0 = 2 * TILES
        n_f = flat[:, 0:W0].rearrange("p (d t) -> p d t", d=2)
        t_f = flat[:, W0:2 * W0].rearrange("p (d t) -> p d t", d=2)
        group = flat[:, 2 * W0:2 * W0 + TILES].bitcast(F16).rearrange("p (d t) -> p d t", d=2)
        place = flat[:, 2 * W0 + TILES:3 * W0].bitcast(F16).rearrange("p (d t) -> p d t", d=2)
        lo_d = flat[:, 3 * W0:3 * W0 + TILES]
        hmask_d = flat[:, 4 * W0:4 * W0 + TILES * H // 2].bitcast(BF16).rearrange("p (h t) -> p h t", h=H)
        iota_kt_i = flat[:, 7 * W0:7 * W0 + NP * DC].bitcast(I32)
        zero_rows = flat[:, 8 * W0 - BZ * R0:8 * W0]
        lo = (lo_s[:, :], lo_d)
        hmask = (hmask_s[:, :, :], hmask_d)
        iota_kt = sb("iota_kt", [EP, NP, DC], F16)

        nx = sb("nx", [NP, G, C])
        nh = sb("nh", [NP, G, C])
        na = sb("na", [NP, G, C])
        nb = sb("nb", [NP, G, C])
        ncc = sb("ncc", [NP, G, C])
        stat = sb("stat", [NP, 4, G])
        degs = sb("degs", [NP, 2, G])
        rdeg = sb("rdeg", [NP, G])
        dis = sb("dis", [NP, G])
        rows0 = sb("rows0", [NP, G, R0])
        rows2 = sb("rows2", [NP, G, 2, C], F16)
        rows3 = sb("rows3", [NP, G, 2, C])
        accs = sb("accs", [NP, LO])

        rd = sb("rd", [EP, TILES])
        upper = sb("upper", [NP, NP])
        ones = sb("ones", [128, NP])
        pos = sb("pos", [NP, 2, G])
        has = sb("has", [NP, G])
        spare_i = sb("spare_i", [NP, G], I32)
        spare = sb("spare", [NP, G])
        last_edge = sb("last_edge", [NP, G], I32)
        first_edge = sb("first_edge", [NP, G], I32)
        last_rows = sb("last_rows", [NP, G, C])
        first_rows = sb("first_rows", [EP, R0])
        oh_place = sb("oh_place", [EP, NP])
        oh_group = sb("oh_group", [EP, G])
        crhs = sb("crhs", [EP, G, C])
        tail = sb("tail", [EP, C])

        istage = sb("istage", [EP, 2, 2, CT], I32)
        gat = sb("gat", [EP, 2, CT, 2 * R0])
        lstage = sb("lstage", [EP, 2, 2, CT])
        onehot = sb("onehot", [EP, 2, 2, OG, LO], BF16)
        stat_m = sb("stat_m", [EP, 2, 4, H * C, CT], BF16)
        stat_h = stat_m[:, :, :, :, :].bitcast(F16)
        ab = sb("ab", [EP, CT, 2, C])
        prod = sb("prod", [EP, CT, 7, C])
        dots = sb("dots", [EP, CT, 7])
        inv = sb("inv", [EP, CT, 2])
        co = sb("co", [EP, CT, 2])
        cx = sb("cx", [EP, CT, 2])
        ga = sb("ga", [EP, CT, 2])
        m = sb("m", [EP, CT, 2, C])
        mt = sb("mt", [EP, CT, 2, C])
        part_h = sb("part_h", [EP, 2, 2, C, CT], F16)
        part_b = sb("part_b", [EP, 3, C, CT], BF16)
        packed = sb("packed", [EP, 2, CT, 2, C])
        rs = sb("rs", [EP, 2, CT])
        xt = sb("xt", [128, 4, EP])
        hid = sb("hid", [128, 4, 4 * EP])
        ea = sb("ea", [EP, 2, CT, C])
        pr = sb("pr", [EP, 2, C, C])
        feat = sb("feat", [128, 3, 4 * NP])

        p_acc = ps("p_acc")
        p_xt = ps("p_xt")
        p_a = ps("p_a")
        p_b = ps("p_b")
        p_c = ps("p_c")
        p_d = ps("p_d")
        p_e = ps("p_e")
        p_hid = [p_a, p_b]
        p_ab = [p_c, p_d]
        p_w = [p_c, p_d, p_e, p_acc]

        s_in = sem("s_in")
        s_w = sem("s_w")
        s_const = sem("s_const")
        s_zero = sem("s_zero")
        s_tab = sem("s_tab")
        s_out = sem("s_out")
        s_dve = sem("s_dve")
        s_sq = sem("s_sq")
        s_rt = sem("s_rt")
        s_rows = sem("s_rows")
        s_cnt_oh = sem("s_cnt_oh")
        s_cnt_mm = sem("s_cnt_mm")
        s_acc0 = sem("s_acc0")
        s_done = sem("s_done")
        s_accs = sem("s_accs")
        s_node = sem("s_node")
        s_feat = sem("s_feat")
        s_stage = sem("s_stage")
        s_viol = sem("s_viol")
        s_flag = sem("s_flag")
        s_fill = sem("s_fill")
        s_deg = sem("s_deg")
        s_pos = sem("s_pos")
        s_put = sem("s_put")
        s_first = sem("s_first")
        s_z = [sem(f"s_z{b}") for b in range(2)]
        s_zfree = sem("s_zfree")
        s_xd = sem("s_xd")
        s_ab = sem("s_ab")
        s_squares = sem("s_squares")
        s_blk = sem("s_blk")
        s_sd = sem("s_sd")
        s_last = sem("s_last")
        s_crhs = sem("s_crhs")
        s_placed = sem("s_placed")
        s_pool = sem("s_pool")
        L = range(4)
        s_gat = [[sem(f"s_gat{n}_{s}") for s in range(2)] for n in L]
        s_gfree = [sem(f"s_gfree{n}") for n in L]
        s_chain = [sem(f"s_chain{n}") for n in L]
        s_stat = [sem(f"s_stat{n}") for n in L]
        s_oh = [sem(f"s_oh{n}") for n in L]
        s_ohfree = [sem(f"s_ohfree{n}") for n in L]
        s_sfree = [sem(f"s_sfree{n}") for n in L]
        s_xt = {n: sem(f"s_xt{n}") for n in (0, 3)}
        s_xts = {n: sem(f"s_xts{n}") for n in (0, 3)}
        s_hp = {n: sem(f"s_hp{n}") for n in (0, 3)}
        s_hs = {n: sem(f"s_hs{n}") for n in (0, 3)}
        s_mlp = {n: sem(f"s_mlp{n}") for n in (0, 3)}
        s_mfree = {n: sem(f"s_mfree{n}") for n in (0, 3)}
        s_ea = [sem(f"s_ea{s}") for s in range(2)]
        s_packed = sem("s_packed")
        s_msg = sem("s_msg")
        s_p1 = sem("s_p1")

        x_groups = x[0:FULL * NP, :].rearrange("(g p) c -> p g c", p=NP)
        x_tail = x[FULL * NP:N, :]
        out_groups = out[0:FULL * NP, :].rearrange("(g p) c -> p g c", p=NP)
        out_tail = out[FULL * NP:N, :]
        ea_rows = edge_attr.rearrange("(p t) c -> p (t c)", p=EP)

        def rows_of(table):
            return table.rearrange("(g p) c -> p g c", p=NP)

        dig_p = stat_m[:, :, :, :, :].rearrange("p s a k t -> p (s a k t)")
        dig_g = onehot[:, :, :, :, :].rearrange("p r e o k -> p (r e o k)")

        def digits(s):
            a = dig_p[:, s * 2 * DC * NP:(s + 1) * 2 * DC * NP].rearrange("p (d k t) -> p d k t", d=2, t=DC)
            b = dig_g[:, s * 2 * DC * G:(s + 1) * 2 * DC * G].rearrange("p (d k t) -> p d k t", d=2, t=DC)
            return a, b

        def onehot_row(ring, g, d, k):
            return onehot[:, g % 2, d, k, :] if ring == 2 else onehot[:, g // 2 % 2, g % 2, k, :]

        zb = dig_p.bitcast(F32)[:, 0:2 * BT * R0].rearrange("p (b t f) -> p b t f", b=2, f=R0)

        block = ctx.enter_context(nc.Block())

        def numbered(names):
            return {what: n + 1 for n, what in enumerate(names)}

        products = [(what, q) for q in range(H) for what in ("turned", "features", "hidden", "update")]
        rooted = [(what, q) for q in range(H) for what in ("turned3", "rooted")]
        node_step = numbered(["degrees", "unsorted", "within"])
        any_step = numbered([*node_step, "sums0", "sums1", "sums2", *products, *rooted, "sums3"])
        sorted_step = numbered([*node_step, "carry0", "sums0", "sums1", "carry2", *products, *rooted, "carry3"])

        @block.sync
        def _(sp):
            sp.dma_start(ends[:, 0, :], src.rearrange("(p t) -> p t", p=EP)).then_inc(s_in, 16)
            sp.dma_start(ends[:, 1, :], dst.rearrange("(p t) -> p t", p=EP)).then_inc(s_in, 16)
            sp.wait_ge(s_zero, 1)
            with nc.allow_non_contiguous_dma(reason="one destination for each partition"):
                sp.dma_start(nxt[0:EP - 1, :], dst.rearrange("(p t) -> p t", p=EP)[1:EP, 0:1]).then_inc(s_in, 16)
            sp.dma_start(nx[:, 0:FULL, :], x_groups).then_inc(s_in, 16)
            sp.dma_start(nx[0:TAIL, FULL, :], x_tail).then_inc(s_in, 16)
            sp.dma_start(starts[0:E, :].rearrange("(p a b) f -> p a (b f)", p=EP, b=BZ),
                         zero_rows.unsqueeze(1).to_broadcast((EP, TILES // BZ, BZ * R0))).then_inc(s_fill, 16)
            sp.dma_start(ew[:, :], edge_weight.rearrange("(p t) -> p t", p=EP)).then_inc(s_w, 16)
            for j in range(4):
                r = 2 * C * j
                sp.dma_start(w1_0[r:r + 2 * C, j, 0:H0], w1_0t).then_inc(s_w, 16)
                sp.dma_start(w1_0[r:r + C, j, H0:2 * H0], w1_0t[C:2 * C, :]).then_inc(s_w, 16)
                sp.dma_start(w1_0[r + C:r + 2 * C, j, H0:2 * H0], w1_0t[0:C, :]).then_inc(s_w, 16)
            for d in range(2):
                sp.dma_start(b1c_0[d * H0:(d + 1) * H0, :], b1_0.rearrange("(k a) -> k a", a=1)).then_inc(s_w, 16)
                sp.dma_start(w2_0[d * H0:(d + 1) * H0, d * C:(d + 1) * C], w2_0t).then_inc(s_w, 16)
                sp.dma_start(b2r_0[:, d, :], b2_0.rearrange("(a c) -> a c", a=1).to_broadcast((EP, C))).then_inc(s_w, 16)
            sp.dma_start(wg[:, :], wg_t).then_inc(s_w, 16)
            sp.dma_start(w1_2[:, :], w1_2t).then_inc(s_w, 16)
            sp.dma_start(b1c_2[:, :], b1_2.rearrange("(k a) -> k a", a=1)).then_inc(s_w, 16)
            sp.dma_start(w2_2[:, :], w2_2t).then_inc(s_w, 16)
            sp.dma_start(b2r_2[:, :], b2_2.rearrange("(a c) -> a c", a=1).to_broadcast((NP, C))).then_inc(s_w, 16)
            for j in range(8):
                sp.dma_start(w1z_3[j * C:(j + 1) * C, j, :], w1_3).then_inc(s_w, 16)
            sp.dma_start(b1c_3[:, :], b1_3.rearrange("(k a) -> k a", a=1)).then_inc(s_w, 16)
            sp.dma_start(w2s_3[:, :], w2_3).then_inc(s_w, 16)
            sp.dma_start(zr_3[:, 0, :], b2_3.rearrange("(i o) -> i o", i=C)).then_inc(s_w, 16)
            sp.dma_start(zr_3[:, 1, :], root).then_inc(s_w, 16)
            sp.wait_ge(s_rows, 1)
            sp.dma_start(rows_of(table0), rows0[:, :, :]).then_inc(s_tab, 16)
            rows_3 = rows3[:, :, :, :].rearrange("p g a c -> p g (a c)")

            def load_attributes(i):
                for s in range(2):
                    sp.wait_ge(s_xt[3], 2 * i + s + 1)
                    sp.dma_start(ea[:, s, :, :].rearrange("p t c -> p (t c)"),
                                 ea_rows[:, bass.ds(i * (2 * CT * C) + s * CT * C, CT * C)]).then_inc(s_ea[s], 16)

            def any_order():
                for n, (table, rows) in enumerate((
                        (table1, nh[:, :, :]),
                        (table2, rows2[:, :, :, :].rearrange("p g a c -> p g (a c)")), (table3, rows_3))):
                    sp.wait_ge(s_rows, n + 2)
                    sp.dma_start(rows_of(table), rows).then_inc(s_tab, 16)
                with sp.Fori(0, PAIRS) as i:
                    load_attributes(i)

            def sorted_order():
                starts_rows = starts[0:E, :].rearrange("(p t) f -> p (t f)", p=EP)
                running_rows = running.rearrange("(p t) c -> p (t c)", p=EP)

                def load_starts(n):
                    sp.wait_ge(s_put, 16 * G * (n + 1))
                    for b in range(BLOCKS):
                        use = n * BLOCKS + b
                        if use >= 2:
                            sp.wait_ge(s_zfree, use - 1)
                        sp.dma_start(zb[0:EP, use % 2, :, :].rearrange("p t f -> p (t f)"),
                                     starts_rows[:, b * BT * R0:(b + 1) * BT * R0]).then_inc(s_z[use % 2], 16)

                def store_running(k, o):
                    sp.wait_ge(s_blk, o + (k * BLOCKS + 1))
                    sp.dma_start(running_rows[:, bass.ds(o * (BT * C), BT * C)],
                                 wide[:, bass.ds(o * BT, BT), :].rearrange("p t c -> p (t c)")).then_inc(s_sd, 16)

                load_starts(0)
                with sp.Fori(0, BLOCKS) as o:
                    store_running(0, o)
                sp.wait_ge(s_rows, 2)
                sp.dma_start(rows_of(table1), nh[:, :, :]).then_inc(s_tab, 16)
                load_starts(1)
                sp.wait_ge(s_rows, 3)
                sp.dma_start(rows_of(table2f), ncc[:, :, :]).then_inc(s_tab, 16)
                with sp.Fori(0, BLOCKS) as o:
                    store_running(1, o)
                sp.wait_ge(s_rows, 4)
                sp.dma_start(rows_of(table3), rows_3).then_inc(s_tab, 16)
                with sp.Fori(0, BP) as k:
                    load_attributes(k)
                with sp.Fori(0, BLOCKS - 1) as o:
                    load_attributes(o * BP + BP)
                    store_running(2, o)
                    with sp.Fori(1, BP) as k:
                        load_attributes(o * BP + BP + k)
                store_running(2, BLOCKS - 1)

            sp.wait_ge(s_flag, 1)
            is_sorted = sp.value_load(flag[0:1, 0:1], min_val=0, max_val=1)
            with sp.If(is_sorted):
                sorted_order()
            with sp.Else():
                any_order()
            sp.wait_ge(s_rows, 5)
            sp.dma_start(out_groups, nx[:, 0:FULL, :]).then_inc(s_out, 16)
            sp.dma_start(out_tail, nx[0:TAIL, FULL, :]).then_inc(s_out, 16)
            sp.wait_ge(s_out, 32)
            sp.wait_ge(s_fill, 16)

        @block.gpsimd
        def _(pool):
            pool.memset(identity[:, :], 0.0).then_inc(s_const, 1)
            pool.wait_ge(s_const, 1)
            pool.affine_select(out=identity[:, :], in_=identity[:, :], compare_op=ALU.not_equal, fill=1.0,
                               base=0, pattern=[[-1, 128]], channel_multiplier=1).then_inc(s_const, 1)
            pool.iota(iota_lo_i[:, :], [[1, LO]], base=0, channel_multiplier=0).then_inc(s_const, 1)
            pool.iota(iota_kt_i.rearrange("p (k t) -> p k t", t=DC), [[1, NP], [0, DC]], base=0,
                      channel_multiplier=0).then_inc(s_const, 1)
            pool.iota(spare_i[:, :], [[NP, G]], base=E, channel_multiplier=1).then_inc(s_const, 1)
            pool.memset(ones[:, :], 1.0).then_inc(s_const, 1)
            pool.memset(upper[:, :], 1.0).then_inc(s_const, 1)
            pool.wait_ge(s_const, 7)
            pool.affine_select(out=upper[:, :], in_=upper[:, :], compare_op=ALU.is_ge, fill=0.0,
                               base=0, pattern=[[1, NP]], channel_multiplier=-1).then_inc(s_const, 1)
            pool.wait_ge(s_in, 80)

            def gather_chunks(n, table, ends_of, row):
                pool.wait_ge(s_tab, 16 * (n + 1))
                with pool.Fori(0, PAIRS) as i:
                    for s in range(2):
                        pool.wait_ge(s_gfree[n], 2 * i + s + 1)
                        pool.sem_inc(s_pool, 1)
                        pool.tensor_copy(istage[:, s, :, :], ends[:, :, bass.ds(i * (2 * CT) + s * CT, CT)]).then_inc(s_stage, 1)
                        pool.wait_ge(s_stage, 2 * i + s + 1 + n * CHUNKS)
                        pool.sem_inc(s_pool, 1)
                        for t in range(CT):
                            for d in ends_of:
                                pool.indirect_dma_start(row(s, t, d), None, table,
                                                        bass.IndirectOffsetOnAxis(istage[:, s, d, t:t + 1], 0)
                                                        ).then_inc(s_gat[n][s], 16)

            def any_order():
                gather_chunks(0, table0, (0, 1), lambda s, t, d: gat[:, s, t, d * R0:(d + 1) * R0])
                gather_chunks(1, table1, (0, 1), lambda s, t, d: gat[:, s, t, d * R0:d * R0 + C])
                gather_chunks(2, table2, (0,), lambda s, t, d: gat[:, s, t, 0:C].bitcast(F16))
                gather_chunks(3, table3, (0,), lambda s, t, d: gat[:, s, t, 0:2 * C])

            def sorted_order():
                def put_rows(n, table):
                    pool.wait_ge(s_rows, n + 1)
                    for g in range(G):
                        pool.indirect_dma_start(starts, bass.IndirectOffsetOnAxis(first_edge[:, g:g + 1], 0),
                                                rows0[:, g, :], None).then_inc(s_put, 16)
                    pool.wait_ge(s_tab, 16 * (n + 1))
                    pool.indirect_dma_start(first_rows[:, 0:table.shape[1]], None, table,
                                            bass.IndirectOffsetOnAxis(ends[:, 1, 0:1], 0)).then_inc(s_first, 16)

                def get_last(k):
                    pool.wait_ge(s_sd, 16 * BLOCKS * (k + 1))
                    for g in range(G):
                        pool.indirect_dma_start(last_rows[:, g, :], None, running,
                                                bass.IndirectOffsetOnAxis(last_edge[:, g:g + 1], 0)).then_inc(s_last, 16)

                pool.wait_ge(s_pos, 1)
                pool.wait_ge(s_fill, 16)
                put_rows(0, table0)
                gather_chunks(0, table0, (0,), lambda s, t, d: gat[:, s, t, 0:R0])
                get_last(0)
                put_rows(1, table1)
                gather_chunks(1, table1, (0,), lambda s, t, d: gat[:, s, t, 0:C])
                gather_chunks(2, table2f, (0,), lambda s, t, d: gat[:, s, t, 0:C])
                get_last(1)
                gather_chunks(3, table3, (0,), lambda s, t, d: gat[:, s, t, 0:2 * C])
                get_last(2)

            pool.wait_ge(s_flag, 1)
            is_sorted = pool.value_load(flag[0:1, 0:1], min_val=0, max_val=1)
            with pool.If(is_sorted):
                sorted_order()
            with pool.Else():
                any_order()

        @block.scalar
        def _(act):
            def square_root(k, out_ap, in_ap):
                act.wait_ge(s_sq, k)
                nc.scalar.activation(out_ap, in_ap, ACT.Sqrt).then_inc(s_rt, 1)

            square_root(1, stat[:, 2, :], stat[:, 1, :])
            square_root(2, stat[:, 2, :], stat[:, 1, :])
            square_root(3, stat[:, 2, :], stat[:, 1, :])

            def hidden0(s, i2):
                act.wait_ge(s_xt[0], i2 + 1)
                nc.scalar.activation(xt[:, :, :], p_xt[:, 0:4 * EP].rearrange("p (q e) -> p q e", q=4),
                                     ACT.Copy).then_inc(s_xts[0], 1)
                for j in range(4):
                    act.wait_ge(s_hp[0], i2 * 4 + j + 1)
                    nc.scalar.activation(hid[:, j, :], p_hid[j % 2][:, 0:4 * EP], ACT.Relu,
                                         bias=b1c_0[:, 0:1]).then_inc(s_hs[0], 1)

            def squares0(i2):
                act.wait_ge(s_ab, i2 + 1)
                nc.scalar.activation(prod[:, :, 0:2, :], ab[:, :, :, :], ACT.Square).then_inc(s_squares, 1)

            def parts0(i2, ends_of):
                act.wait_ge(s_msg, i2 + 1)
                for d in ends_of:
                    last = nc.scalar.activation(part_h[:, 0, d].rearrange("p c t -> p t c"), m[:, :, d, :], ACT.Copy)
                last.then_inc(s_p1, 1)

            def layer0(pack, ends_of):
                pack(0, 0)
                hidden0(0, 0)
                pack(0, 1)
                squares0(0)
                hidden0(1, 1)
                with act.Fori(0, PAIRS - 1) as i:
                    parts0(2 * i, ends_of)
                    pack(i + 1, 0)
                    squares0(2 * i + 1)
                    hidden0(0, 2 * i + 2)
                    parts0(2 * i + 1, ends_of)
                    pack(i + 1, 1)
                    squares0(2 * i + 2)
                    hidden0(1, 2 * i + 3)
                parts0(CHUNKS - 2, ends_of)
                squares0(CHUNKS - 1)
                parts0(CHUNKS - 1, ends_of)

            def hidden2(step):
                for q in range(H):
                    act.wait_ge(s_node, step[("hidden", q)])
                    nc.scalar.activation(feat[0:H2, 2, :], p_b[0:H2, 0:LO], ACT.Relu,
                                         bias=b1c_2[:, 0:1]).then_inc(s_feat, 1)

            def layer3():
                with act.Fori(0, PAIRS) as i:
                    for s in range(2):
                        act.wait_ge(s_xt[3], 2 * i + s + 3)
                        nc.scalar.activation(xt[:, 0:2, :], p_xt[:, 0:2 * EP].rearrange("p (u e) -> p u e", u=2),
                                             ACT.Copy).then_inc(s_xts[3], 1)
                        for j in range(4):
                            act.wait_ge(s_hp[3], (2 * i + s) * 4 + j + 1)
                            nc.scalar.activation(hid[:, j, :], p_hid[j % 2][:, 0:4 * EP], ACT.Relu,
                                                 bias=b1c_3[:, 0:1]).then_inc(s_hs[3], 1)

            def any_order():
                def pack(i, s):
                    act.wait_ge(s_gat[0][s], (i + 1) * (2 * CT * 16))
                    nc.scalar.activation(packed[:, s, :, :, :],
                                         gat[:, s, :, :].rearrange("p t (d f) -> p t d f", d=2)[:, :, :, 0:C],
                                         ACT.Copy).then_inc(s_packed, 1)

                layer0(pack, (0, 1))
                square_root(4, stat[:, 2, :], stat[:, 1, :])
                square_root(5, stat[:, 2, :], stat[:, 1, :])
                hidden2(any_step)
                square_root(6, stat[:, 2, :], stat[:, 1, :])
                layer3()

            def sorted_order():
                def pack(i, s):
                    act.wait_ge(s_gat[0][s], (i + 1) * (CT * 16))
                    nc.scalar.activation(packed[:, s, :, 0, :], gat[:, s, :, 0:C], ACT.Copy)
                    nc.scalar.activation(rs[:, s, :], gat[:, s, :, C], ACT.Copy).then_inc(s_gfree[0], 1)
                    nc.scalar.activation(packed[:, s, :, 1, :], wide[:, bass.ds(i * (2 * CT) + s * CT, CT), :],
                                         ACT.Copy).then_inc(s_packed, 1)

                act.wait_ge(s_xd, 1)
                layer0(pack, (0,))
                square_root(4, stat[:, 2, :], stat[:, 1, :])
                square_root(5, stat[:, 2, :], stat[:, 1, :])
                act.sem_inc(s_gfree[2], 2)
                with act.Fori(0, PAIRS) as i:
                    for s in range(2):
                        act.wait_ge(s_gat[2][s], (i + 1) * (CT * 16))
                        nc.scalar.activation(mt[:, :, s, :], gat[:, s, :, 0:C], ACT.Copy).then_inc(s_gfree[2], 1)
                        act.wait_ge(s_gfree[2], 2 * i + s + 3)
                        nc.scalar.activation(wide[:, bass.ds(i * (2 * CT) + s * CT, CT), :], mt[:, :, s, :],
                                             ACT.Copy).then_inc(s_placed, 1)
                hidden2(sorted_step)
                square_root(6, stat[:, 2, :], stat[:, 1, :])
                layer3()

            act.wait_ge(s_flag, 1)
            is_sorted = act.value_load(flag[0:1, 0:1], min_val=0, max_val=1)
            with act.If(is_sorted):
                sorted_order()
            with act.Else():
                any_order()

        @block.vector
        def _(dve):
            step = {}
            v = nc.vector
            c = Chain(dve, s_dve)

            v.memset(nx[:, FULL, :], 0.0)
            v.memset(nxt[:, :], NP * G)
            v.memset(zero_rows, 0.0)
            v.memset(w1_0[:, :, :], 0.0)
            v.memset(w2_0[:, :], 0.0)
            v.memset(w1z_3[:, :, :], 0.0)
            v.memset(rows0[:, :, C:R0], 0.0)
            v.memset(zeros[:, :], 0.0)
            v.memset(rows3[:, :, :, :], 0.0).then_inc(s_zero, 1)
            dve.wait_ge(s_zero, 1)

            dve.wait_ge(s_in, 80)
            dve.wait_ge(s_const, 8)
            c.link(v.tensor_copy(iota_lo[:, :], iota_lo_i[:, :]))
            c.link(v.tensor_copy(n_f[:, :, :], ends[:, :, :]))
            c.link(v.tensor_scalar(t_f[:, :, :], n_f[:, :, :], -(NP - 1) / 2.0, 1.0 / NP, ALU.add, ALU.mult))
            c.link(v.tensor_scalar(t_f[:, :, :], t_f[:, :, :], MAGIC, None, ALU.add))
            c.link(v.tensor_scalar(t_f[:, :, :], t_f[:, :, :], -MAGIC, None, ALU.add))
            v.tensor_copy(group[:, :, :], t_f[:, :, :])
            c.link(v.scalar_tensor_tensor(place[:, :, :], t_f[:, :, :], -float(NP), n_f[:, :, :], ALU.mult, ALU.add))
            c.link(v.tensor_scalar(t_f[:, :, :], n_f[:, :, :], -(LO - 1) / 2.0, 1.0 / LO, ALU.add, ALU.mult))
            c.link(v.tensor_scalar(t_f[:, :, :], t_f[:, :, :], MAGIC, None, ALU.add))
            c.link(v.tensor_scalar(t_f[:, :, :], t_f[:, :, :], -MAGIC, None, ALU.add))
            for d in range(2):
                v.scalar_tensor_tensor(lo[d], t_f[:, d, :], -float(LO), n_f[:, d, :], ALU.mult, ALU.add)
                v.tensor_tensor(hmask[d], t_f[:, d, :].unsqueeze(1).to_broadcast((EP, H, TILES)),
                                iota_lo[0:EP, 0:H].unsqueeze(2).to_broadcast((EP, H, TILES)), ALU.is_equal)
            v.tensor_copy(iota_kt[:, :, :], iota_kt_i.rearrange("p (k t) -> p k t", t=DC))
            v.tensor_copy(dig_l[:, 0:1], place[:, 1, TILES - 1:TILES])
            v.tensor_copy(dig_l[:, 1:2], group[:, 1, TILES - 1:TILES])
            v.memset(same[:, 0:1], 0.0)
            v.tensor_tensor(same[:, 1:TILES], n_f[:, 1, 1:TILES], n_f[:, 1, 0:TILES - 1], ALU.is_equal)
            c.link(v.tensor_copy(nxt_f[:, :], nxt[:, :]))
            v.tensor_tensor(cont[:, :], nxt_f[:, :], n_f[:, 1, TILES - 1:TILES], ALU.is_equal)
            v.tensor_tensor(viol[:, 1:2], nxt_f[:, :], n_f[:, 1, TILES - 1:TILES], ALU.is_lt)
            c.link(v.tensor_tensor(t_f[:, 1, 1:TILES], n_f[:, 1, 1:TILES], n_f[:, 1, 0:TILES - 1], ALU.is_lt))
            c.link(v.tensor_reduce(viol[:, 0:1], t_f[:, 1, 1:TILES], AX_X, ALU.add))
            c.link(v.tensor_tensor(viol_f[:, :], viol[:, 0:1], viol[:, 1:2], ALU.add))
            dve.sem_inc(s_viol, 1)

            dve.sem_inc(s_cnt_mm, 2)
            with dve.Fori(0, TILES // DC // 2) as i:
                for s in range(2):
                    dve.wait_ge(s_cnt_mm, 2 * i + s + 1)
                    a, b = digits(s)
                    at = bass.ds(i * (2 * DC) + s * DC, DC)
                    for d in range(2):
                        v.tensor_tensor(a[:, d], place[:, d, at].unsqueeze(1).to_broadcast((EP, NP, DC)),
                                        iota_kt[:, :, :], ALU.is_equal)
                        last = v.tensor_tensor(b[:, d], group[:, d, at].unsqueeze(1).to_broadcast((EP, G, DC)),
                                               iota_kt[:, 0:G, :], ALU.is_equal)
                    last.then_inc(s_cnt_oh, 1)

            roots = [0]

            def inverse_root(out_ap, in_ap):
                c.link(v.tensor_copy(stat[:, 1, :], in_ap))
                roots[0] += 1
                dve.sem_inc(s_sq, 1)
                dve.wait_ge(s_rt, roots[0])
                c.link(v.reciprocal(stat[:, 3, :], stat[:, 2, :]))
                c.link(v.tensor_tensor(stat[:, 2, :], stat[:, 3, :], stat[:, 3, :], ALU.mult))
                c.link(v.scalar_tensor_tensor(stat[:, 2, :], stat[:, 2, :], -0.5, stat[:, 1, :], ALU.mult, ALU.mult))
                c.link(v.scalar_tensor_tensor(out_ap, stat[:, 2, :], 1.5, stat[:, 3, :], ALU.add, ALU.mult))

            def over_channels(ap):
                return ap.unsqueeze(2).to_broadcast((NP, G, C))

            def layernorm_relu():
                c.link(v.tensor_reduce(stat[:, 0, :], nx[:, :, :], AX_X, ALU.add))
                c.link(v.tensor_scalar(stat[:, 0, :], stat[:, 0, :], 1.0 / C, None, ALU.mult))
                c.link(v.tensor_tensor(na[:, :, :], nx[:, :, :], over_channels(stat[:, 0, :]), ALU.subtract))
                c.link(v.tensor_tensor(nb[:, :, :], na[:, :, :], na[:, :, :], ALU.mult))
                c.link(v.tensor_reduce(stat[:, 3, :], nb[:, :, :], AX_X, ALU.add))
                c.link(v.tensor_scalar(stat[:, 3, :], stat[:, 3, :], 1.0 / C, EPS, ALU.mult, ALU.add))
                inverse_root(stat[:, 0, :], stat[:, 3, :])
                c.link(v.tensor_tensor(nb[:, :, :], na[:, :, :], over_channels(stat[:, 0, :]), ALU.mult))
                c.link(v.tensor_scalar(nh[:, :, :], nb[:, :, :], 0.0, None, ALU.max))

            def layer_sums(n, what):
                dve.wait_ge(s_done, n + 1)
                v.tensor_copy(accs[:, :], p_acc[0:NP, 0:LO]).then_inc(s_accs, 1)
                dve.wait_ge(s_node, step[what])
                return p_a[0:NP, 0:G * C].rearrange("p (b h c) -> p h b c", b=B, h=H)

            def by_high(t):
                return t[:, :, :].rearrange("p (h b) c -> p h b c", b=B)

            def sums_to(t, n, what):
                c.link(v.tensor_copy(by_high(t), layer_sums(n, what)))

            def onehots(n, chunk, s, g, og, ring, ends_of):
                dve.wait_ge(s_ohfree[n], chunk * (CT // og) + g + 1)
                for k in range(og):
                    for d in ends_of:
                        last = v.tensor_scalar(onehot_row(ring, g, d, k), iota_lo[0:EP, :],
                                               lstage[:, s, d, g * og + k:g * og + k + 1], None, ALU.is_equal)
                last.then_inc(s_oh[n], 1)

            def build_onehots(n, chunk, s, ring, ends_of):
                for g in range(CT // OG):
                    onehots(n, chunk, s, g, OG, ring, ends_of)

            def stage_low(i, s, ends_of):
                for d in ends_of:
                    last = v.tensor_scalar(lstage[:, s, d, :], lo[d][:, bass.ds(i * (2 * CT) + s * CT, CT)],
                                           0.0, None, ALU.add)
                return last

            def weigh(out2, part, i, s, d):
                mask = hmask[d][:, :, bass.ds(i * (2 * CT) + s * CT, CT)]
                return v.tensor_tensor(out2.rearrange("p (h c) t -> p h c t", h=H),
                                       part.unsqueeze(1).to_broadcast((EP, H, C, CT)),
                                       mask.unsqueeze(2).to_broadcast((EP, H, C, CT)), ALU.mult)

            def split3(link, msg):
                parts = [part_b[:, q].rearrange("p c t -> p t c") for q in range(3)]
                link(v.tensor_copy(parts[0], msg))
                link(v.tensor_tensor(mt[:, :, 0, :], msg, parts[0], ALU.subtract))
                link(v.tensor_copy(parts[1], mt[:, :, 0, :]))
                link(v.tensor_tensor(parts[2], mt[:, :, 0, :], parts[1], ALU.subtract))

            layernorm_relu()
            dve.wait_ge(s_node, node_step["degrees"])
            c.link(v.tensor_copy(degs[:, :, :], p_a[0:NP, 0:2 * G].rearrange("p (d g) -> p d g", d=2)))
            dve.sem_inc(s_deg, 1)
            c.link(v.tensor_tensor(rdeg[:, :], degs[:, 0, :], degs[:, 1, :], ALU.add))
            c.link(v.tensor_scalar(rdeg[:, :], rdeg[:, :], EPS, None, ALU.max))
            inverse_root(rdeg[:, :], rdeg[:, :])
            c.link(v.tensor_scalar(dis[:, :], degs[:, 1, :], 1.0, None, ALU.add))
            inverse_root(dis[:, :], dis[:, :])
            v.tensor_scalar(rows0[:, :, C], rdeg[:, :], SCALE16, None, ALU.mult)
            v.tensor_copy(rows0[:, :, 0:C], nh[:, :, :]).then_inc(s_rows, 1)

            dve.wait_ge(s_node, node_step["unsorted"])
            v.tensor_scalar(flag[:, :], p_c[0:1, 0:1], 0.5, None, ALU.is_lt).then_inc(s_flag, 1)

            def nodes0():
                c.link(v.tensor_tensor(nb[:, :, :], na[:, :, :], over_channels(rdeg[:, :]), ALU.mult))
                c.link(v.scalar_tensor_tensor(na[:, :, :], nb[:, :, :], 1.0 / SCALE16, nh[:, :, :], ALU.mult, ALU.add))
                c.link(v.scalar_tensor_tensor(nx[:, :, :], na[:, :, :], 0.0, nx[:, :, :], ALU.max, ALU.add))

            def nodes1():
                c.link(v.tensor_tensor(nb[:, :, :], na[:, :, :], nx[:, :, :], ALU.add))
                c.link(v.tensor_scalar(na[:, :, :], nh[:, :, :], -0.2, 1.0, ALU.mult, ALU.add))
                c.link(v.tensor_tensor(ncc[:, :, :], na[:, :, :], nh[:, :, :], ALU.mult))
                c.link(v.scalar_tensor_tensor(na[:, :, :], nh[:, :, :], -1.0, ncc[:, :, :], ALU.add, ALU.mult))
                c.link(v.scalar_tensor_tensor(nx[:, :, :], na[:, :, :], 0.1, nb[:, :, :], ALU.add, ALU.add))

            def nodes2(scale):
                c.link(v.scalar_tensor_tensor(nb[:, :, :], na[:, :, :], scale, ncc[:, :, :], ALU.mult, ALU.add))
                c.link(v.tensor_tensor(na[:, :, :], nb[:, :, :], over_channels(dis[:, :]), ALU.mult))
                dve.sem_inc(s_feat, 1)
                for q in range(H):
                    dve.wait_ge(s_node, step[("turned", q)])
                    v.tensor_copy(feat[0:C, 0, :], p_xt[0:C, 0:LO]).then_inc(s_feat, 1)
                    dve.wait_ge(s_node, step[("features", q)])
                    v.tensor_copy(feat[0:PC, 1, :], p_a[0:PC, 0:LO]).then_inc(s_feat, 1)
                dve.wait_ge(s_node, step[("update", H - 1)])
                c.link(v.tensor_tensor(nb[:, :, :], p_c[0:NP, 0:G * C].rearrange("p (g c) -> p g c", g=G),
                                       b2r_2[:, :].unsqueeze(1).to_broadcast((NP, G, C)), ALU.add))
                c.link(v.tensor_tensor(na[:, :, :], nb[:, :, :], nh[:, :, :], ALU.add))
                c.link(v.tensor_tensor(nx[:, :, :], nx[:, :, :], na[:, :, :], ALU.add))

            def rows_3():
                layernorm_relu()
                dve.sem_inc(s_feat, 1)
                for q in range(H):
                    dve.wait_ge(s_node, step[("turned3", q)])
                    v.tensor_copy(feat[0:C, 0, :], p_xt[0:C, 0:LO]).then_inc(s_feat, 1)
                    dve.wait_ge(s_node, step[("rooted", q)])
                    both = p_a[0:NP, 0:B * 2 * C].rearrange("p (b r c) -> p b r c", b=B, r=2)
                    v.tensor_copy(rows3[:, q * B:(q + 1) * B, 1, :], both[:, :, 0, :])
                    v.tensor_copy(ncc[:, q * B:(q + 1) * B, :], both[:, :, 1, :]).then_inc(s_feat, 1)
                v.tensor_copy(rows3[:, :, 0, :], nh[:, :, :]).then_inc(s_rows, 1)

            def nodes3():
                c.link(v.tensor_tensor(nb[:, :, :], na[:, :, :], ncc[:, :, :], ALU.add))
                c.link(v.tensor_tensor(nx[:, :, :], nx[:, :, :], nb[:, :, :], ALU.add))
                dve.sem_inc(s_rows, 1)

            def messages0(link, s, chunk, xs, xd, rs, rd, to_dst, between=lambda g: None):
                dve.wait_ge(s_mlp[0], chunk + 1)
                link(v.tensor_tensor(ab[:, :, :, :], p_ab[s][0:EP, :].rearrange("p (t d c) -> p t d c", t=CT, d=2),
                                     b2r_0[:, :, :].unsqueeze(1).to_broadcast((EP, CT, 2, C)), ALU.add))
                dve.sem_inc(s_mfree[0], 1)
                dve.sem_inc(s_ab, 1)
                a, b = ab[:, :, 0, :], ab[:, :, 1, :]
                v.tensor_tensor(prod[:, :, 2, :], a, xs, ALU.mult)
                v.tensor_tensor(prod[:, :, 3, :], b, xd, ALU.mult)
                v.tensor_tensor(prod[:, :, 4, :], a, xd, ALU.mult)
                v.tensor_tensor(prod[:, :, 5, :], b, xs, ALU.mult)
                link(v.tensor_tensor(prod[:, :, 6, :], a, b, ALU.mult))
                between(0)
                dve.wait_ge(s_squares, chunk + 1)
                link(v.tensor_reduce(dots[:, :, :], prod[:, :, :, :], AX_X, ALU.add))
                between(1)
                link(v.tensor_scalar(inv[:, :, :], dots[:, :, 0:2], 1e-24, 0.5, ALU.max, ALU.mult))
                link(v.reciprocal(inv[:, :, :], inv[:, :, :]))
                link(v.tensor_tensor(co[:, :, :], inv[:, :, :], dots[:, :, 2:4], ALU.mult))
                link(v.tensor_tensor(cx[:, :, :], co[:, :, :], dots[:, :, 6:7].to_broadcast((EP, CT, 2)), ALU.mult))
                v.tensor_tensor(ga[:, :, 0], dots[:, :, 4], cx[:, :, 1], ALU.subtract)
                link(v.tensor_tensor(ga[:, :, 1], dots[:, :, 5], cx[:, :, 0], ALU.subtract))
                link(v.tensor_tensor(ga[:, :, :], ga[:, :, :], inv[:, :, :], ALU.mult))
                between(2)
                link(v.tensor_tensor(mt[:, :, :, :], ab[:, :, :, :],
                                     co[:, :, :].unsqueeze(3).to_broadcast((EP, CT, 2, C)), ALU.mult))
                v.tensor_tensor(m[:, :, 0, :], xd, mt[:, :, 1, :], ALU.subtract)
                link(v.tensor_tensor(m[:, :, 1, :], xs, mt[:, :, 0, :], ALU.subtract))
                link(v.tensor_tensor(mt[:, :, :, :], ab[:, :, :, :],
                                     ga[:, :, :].unsqueeze(3).to_broadcast((EP, CT, 2, C)), ALU.mult))
                link(v.tensor_tensor(m[:, :, :, :], m[:, :, :, :], mt[:, :, :, :], ALU.subtract))
                v.tensor_tensor(m[:, :, 0, :], m[:, :, 0, :], rd, ALU.mult)
                link(v.tensor_tensor(to_dst, m[:, :, 1, :], rs, ALU.mult))
                dve.sem_inc(s_msg, 1)
                between(3)

            def messages1(link, i, s, xd):
                xs = gat[:, s, :, 0:C]
                link(v.tensor_scalar(mt[:, :, 0, :], xs, 0.9, 5.0, ALU.mult, ALU.add))
                link(v.scalar_tensor_tensor(mt[:, :, 1, :], xd, 0.1, mt[:, :, 0, :], ALU.mult, ALU.add))
                v.reciprocal(mt[:, :, 0, :], mt[:, :, 1, :])
                link(v.tensor_tensor(m[:, :, 0, :], xs, xd, ALU.mult))
                dve.sem_inc(s_gfree[1], 1)
                link(v.tensor_tensor(m[:, :, 1, :], m[:, :, 0, :], mt[:, :, 0, :], ALU.mult))
                link(v.tensor_tensor(m[:, :, 0, :], m[:, :, 1, :],
                                     ew[:, bass.ds(i * (2 * CT) + s * CT, CT)].unsqueeze(2)
                                     .to_broadcast((EP, CT, C)), ALU.mult))

            def use_weights(link, s, chunk, j, banks):
                dve.wait_ge(s_mlp[3], chunk * HALF + j + 1)
                rows = gat[:, s, :, :].rearrange("p (u j) f -> p j u f", u=2)[:, j, :, 0:C]
                link(v.tensor_tensor(pr[:, :, :, :], p_w[j % banks][0:EP, :].rearrange("p (u i o) -> p u i o", u=2, i=C),
                                     rows.unsqueeze(3).to_broadcast((EP, 2, C, C)), ALU.mult))
                dve.sem_inc(s_mfree[3], 1)
                link(v.tensor_reduce(m[:, :, 0, :].rearrange("p (u j) c -> p j u c", u=2)[:, j],
                                     pr[:, :, :, :].rearrange("p u i o -> p u o i"), AX_X, ALU.add))

            def any_order():
                dve.wait_ge(s_w, 16 * W_LOADS)
                dve.sem_inc(s_gfree[0], 2)
                dve.sem_inc(s_ohfree[0], 2)
                dve.sem_inc(s_sfree[0], 2)
                dve.sem_inc(s_mfree[0], 2)
                STEPS0 = 17
                with dve.Fori(0, PAIRS) as i:
                    c0 = Chain(dve, s_chain[0], i * (2 * STEPS0))
                    for s in range(2):
                        dve.wait_ge(s_gat[0][s], (i + 1) * (2 * CT * 16))
                        messages0(c0.link, s, 2 * i + s, gat[:, s, :, 0:C], gat[:, s, :, R0:R0 + C],
                                  gat[:, s, :, C:C + 1].to_broadcast((EP, CT, C)),
                                  gat[:, s, :, R0 + C:R0 + C + 1].to_broadcast((EP, CT, C)), m[:, :, 1, :])
                        dve.sem_inc(s_gfree[0], 1)
                        dve.wait_ge(s_p1, 2 * i + s + 1)
                        c0.link(v.tensor_tensor(part_h[:, 1].rearrange("p d c t -> p t d c"), m[:, :, :, :],
                                                part_h[:, 0].rearrange("p d c t -> p t d c"), ALU.subtract))
                        dve.wait_ge(s_sfree[0], 2 * i + s + 1)
                        c0.link(stage_low(i, s, (0, 1)))
                        for d in range(2):
                            for q in range(2):
                                last = weigh(stat_h[:, s, 2 * d + q], part_h[:, q, d], i, s, d)
                        c0.link(last)
                        dve.sem_inc(s_stat[0], 1)
                        build_onehots(0, 2 * i + s, s, 2, (0, 1))
                    assert c0.n == 2 * STEPS0, c0.n

                sums_to(na, 0, "sums0")
                nodes0()

                layernorm_relu()
                dve.sem_inc(s_rows, 1)
                dve.sem_inc(s_gfree[1], 2)
                dve.sem_inc(s_ohfree[1], 4)
                dve.sem_inc(s_sfree[1], 2)
                STEPS1 = 11
                with dve.Fori(0, PAIRS) as i:
                    c1 = Chain(dve, s_chain[1], i * (2 * STEPS1))
                    for s in range(2):
                        dve.wait_ge(s_gat[1][s], (i + 1) * (2 * CT * 16))
                        messages1(c1.link, i, s, gat[:, s, :, R0:R0 + C])
                        split3(c1.link, m[:, :, 0, :])
                        dve.wait_ge(s_sfree[1], 2 * i + s + 1)
                        c1.link(stage_low(i, s, (0,)))
                        for q in range(3):
                            last = weigh(stat_m[:, s, q], part_b[:, q], i, s, 0)
                        c1.link(last)
                        dve.sem_inc(s_stat[1], 1)
                        build_onehots(1, 2 * i + s, s, 4, (0,))
                    assert c1.n == 2 * STEPS1, c1.n

                sums_to(na, 1, "sums1")
                nodes1()

                layernorm_relu()
                c.link(v.tensor_tensor(ncc[:, :, :], nh[:, :, :], over_channels(dis[:, :]), ALU.mult))
                c.link(v.tensor_scalar(rows2[:, :, 0, :], ncc[:, :, :], SCALE16, None, ALU.mult))
                c.link(v.scalar_tensor_tensor(rows2[:, :, 1, :], ncc[:, :, :], SCALE16, rows2[:, :, 0, :],
                                              ALU.mult, ALU.subtract))
                dve.sem_inc(s_rows, 1)
                dve.sem_inc(s_gfree[2], 2)
                dve.sem_inc(s_ohfree[2], 4)
                dve.sem_inc(s_sfree[2], 2)
                STEPS2 = 2
                with dve.Fori(0, PAIRS) as i:
                    c2 = Chain(dve, s_chain[2], i * (2 * STEPS2))
                    for s in range(2):
                        dve.wait_ge(s_gat[2][s], (i + 1) * (CT * 16))
                        dve.wait_ge(s_sfree[2], 2 * i + s + 1)
                        c2.link(stage_low(i, s, (1,)))
                        halves = gat[:, s, :, 0:C].bitcast(F16)
                        for q in range(2):
                            last = weigh(stat_h[:, s, q], halves[:, :, q * C:(q + 1) * C].rearrange("p t c -> p c t"), i, s, 1)
                        c2.link(last)
                        dve.sem_inc(s_stat[2], 1)
                        dve.sem_inc(s_gfree[2], 1)
                        build_onehots(2, 2 * i + s, s, 4, (1,))
                    assert c2.n == 2 * STEPS2, c2.n

                sums_to(na, 2, "sums2")
                nodes2(1.0 / SCALE16)

                rows_3()
                dve.sem_inc(s_gfree[3], 2)
                dve.sem_inc(s_ohfree[3], 2)
                dve.sem_inc(s_sfree[3], 2)
                dve.sem_inc(s_mfree[3], 2)
                STEPS3 = 2 * HALF + 7

                def weigh_messages(link, i, s, chunk):
                    link(v.tensor_tensor(m[:, :, 1, :], m[:, :, 0, :], gat[:, s, :, C:2 * C], ALU.add))
                    dve.sem_inc(s_gfree[3], 1)
                    split3(link, m[:, :, 1, :])
                    dve.wait_ge(s_sfree[3], chunk + 1)
                    link(stage_low(i, s, (1,)))
                    for q in range(3):
                        last = weigh(stat_m[:, s, q], part_b[:, q], i, s, 1)
                    link(last)
                    dve.sem_inc(s_stat[3], 1)

                def finish_and_begin(link, i, s, chunk, i_next):
                    weigh_messages(link, i, s, chunk)
                    dve.wait_ge(s_gat[3][1 - s], (i_next + 1) * (CT * 16))
                    for g in range(HALF):
                        onehots(3, chunk, s, g, 2, 2, (1,))
                        use_weights(link, 1 - s, chunk + 1, g, 2)

                dve.wait_ge(s_gat[3][0], CT * 16)
                for j in range(HALF):
                    use_weights(c.link, 0, 0, j, 2)
                with dve.Fori(0, PAIRS - 1) as i:
                    c3 = Chain(dve, s_chain[3], i * (2 * STEPS3))
                    finish_and_begin(c3.link, i, 0, 2 * i, i)
                    finish_and_begin(c3.link, i, 1, 2 * i + 1, i + 1)
                    assert c3.n == 2 * STEPS3, c3.n
                finish_and_begin(c.link, PAIRS - 1, 0, CHUNKS - 2, PAIRS - 1)
                weigh_messages(c.link, PAIRS - 1, 1, CHUNKS - 1)
                for g in range(HALF):
                    onehots(3, CHUNKS - 1, 1, g, 2, 2, (1,))

                sums_to(na, 3, "sums3")
                nodes3()

            def sorted_order():
                dve.wait_ge(s_node, step["within"])
                c.link(v.tensor_copy(pos[:, 0, :], p_b[0:NP, G:2 * G]))
                c.link(v.tensor_tensor_scan(pos[:, 1, :], ones[0:NP, 0:G], pos[:, 0, :], 0.0, ALU.mult, ALU.add))
                c.link(v.tensor_tensor(pos[:, 1, :], pos[:, 1, :], pos[:, 0, :], ALU.subtract))
                c.link(v.tensor_tensor(pos[:, 0, :], p_b[0:NP, 0:G], pos[:, 1, :], ALU.add))
                c.link(v.tensor_tensor(pos[:, 1, :], pos[:, 0, :], degs[:, 1, :], ALU.subtract))
                v.tensor_scalar(has[:, :], degs[:, 1, :], 0.5, None, ALU.is_gt)
                c.link(v.tensor_copy(spare[:, :], spare_i[:, :]))
                v.tensor_scalar(last_edge[:, :], pos[:, 0, :], -1.0, 0.0, ALU.add, ALU.max)
                c.link(v.tensor_tensor(pos[:, 1, :], pos[:, 1, :], spare[:, :], ALU.subtract))
                c.link(v.tensor_tensor(pos[:, 1, :], pos[:, 1, :], has[:, :], ALU.mult))
                c.link(v.tensor_tensor(first_edge[:, :], pos[:, 1, :], spare[:, :], ALU.add))
                v.tensor_tensor(oh_place[:, :], dig_l[:, 0:1].to_broadcast((EP, NP)), iota_lo[0:EP, 0:NP], ALU.is_equal)
                c.link(v.tensor_tensor(oh_group[:, :], dig_l[:, 1:2].to_broadcast((EP, G)), iota_lo[0:EP, 0:G],
                                       ALU.is_equal))
                dve.sem_inc(s_pos, 1)

                def spread_rows(n, channels):
                    for b in range(BLOCKS):
                        use = n * BLOCKS + b
                        dve.wait_ge(s_z[use % 2], 16 * (use // 2 + 1))
                        if b == 0:
                            dve.wait_ge(s_first, 16 * (n + 1))
                            c.link(v.tensor_copy(zb[0:EP, use % 2, 0, :], first_rows[:, :]))
                        at = slice(b * BT, (b + 1) * BT)
                        for f in range(channels):
                            before = max(b * BT - 1, 0)
                            if f < C:
                                to, start = wide[:, at, f], wide[:, before, f:f + 1]
                            else:
                                to, start = rd[:, at], rd[:, before:before + 1]
                            last = v.tensor_tensor_scan(to, same[:, at], zb[0:EP, use % 2, :, f],
                                                        start if b else 0.0, ALU.mult, ALU.add)
                        c.link(last)
                        dve.sem_inc(s_zfree, 1)

                def scan_block(link, o):
                    at = bass.ds(o * BT, BT)
                    for f in range(C):
                        last = v.tensor_tensor_scan(wide[:, at, f], same[:, at], wide[:, at, f],
                                                    tail[:, f:f + 1], ALU.mult, ALU.add)
                    link(last)
                    link(v.tensor_scalar(tail[:, :], wide[:, bass.ds(o * BT + BT - 1, 1), :].rearrange("p a c -> p (a c)"),
                                         0.0, None, ALU.add))
                    dve.sem_inc(s_blk, 1)

                def carried_sums(k, what):
                    c.link(v.tensor_scalar(tail[:, :], tail[:, :], cont[:, 0:1], None, ALU.mult))
                    v.tensor_tensor(crhs[:, :, :], oh_group[:, :].unsqueeze(2).to_broadcast((EP, G, C)),
                                    tail[:, :].unsqueeze(1).to_broadcast((EP, G, C)), ALU.mult).then_inc(s_crhs, 1)
                    dve.wait_ge(s_last, 16 * G * (k + 1))
                    c.link(v.tensor_tensor(na[:, :, :], last_rows[:, :, :], over_channels(has[:, :]), ALU.mult))
                    dve.wait_ge(s_node, step[what])
                    c.link(v.tensor_tensor(nb[:, :, :], na[:, :, :],
                                           p_b[0:NP, 0:G * C].rearrange("p (g c) -> p g c", g=G), ALU.add))

                spread_rows(0, C + 1)
                dve.sem_inc(s_xd, 1)
                dve.wait_ge(s_w, 16 * W_LOADS)
                c.link(v.memset(tail[:, :], 0.0))
                dve.sem_inc(s_gfree[0], 2)
                dve.sem_inc(s_ohfree[0], 4)
                dve.sem_inc(s_sfree[0], 2)
                dve.sem_inc(s_mfree[0], 2)
                F0 = BP * 2 * 17 + 2
                with dve.Fori(0, BLOCKS) as o:
                    with dve.Fori(0, BP) as k:
                        i = o * BP + k
                        c0 = Chain(dve, s_chain[0], o * F0 + k * 34)
                        for s in range(2):
                            at = bass.ds(i * (2 * CT) + s * CT, CT)
                            c0.link(stage_low(i, s, (0,)))
                            messages0(c0.link, s, 2 * i + s, packed[:, s, :, 0, :], packed[:, s, :, 1, :],
                                      rs[:, s, :].unsqueeze(2).to_broadcast((EP, CT, C)),
                                      rd[:, at].unsqueeze(2).to_broadcast((EP, CT, C)), wide[:, at, :],
                                      between=lambda g: onehots(0, 2 * i + s, s, g, OG, 4, (0,)))
                            dve.wait_ge(s_p1, 2 * i + s + 1)
                            c0.link(v.tensor_tensor(part_h[:, 1, 0].rearrange("p c t -> p t c"), m[:, :, 0, :],
                                                    part_h[:, 0, 0].rearrange("p c t -> p t c"), ALU.subtract))
                            dve.wait_ge(s_sfree[0], 2 * i + s + 1)
                            for q in range(2):
                                last = weigh(stat_h[:, s, q], part_h[:, q, 0], i, s, 0)
                            c0.link(last)
                            dve.sem_inc(s_stat[0], 1)
                        assert c0.n == 34, c0.n
                    cb = Chain(dve, s_chain[0], o * F0 + BP * 34)
                    scan_block(cb.link, o)
                    assert BP * 34 + cb.n == F0
                carried_sums(0, "carry0")
                c.link(v.tensor_tensor(by_high(na), layer_sums(0, "sums0"), by_high(nb), ALU.add))
                nodes0()

                layernorm_relu()
                c.link(v.tensor_copy(rows0[:, :, 0:C], nh[:, :, :]))
                dve.sem_inc(s_rows, 1)
                spread_rows(1, C)
                dve.sem_inc(s_gfree[1], 2)
                dve.sem_inc(s_ohfree[1], 4)
                dve.sem_inc(s_sfree[1], 2)
                STEPS1 = 11
                with dve.Fori(0, PAIRS) as i:
                    c1 = Chain(dve, s_chain[1], i * (2 * STEPS1))
                    for s in range(2):
                        dve.wait_ge(s_gat[1][s], (i + 1) * (CT * 16))
                        c1.link(stage_low(i, s, (0,)))
                        messages1(c1.link, i, s, wide[:, bass.ds(i * (2 * CT) + s * CT, CT), :])
                        build_onehots(1, 2 * i + s, s, 4, (0,))
                        split3(c1.link, m[:, :, 0, :])
                        dve.wait_ge(s_sfree[1], 2 * i + s + 1)
                        for q in range(3):
                            last = weigh(stat_m[:, s, q], part_b[:, q], i, s, 0)
                        c1.link(last)
                        dve.sem_inc(s_stat[1], 1)
                    assert c1.n == 2 * STEPS1, c1.n
                sums_to(na, 1, "sums1")
                nodes1()

                layernorm_relu()
                c.link(v.tensor_tensor(ncc[:, :, :], nh[:, :, :], over_channels(dis[:, :]), ALU.mult))
                c.link(v.memset(tail[:, :], 0.0))
                dve.sem_inc(s_rows, 1)
                with dve.Fori(0, BLOCKS) as o:
                    dve.wait_ge(s_placed, (o + 1) * (BT // CT))
                    cb = Chain(dve, s_chain[2], o * 2)
                    scan_block(cb.link, o)
                carried_sums(1, "carry2")
                c.link(v.tensor_copy(na[:, :, :], nb[:, :, :]))
                nodes2(1.0)

                rows_3()
                c.link(v.memset(tail[:, :], 0.0))
                dve.sem_inc(s_gfree[3], 2)
                dve.sem_inc(s_mfree[3], 4)
                F3 = BP * 2 * (2 * HALF + 1) + 2
                with dve.Fori(0, BLOCKS) as o:
                    with dve.Fori(0, BP) as k:
                        i = o * BP + k
                        c3 = Chain(dve, s_chain[3], o * F3 + k * (2 * (2 * HALF + 1)))
                        for s in range(2):
                            dve.wait_ge(s_gat[3][s], (i + 1) * (CT * 16))
                            for j in range(HALF):
                                use_weights(c3.link, s, 2 * i + s, j, 4)
                            at = bass.ds(i * (2 * CT) + s * CT, CT)
                            c3.link(v.tensor_tensor(wide[:, at, :], m[:, :, 0, :], gat[:, s, :, C:2 * C], ALU.add))
                            dve.sem_inc(s_gfree[3], 1)
                    cb = Chain(dve, s_chain[3], o * F3 + F3 - 2)
                    scan_block(cb.link, o)
                carried_sums(2, "carry3")
                c.link(v.tensor_copy(na[:, :, :], nb[:, :, :]))
                nodes3()

            steps_before, roots_before = c.n, roots[0]
            dve.wait_ge(s_flag, 1)
            is_sorted = dve.value_load(flag[0:1, 0:1], min_val=0, max_val=1)
            with dve.If(is_sorted):
                step = sorted_step
                sorted_order()
            c.n, roots[0] = steps_before, roots_before
            with dve.Else():
                step = any_step
                any_order()

        @block.tensor
        def _(pe):
            te = nc.tensor
            acc = p_acc[0:NP, 0:LO]

            def clear(last=False):
                return te.matmul(acc, zeros[0:1, 0:NP], zeros[0:1, :], start=not last, stop=last,
                                 skip_group_check=True)

            def turn_sums(n):
                pe.wait_ge(s_accs, n + 1)
                for b in range(B):
                    last = te.transpose(p_a[0:NP, b * NP:(b + 1) * NP], accs[:, b * NP:(b + 1) * NP],
                                        identity[0:NP, 0:NP])
                last.then_inc(s_node, 1)

            def scatter_group(n, chunk, s, g, og, ring, terms, masks):
                pe.wait_ge(s_oh[n], chunk * (CT // og) + g + 1)
                for k in range(og):
                    for d, q in terms:
                        last = te.matmul(acc, masks[:, s, q, :, g * og + k], onehot_row(ring, g, d, k),
                                         start=False, stop=False, skip_group_check=True)
                last.then_inc(s_ohfree[n], 1)

            def masks_used(n):
                te.matmul(acc, zeros[0:1, 0:NP], zeros[0:1, :], start=False, stop=False,
                          skip_group_check=True).then_inc(s_sfree[n], 1)

            def scatter(n, chunk, s, ring, terms, masks):
                pe.wait_ge(s_stat[n], chunk + 1)
                for g in range(CT // OG):
                    scatter_group(n, chunk, s, g, OG, ring, terms, masks)
                masks_used(n)

            pe.wait_ge(s_zero, 1)
            te.matmul(p_a[0:NP, 0:2 * G], zeros[0:1, 0:NP], zeros[0:1, 0:2 * G], start=True, stop=False,
                      skip_group_check=True)
            with pe.Fori(0, TILES // DC // 2) as i:
                for s in range(2):
                    pe.wait_ge(s_cnt_oh, 2 * i + s + 1)
                    a, b = digits(s)
                    for d in range(2):
                        for t in range(DC):
                            last = te.matmul(p_a[0:NP, d * G:(d + 1) * G], a[:, d, :, t], b[:, d, :, t],
                                             start=False, stop=False, skip_group_check=True)
                    last.then_inc(s_cnt_mm, 1)
            te.matmul(p_a[0:NP, 0:2 * G], zeros[0:1, 0:NP], zeros[0:1, 0:2 * G], start=False, stop=True,
                      skip_group_check=True).then_inc(s_node, 1)

            pe.wait_ge(s_viol, 1)
            pe.wait_ge(s_const, 8)
            te.matmul(p_c[0:1, 0:1], viol_f[:, :], ones[0:EP, 0:1], start=True, stop=True).then_inc(s_node, 1)
            pe.wait_ge(s_deg, 1)
            te.matmul(p_b[0:NP, 0:G], upper[:, :], degs[:, 1, :], start=True, stop=True)
            te.matmul(p_b[0:NP, G:2 * G], ones[0:NP, :], degs[:, 1, :], start=True, stop=True).then_inc(s_node, 1)

            clear()
            pe.wait_ge(s_w, 16 * W_LOADS)
            pe.wait_ge(s_const, 2)

            def mlp0(s, i2):
                pe.wait_ge(s_packed, i2 + 1)
                for q in range(4):
                    last = te.transpose(p_xt[:, q * EP:(q + 1) * EP],
                                        packed[:, s, 4 * q:4 * q + 4, :, :].rearrange("p t d c -> p (t d c)"),
                                        identity[0:EP, 0:EP])
                last.then_inc(s_xt[0], 1)
                pe.wait_ge(s_xts[0], i2 + 1)
                for j in range(4):
                    if j >= 2:
                        pe.wait_ge(s_hs[0], i2 * 4 + j - 1)
                    te.matmul(p_hid[j % 2][:, 0:4 * EP], w1_0[:, j, :],
                              xt[:, :, :].rearrange("p q e -> p (q e)"), start=True, stop=True).then_inc(s_hp[0], 1)
                pe.wait_ge(s_mfree[0], i2 + 1)
                for j in range(4):
                    pe.wait_ge(s_hs[0], i2 * 4 + j + 1)
                    for q in range(4):
                        t = 4 * q + j
                        last = te.matmul(p_ab[s][0:EP, t * 2 * C:(t + 1) * 2 * C], hid[:, j, q * EP:(q + 1) * EP],
                                         w2_0[:, :], start=True, stop=True)
                last.then_inc(s_mlp[0], 1)

            def layer0(ring, terms):
                mlp0(0, 0)
                mlp0(1, 1)
                with pe.Fori(0, PAIRS - 1) as i:
                    for s in range(2):
                        scatter(0, 2 * i + s, s, ring, terms, stat_h)
                        mlp0(s, 2 * i + s + 2)
                scatter(0, CHUNKS - 2, 0, ring, terms, stat_h)
                scatter(0, CHUNKS - 1, 1, ring, terms, stat_h)
                clear(last=True).then_inc(s_done, 1)

            def scatter_layer(n, ring, terms, masks):
                clear()
                with pe.Fori(0, PAIRS) as i:
                    for s in range(2):
                        scatter(n, 2 * i + s, s, ring, terms, masks)
                clear(last=True).then_inc(s_done, 1)
                turn_sums(n)

            def carry(k):
                pe.wait_ge(s_crhs, k + 1)
                te.matmul(p_b[0:NP, 0:G * C], oh_place[:, :], crhs[:, :, :].rearrange("p g c -> p (g c)"),
                          start=True, stop=True).then_inc(s_node, 1)

            def products2():
                copied = 1
                pe.wait_ge(s_feat, copied)
                for q in range(H):
                    for b in range(B):
                        last = te.transpose(p_xt[0:C, b * NP:(b + 1) * NP], na[:, q * B + b, :], identity[0:NP, 0:NP])
                    last.then_inc(s_node, 1)
                    copied += 1
                    pe.wait_ge(s_feat, copied)
                    te.matmul(p_a[0:PC, 0:LO], wg[:, :], feat[0:C, 0, :], start=True, stop=True).then_inc(s_node, 1)
                    copied += 1
                    pe.wait_ge(s_feat, copied)
                    te.matmul(p_b[0:H2, 0:LO], w1_2[:, :], feat[0:PC, 1, :], start=True, stop=True).then_inc(s_node, 1)
                    copied += 1
                    pe.wait_ge(s_feat, copied)
                    for b in range(B):
                        g = q * B + b
                        last = te.matmul(p_c[0:NP, g * C:(g + 1) * C], feat[0:H2, 2, b * NP:(b + 1) * NP], w2_2[:, :],
                                         start=True, stop=True)
                    last.then_inc(s_node, 1)

            def rows_3():
                copied = 1 + 3 * H
                copied += 1
                pe.wait_ge(s_feat, copied)
                for q in range(H):
                    for b in range(B):
                        last = te.transpose(p_xt[0:C, b * NP:(b + 1) * NP], nh[:, q * B + b, :], identity[0:NP, 0:NP])
                    last.then_inc(s_node, 1)
                    copied += 1
                    pe.wait_ge(s_feat, copied)
                    for b in range(B):
                        last = te.matmul(p_a[0:NP, b * 2 * C:(b + 1) * 2 * C], feat[0:C, 0, b * NP:(b + 1) * NP],
                                         zr_3[:, :, :].rearrange("i r o -> i (r o)"), start=True, stop=True)
                    last.then_inc(s_node, 1)
                    copied += 1
                    pe.wait_ge(s_feat, copied)

            def turn_attributes(i, s):
                pe.wait_ge(s_ea[s], (i + 1) * 16)
                for u in range(2):
                    last = te.transpose(p_xt[:, u * EP:(u + 1) * EP],
                                        ea[:, s, u * HALF:(u + 1) * HALF, :].rearrange("p t c -> p (t c)"),
                                        identity[0:EP, 0:EP])
                last.then_inc(s_xt[3], 1)

            def hidden_sums(jj):
                for k in range(2):
                    last = te.matmul(p_hid[jj % 2][:, k * 2 * EP:(k + 1) * 2 * EP], w1z_3[:, 2 * jj + k, :],
                                     xt[:, 0:2, :].rearrange("p u e -> p (u e)"), start=True, stop=True)
                last.then_inc(s_hp[3], 1)

            def hidden3(i, s, i2):
                turn_attributes(i, s)
                pe.wait_ge(s_xts[3], i2 + 1)
                for jj in range(4):
                    if jj >= 2:
                        pe.wait_ge(s_hs[3], i2 * 4 + jj - 1)
                    hidden_sums(jj)

            def weights3(i2, j, banks):
                pe.wait_ge(s_hs[3], i2 * 4 + j // 2 + 1)
                pe.wait_ge(s_mfree[3], i2 * HALF + j + 1)
                for u in range(2):
                    at = ((j % 2) * 2 + u) * EP
                    last = te.matmul(p_w[j % banks][0:EP, u * OO:(u + 1) * OO], hid[:, j // 2, at:at + EP],
                                     w2s_3[:, :], start=True, stop=True)
                last.then_inc(s_mlp[3], 1)

            def any_order():
                layer0(2, ((0, 0), (0, 1), (1, 2), (1, 3)))
                turn_sums(0)
                scatter_layer(1, 4, ((0, 0), (0, 1), (0, 2)), stat_m)
                scatter_layer(2, 4, ((1, 0), (1, 1)), stat_h)
                products2()
                rows_3()
                clear()

                def scatter_and_weights(chunk, s, i_next):
                    hidden3(i_next, 1 - s, chunk + 1)
                    pe.wait_ge(s_stat[3], chunk + 1)
                    for g in range(HALF):
                        scatter_group(3, chunk, s, g, 2, 2, terms3, stat_m)
                        weights3(chunk + 1, g, 2)
                    masks_used(3)

                terms3 = ((1, 0), (1, 1), (1, 2))
                pe.sem_inc(s_xt[3], 2)
                hidden3(0, 0, 0)
                for j in range(HALF):
                    weights3(0, j, 2)
                with pe.Fori(0, PAIRS - 1) as i:
                    scatter_and_weights(2 * i, 0, i)
                    scatter_and_weights(2 * i + 1, 1, i + 1)
                scatter_and_weights(CHUNKS - 2, 0, PAIRS - 1)
                pe.wait_ge(s_stat[3], CHUNKS)
                for g in range(HALF):
                    scatter_group(3, CHUNKS - 1, 1, g, 2, 2, terms3, stat_m)
                masks_used(3)
                clear(last=True).then_inc(s_done, 1)
                turn_sums(3)

            def sorted_order():
                layer0(4, ((0, 0), (0, 1)))
                carry(0)
                turn_sums(0)
                scatter_layer(1, 4, ((0, 0), (0, 1), (0, 2)), stat_m)
                carry(1)
                products2()
                rows_3()

                def chunk3(chunk, i_next, s_next):
                    turn_attributes(i_next, s_next)
                    for jj in range(4):
                        weights3(chunk, 2 * jj, 4)
                        weights3(chunk, 2 * jj + 1, 4)
                        if jj == 0:
                            pe.wait_ge(s_xts[3], chunk + 2)
                        pe.wait_ge(s_hs[3], chunk * 4 + 4 + jj - 1)
                        hidden_sums(jj)

                pe.sem_inc(s_xt[3], 2)
                hidden3(0, 0, 0)
                with pe.Fori(0, PAIRS - 1) as i:
                    chunk3(2 * i, i, 1)
                    chunk3(2 * i + 1, i + 1, 0)
                chunk3(CHUNKS - 2, PAIRS - 1, 1)
                for j in range(HALF):
                    weights3(CHUNKS - 1, j, 4)
                carry(2)

            pe.wait_ge(s_flag, 1)
            is_sorted = pe.value_load(flag[0:1, 0:1], min_val=0, max_val=1)
            with pe.If(is_sorted):
                sorted_order()
            with pe.Else():
                any_order()


W_LOADS = 1 + 4 * 3 + 2 * 3 + 5 + 8 + 4


_INS = ["x", "src", "dst", "edge_attr_16", "edge_weight", "L0_gnn_W1", "L0_gnn_b1", "L0_gnn_W2", "L0_gnn_b2",
        "L2_gnn_W_gcn", "L2_gnn_W1", "L2_gnn_b1", "L2_gnn_W2", "L2_gnn_b2",
        "L3_gnn_W1", "L3_gnn_b1", "L3_gnn_W2", "L3_gnn_b2", "L3_gnn_root"]
_TURNED = {"L0_gnn_W1", "L0_gnn_W2", "L2_gnn_W_gcn", "L2_gnn_W1", "L2_gnn_W2"}


def kernel(**inputs):
    import numpy as _np
    import concourse.bacc as _bacc
    from concourse import mybir as _mybir
    from concourse.bass_utils import run_bass_kernel_spmd as _run

    nc = _bacc.Bacc("TRN2", target_bir_lowering=False, num_devices=1)
    arrays, args = {}, []
    for name in _INS:
        a = _np.asarray(inputs[name])
        a = _np.ascontiguousarray(a.T if name in _TURNED else a)
        arrays[f"in_{name}_dram"] = a
        args.append(nc.dram_tensor(f"in_{name}_dram", a.shape, _mybir.dt.from_np(a.dtype), kind="ExternalInput").ap())
    args.append(nc.dram_tensor("out_0_dram", (N, C), F32, kind="ExternalOutput").ap())
    gnn_program(nc, *args)
    r = _run(nc, [arrays], core_ids=[0])
    return r.results[0]["out_0_dram"]
```

```python
from contextlib import ExitStack

import concourse.bass as bass
from concourse import mybir

ALU = mybir.AluOpType
ACT = mybir.ActivationFunctionType
AX_X = mybir.AxisListType.X
F32 = mybir.dt.float32
F16 = mybir.dt.float16
BF16 = mybir.dt.bfloat16
I32 = mybir.dt.int32

N = 3125
C = 16
E = 100000
EP = 125
TILES = E // EP
CT = 16
CHUNKS = TILES // CT
PAIRS = CHUNKS // 2
NP = 112
G = 28
H = 7
LO = NP * G // H
B = LO // NP
FULL = N // NP
TAIL = N - FULL * NP
R0 = 20
OG = 4
HALF = CT // 2
DC = 8
DU = 10
BT = 160
BLOCKS = TILES // BT
BP = BT // (2 * CT)
PT = {1: 4, 2: 9, 3: 3}
UNITS = {n: [(o, min(4, PT[n] - o)) for o in range(0, PT[n], 4)] for n in PT}
UN = {n: len(UNITS[n]) for n in PT}
RING = {1: 2, 2: 3, 3: 1}
DT = TILES // 8
SG = 2
SHARED = CT // OG - SG
LAG = 2
BZ = 32
MAGIC = float(3 * 2 ** 22)
SCALE16 = 8192.0
EPS = 1e-5


class Chain:

    def __init__(self, engine, sem, base=0):
        self.engine, self.sem, self.base, self.n = engine, sem, base, 0

    def mark(self, ins):
        self.n += 1
        ins.then_inc(self.sem, 1)

    def wait(self, back=0):
        self.engine.wait_ge(self.sem, self.base + self.n - back)

    def link(self, ins, meanwhile=lambda: None):
        self.mark(ins)
        meanwhile()
        self.wait()


def gnn_program(nc, x, src, dst, edge_attr, edge_weight, w1_0t, b1_0, w2_0t, b2_0,
                wg_t, w1_2t, b1_2, w2_2t, b2_2, w1_3, b1_3, w2_3, b2_3, root, out):
    H0 = b1_0.shape[0]
    H2 = b1_2.shape[0]
    PC = wg_t.shape[1]
    H3 = b1_3.shape[0]
    OO = C * C

    table0 = nc.dram_tensor("table0", (NP * G, R0), F32, kind="Internal").ap()
    table1 = nc.dram_tensor("table1", (NP * G, C), F32, kind="Internal").ap()
    table2 = nc.dram_tensor("table2", (NP * G, 2 * C), F16, kind="Internal").ap()
    table2f = nc.dram_tensor("table2f", (NP * G, C), F32, kind="Internal").ap()
    starts = nc.dram_tensor("starts", (E + NP * G, R0), F32, kind="Internal").ap()
    running = nc.dram_tensor("running", (E, C), F32, kind="Internal").ap()
    digits_t = nc.dram_tensor("digits_t", (2, TILES, EP), F16, kind="Internal").ap()
    table3 = nc.dram_tensor("table3", (NP * G, 2 * C), F32, kind="Internal").ap()

    with ExitStack() as ctx:
        def sb(name, shape, dt=F32):
            return ctx.enter_context(nc.sbuf_tensor(name, shape, dt))

        def ps(name, shape=(128, 512)):
            return ctx.enter_context(nc.psum_tensor(name, list(shape), F32))

        def sem(name):
            return ctx.enter_context(nc.semaphore(name))

        identity = sb("identity", [128, 128])
        iota_lo = sb("iota_lo", [EP, LO], F16)
        zeros = sb("zeros", [128, LO], BF16)
        w1_0 = sb("w1_0", [128, 4, 2 * H0])
        b1c_0 = sb("b1c_0", [128, 1])
        w2_0 = sb("w2_0", [128, 2 * C])
        b2r_0 = sb("b2r_0", [EP, 2, C])
        wg = sb("wg", [C, PC])
        w1_2 = sb("w1_2", [PC, H2])
        b1c_2 = sb("b1c_2", [H2, 1])
        w2_2 = sb("w2_2", [H2, C])
        b2r_2 = sb("b2r_2", [NP, C])
        w1z_3 = sb("w1z_3", [128, 8, H3])
        b1c_3 = sb("b1c_3", [H3, 1])
        w2s_3 = sb("w2s_3", [H3, OO])
        zr_3 = sb("zr_3", [C, 2, C])

        ends = sb("ends", [EP, 2, TILES], I32)
        ew = sb("ew", [EP, TILES])
        lo_s = sb("lo_s", [EP, TILES])
        hmask_s = sb("hmask_s", [EP, H, TILES], BF16)
        same = sb("same", [EP, TILES])
        nxt = sb("nxt", [EP, 1], I32)
        nxt_f = sb("nxt_f", [EP, 1])
        cont = sb("cont", [EP, 1])
        viol = sb("viol", [EP, 2])
        viol_f = sb("viol_f", [EP, 1])
        flag = sb("flag", [1, 1], I32)
        dig_l = sb("dig_l", [EP, 2])

        wide = sb("wide", [EP, TILES, C])
        flat = wide[:, :, :].rearrange("p t c -> p (t c)")
        W0 = 2 * TILES
        n_f = flat[:, 0:W0].rearrange("p (d t) -> p d t", d=2)
        t_f = flat[:, W0:2 * W0].rearrange("p (d t) -> p d t", d=2)
        group = flat[:, 2 * W0:2 * W0 + TILES].bitcast(F16).rearrange("p (d t) -> p d t", d=2)
        place = flat[:, 2 * W0 + TILES:3 * W0].bitcast(F16).rearrange("p (d t) -> p d t", d=2)
        lo_d = flat[:, 3 * W0:3 * W0 + TILES]
        hmask_d = flat[:, 4 * W0:4 * W0 + TILES * H // 2].bitcast(BF16).rearrange("p (h t) -> p h t", h=H)
        iota_kt_i = flat[:, 7 * W0:7 * W0 + NP * DC].bitcast(I32)
        zero_rows = flat[:, 8 * W0 - BZ * R0:8 * W0]
        lo = (lo_s[:, :], lo_d)
        hmask = (hmask_s[:, :, :], hmask_d)
        iota_kt = sb("iota_kt", [EP, NP, DC], F16)

        nx = sb("nx", [NP, G, C])
        nh = sb("nh", [NP, G, C])
        na = sb("na", [NP, G, C])
        nb = sb("nb", [NP, G, C])
        ncc = sb("ncc", [NP, G, C])
        stat = sb("stat", [NP, 4, G])
        degs = sb("degs", [NP, 2, G])
        rdeg = sb("rdeg", [NP, G])
        dis = sb("dis", [NP, G])
        rows0 = sb("rows0", [NP, G, R0])
        rows2 = sb("rows2", [NP, G, 2, C], F16)
        rows3 = sb("rows3", [NP, G, 2, C])
        accs = sb("accs", [NP, LO])

        rd = sb("rd", [EP, TILES])
        upper = sb("upper", [NP, NP])
        ones = sb("ones", [128, NP])
        pos = sb("pos", [NP, 2, G])
        has = sb("has", [NP, G])
        spare_i = sb("spare_i", [NP, G], I32)
        spare = sb("spare", [NP, G])
        last_edge = sb("last_edge", [NP, G], I32)
        first_edge = sb("first_edge", [NP, G], I32)
        last_rows = sb("last_rows", [NP, G, C])
        first_rows = sb("first_rows", [EP, R0])
        oh_place = sb("oh_place", [EP, NP])
        oh_group = sb("oh_group", [EP, G])
        crhs = sb("crhs", [EP, G, C])
        tail = sb("tail", [EP, C])

        place_i = sb("place_i", [NP, B], I32)
        row_lo = sb("row_lo", [NP, B])
        row_high = sb("row_high", [NP, 1])
        row_c = sb("row_c", [NP, 1])
        fold = sb("fold", [NP, C], F16)
        fold_z = sb("fold_z", [NP, 2 * C])
        tabs = sb("tabs", [NP, B, 2, H * C], F16)

        istage = sb("istage", [EP, 2, 2, CT], I32)
        gat = sb("gat", [EP, 2, CT, 2 * R0])
        lstage = sb("lstage", [EP, 2, 2, CT])
        onehot = sb("onehot", [EP, 2, 2, OG, LO], BF16)
        stat_m = sb("stat_m", [EP, 2, 4, H * C, CT], BF16)
        stat_h = stat_m[:, :, :, :, :].bitcast(F16)
        ab = sb("ab", [EP, CT, 2, C])
        prod = sb("prod", [EP, CT, 7, C])
        dots = sb("dots", [EP, CT, 7])
        inv = sb("inv", [EP, CT, 2])
        co = sb("co", [EP, CT, 2])
        cx = sb("cx", [EP, CT, 2])
        ga = sb("ga", [EP, CT, 2])
        m = sb("m", [EP, CT, 2, C])
        mt = sb("mt", [EP, CT, 2, C])
        part_h = sb("part_h", [EP, 2, 2, C, CT], F16)
        part_b = sb("part_b", [EP, 3, C, CT], BF16)
        packed = sb("packed", [EP, 2, CT, 2, C])
        rs = sb("rs", [EP, 2, CT])
        xt = sb("xt", [128, 4, EP])
        hid = sb("hid", [128, 4, 4 * EP])
        ea = sb("ea", [EP, 2, CT, C])
        pr = sb("pr", [EP, 2, C, C])
        feat = sb("feat", [TILES // 8, 8 * EP])

        p_acc = ps("p_acc")
        p_xt = ps("p_xt")
        p_pair = [ps(f"p_pair{k}", (128, 2 * 512)) for k in range(2)]
        p_a, p_b = (p_pair[0][:, k * 512:(k + 1) * 512] for k in range(2))
        p_c, p_d = (p_pair[1][:, k * 512:(k + 1) * 512] for k in range(2))
        p_e = ps("p_e")
        p_pick = ps("p_pick")
        p_hid = [p_a, p_b]
        p_ab = [p_c, p_d]
        p_w = [p_c, p_d, p_e, p_acc]

        s_in = sem("s_in")
        s_w = sem("s_w")
        s_const = sem("s_const")
        s_zero = sem("s_zero")
        s_tab = sem("s_tab")
        s_out = sem("s_out")
        s_dve = sem("s_dve")
        s_sq = sem("s_sq")
        s_rt = sem("s_rt")
        s_rows = sem("s_rows")
        s_cnt_oh = sem("s_cnt_oh")
        s_cnt_mm = sem("s_cnt_mm")
        s_acc0 = sem("s_acc0")
        s_done = sem("s_done")
        s_accs = sem("s_accs")
        s_node = sem("s_node")
        s_feat = sem("s_feat")
        s_stage = sem("s_stage")
        s_viol = sem("s_viol")
        s_flag = sem("s_flag")
        s_fill = sem("s_fill")
        s_deg = sem("s_deg")
        s_pos = sem("s_pos")
        s_put = sem("s_put")
        s_first = sem("s_first")
        s_z = [sem(f"s_z{b}") for b in range(2)]
        s_zfree = sem("s_zfree")
        s_xd = sem("s_xd")
        s_ab = sem("s_ab")
        s_squares = sem("s_squares")
        s_blk = sem("s_blk")
        s_sd = sem("s_sd")
        s_last = sem("s_last")
        s_crhs = sem("s_crhs")
        s_relu = sem("s_relu")
        s_pool = sem("s_pool")
        L = range(4)
        s_gat = [[sem(f"s_gat{n}_{s}") for s in range(2)] for n in L]
        s_gfree = [sem(f"s_gfree{n}") for n in L]
        s_chain = [sem(f"s_chain{n}") for n in L]
        s_stat = [sem(f"s_stat{n}") for n in L]
        s_oh = [sem(f"s_oh{n}") for n in L]
        s_ohfree = [sem(f"s_ohfree{n}") for n in L]
        s_sfree = [sem(f"s_sfree{n}") for n in L]
        s_xt = {n: sem(f"s_xt{n}") for n in (0, 3)}
        s_xts = {n: sem(f"s_xts{n}") for n in (0, 3)}
        s_hp = {n: sem(f"s_hp{n}") for n in (0, 3)}
        s_hs = {n: sem(f"s_hs{n}") for n in (0, 3)}
        s_mlp = {n: sem(f"s_mlp{n}") for n in (0, 3)}
        s_mfree = {n: sem(f"s_mfree{n}") for n in (0, 3)}
        s_ea = [sem(f"s_ea{s}") for s in range(2)]
        s_packed = sem("s_packed")
        s_msg = sem("s_msg")
        s_p1 = sem("s_p1")

        s_low = [sem(f"s_low{n}") for n in range(2)]
        s_far = sem("s_far")
        s_ohs = sem("s_ohs")
        s_turned = sem("s_turned")
        s_dig = sem("s_dig")
        s_digits = sem("s_digits")
        s_lob = {n: [sem(f"s_lob{n}_{s}") for s in range(2)] for n in PT}
        s_oht = {n: sem(f"s_oht{n}") for n in PT}
        s_picked = {n: sem(f"s_picked{n}") for n in PT}
        s_masked = {n: sem(f"s_masked{n}") for n in PT}
        s_folded = {n: sem(f"s_folded{n}") for n in PT}
        s_put_in = {n: sem(f"s_put_in{n}") for n in PT}

        x_groups = x[0:FULL * NP, :].rearrange("(g p) c -> p g c", p=NP)
        x_tail = x[FULL * NP:N, :]
        out_groups = out[0:FULL * NP, :].rearrange("(g p) c -> p g c", p=NP)
        out_tail = out[FULL * NP:N, :]
        ea_rows = edge_attr.rearrange("(p t) c -> p (t c)", p=EP)

        def rows_of(table):
            return table.rearrange("(g p) c -> p g c", p=NP)

        dig_p = stat_m[:, :, :, :, :].rearrange("p s a k t -> p (s a k t)")
        dig_g = onehot[:, :, :, :, :].rearrange("p r e o k -> p (r e o k)")
        iota_lo_i = dig_g.bitcast(I32)[:, 0:LO]

        def digits(s):
            a = dig_p[:, s * 2 * DC * NP:(s + 1) * 2 * DC * NP].rearrange("p (d k t) -> p d k t", d=2, t=DC)
            b = dig_g[:, s * 2 * DC * G:(s + 1) * 2 * DC * G].rearrange("p (d k t) -> p d k t", d=2, t=DC)
            return a, b

        def onehot_row(ring, g, d, k):
            return onehot[:, g % 2, d, k, :] if ring == 2 else onehot[:, g // 2 % 2, g % 2, k, :]

        def part_of(t, start, dims):
            size = 1
            for d in dims:
                size *= d
            flat16 = t[0:NP, start:start + size]
            if len(dims) == 2:
                return flat16.rearrange("p (a b) -> p a b", a=dims[0])
            return flat16.rearrange("p (r a b) -> p r a b", r=dims[0], a=dims[1])

        prod16 = prod[:, :, :, :].rearrange("p t a c -> p (t a c)").bitcast(F16)
        hid16 = hid[:, :, :].rearrange("p j e -> p (j e)").bitcast(F16)
        packed16 = packed[:, :, :, :, :].rearrange("p s t d c -> p (s t d c)").bitcast(F16)
        oht = {1: part_of(hid16, 0, (2, B, PT[1] * EP))} | {
            n: part_of(dig_p.bitcast(F16), 0, (2, B, PT[n] * EP)) for n in (2, 3)}
        lob = {1: part_of(packed16, 0, (2, 2, PT[1] * EP))} | {
            n: part_of(dig_g.bitcast(F16), 0, (2, 2, PT[n] * EP)) for n in (2, 3)}
        masked3 = (prod[:, :, :, :].rearrange("p t a c -> p (t a c)")[0:NP, 0:2 * PT[3] * EP]
                   .rearrange("p (r e) -> p r e", r=2))
        p_folded3 = p_pick[0:EP, PT[3] * EP:PT[3] * EP + PT[3] * 2 * C]
        picked = {1: [t[:, :].rearrange("p (q w) -> p q w", q=2) for t in p_pair],
                  2: [*(t[:, :].rearrange("p (q w) -> p q w", q=2) for t in p_pair),
                      p_acc[:, :].rearrange("p (q w) -> p q w", q=2)]}
        p_folded = [p_e, p_xt]
        dig_f = dig_p.bitcast(F32)
        turned = dig_f[0:C, 0:NP * G]
        features = dig_f[0:PC, NP * G:2 * NP * G]
        hidden = dig_g.bitcast(F32)[0:H2, 0:NP * G]
        p_turned, p_features, p_hidden2, p_rooted = (p_xt, p_e), (p_a, p_pick), (p_b, p_d), (p_a, p_b)
        digits_s = feat[:, :].bitcast(F16)

        def unit_masked(n, u, s):
            o, tiles = UNITS[n][u]
            slot = u if n == 2 else s
            return part_of(prod16, slot * 8 * EP, (2, tiles * EP))

        def unit_picked(n, u, s):
            return picked[n][u if n == 2 else s][0:NP, :, 0:UNITS[n][u][1] * EP]

        zb = dig_p.bitcast(F32)[:, 0:2 * BT * R0].rearrange("p (b t f) -> p b t f", b=2, f=R0)

        block = ctx.enter_context(nc.Block())

        def numbered(names):
            return {what: n + 1 for n, what in enumerate(names)}

        products = [(what, q) for what in ("turned", "features", "hidden") for q in range(H)] + ["update"]
        rooted = [("turned3", q) for q in range(H)] + [("rooted", k) for k in range(2)]
        node_step = numbered(["degrees", "unsorted", "within"])
        any_step = numbered([*node_step, "sums0", "sums1", "sums2", *products, *rooted, "sums3"])
        sorted_step = numbered([*node_step, "carry0", "sums0", "sums1", "carry2", *products, *rooted, "carry3"])

        @block.sync
        def _(sp):
            sp.dma_start(ends[:, 0, :], src.rearrange("(p t) -> p t", p=EP)).then_inc(s_in, 16)
            sp.dma_start(ends[:, 1, :], dst.rearrange("(p t) -> p t", p=EP)).then_inc(s_in, 16)
            sp.wait_ge(s_zero, 1)
            with nc.allow_non_contiguous_dma(reason="one destination for each partition"):
                sp.dma_start(nxt[0:EP - 1, :], dst.rearrange("(p t) -> p t", p=EP)[1:EP, 0:1]).then_inc(s_in, 16)
            sp.dma_start(nx[:, 0:FULL, :], x_groups).then_inc(s_in, 16)
            sp.dma_start(nx[0:TAIL, FULL, :], x_tail).then_inc(s_in, 16)
            sp.dma_start(starts[0:E, :].rearrange("(p a b) f -> p a (b f)", p=EP, b=BZ),
                         zero_rows.unsqueeze(1).to_broadcast((EP, TILES // BZ, BZ * R0))).then_inc(s_fill, 16)
            sp.dma_start(ew[:, :], edge_weight.rearrange("(p t) -> p t", p=EP)).then_inc(s_w, 16)
            for j in range(4):
                r = 2 * C * j
                sp.dma_start(w1_0[r:r + 2 * C, j, 0:H0], w1_0t).then_inc(s_w, 16)
                sp.dma_start(w1_0[r:r + C, j, H0:2 * H0], w1_0t[C:2 * C, :]).then_inc(s_w, 16)
                sp.dma_start(w1_0[r + C:r + 2 * C, j, H0:2 * H0], w1_0t[0:C, :]).then_inc(s_w, 16)
            for d in range(2):
                sp.dma_start(b1c_0[d * H0:(d + 1) * H0, :], b1_0.rearrange("(k a) -> k a", a=1)).then_inc(s_w, 16)
                sp.dma_start(w2_0[d * H0:(d + 1) * H0, d * C:(d + 1) * C], w2_0t).then_inc(s_w, 16)
                sp.dma_start(b2r_0[:, d, :], b2_0.rearrange("(a c) -> a c", a=1).to_broadcast((EP, C))).then_inc(s_w, 16)
            sp.dma_start(wg[:, :], wg_t).then_inc(s_w, 16)
            sp.dma_start(w1_2[:, :], w1_2t).then_inc(s_w, 16)
            sp.dma_start(b1c_2[:, :], b1_2.rearrange("(k a) -> k a", a=1)).then_inc(s_w, 16)
            sp.dma_start(w2_2[:, :], w2_2t).then_inc(s_w, 16)
            sp.dma_start(b2r_2[:, :], b2_2.rearrange("(a c) -> a c", a=1).to_broadcast((NP, C))).then_inc(s_w, 16)
            for j in range(8):
                sp.dma_start(w1z_3[j * C:(j + 1) * C, j, :], w1_3).then_inc(s_w, 16)
            sp.dma_start(b1c_3[:, :], b1_3.rearrange("(k a) -> k a", a=1)).then_inc(s_w, 16)
            sp.dma_start(w2s_3[:, :], w2_3).then_inc(s_w, 16)
            sp.dma_start(zr_3[:, 0, :], b2_3.rearrange("(i o) -> i o", i=C)).then_inc(s_w, 16)
            sp.dma_start(zr_3[:, 1, :], root).then_inc(s_w, 16)
            for h in range(H):
                sp.dma_start(fold_z[h * C:(h + 1) * C, C:2 * C], b2_3.rearrange("(i o) -> i o", i=C)).then_inc(s_w, 16)
            sp.wait_ge(s_rows, 1)
            sp.dma_start(rows_of(table0), rows0[:, :, :]).then_inc(s_tab, 16)
            rows_3 = rows3[:, :, :, :].rearrange("p g a c -> p g (a c)")

            def load_attributes(i):
                for s in range(2):
                    sp.wait_ge(s_xt[3], 2 * i + s + 1)
                    sp.dma_start(ea[:, s, :, :].rearrange("p t c -> p (t c)"),
                                 ea_rows[:, bass.ds(i * (2 * CT * C) + s * CT * C, CT * C)]).then_inc(s_ea[s], 16)

            def any_order():
                for n, (table, rows) in enumerate((
                        (table1, nh[:, :, :]),
                        (table2, rows2[:, :, :, :].rearrange("p g a c -> p g (a c)")), (table3, rows_3))):
                    sp.wait_ge(s_rows, n + 2)
                    sp.dma_start(rows_of(table), rows).then_inc(s_tab, 16)
                with sp.Fori(0, PAIRS) as i:
                    load_attributes(i)

            def sorted_order():
                starts_rows = starts[0:E, :].rearrange("(p t) f -> p (t f)", p=EP)
                running_rows = running.rearrange("(p t) c -> p (t c)", p=EP)

                def load_starts(n):
                    sp.wait_ge(s_put, 16 * G * (n + 1))
                    for b in range(BLOCKS):
                        use = n * BLOCKS + b
                        if use >= 2:
                            sp.wait_ge(s_zfree, use - 1)
                        sp.dma_start(zb[0:EP, use % 2, :, :].rearrange("p t f -> p (t f)"),
                                     starts_rows[:, b * BT * R0:(b + 1) * BT * R0]).then_inc(s_z[use % 2], 16)

                def store_running(k, o):
                    sp.wait_ge(s_blk, o + (k * BLOCKS + 1))
                    sp.dma_start(running_rows[:, bass.ds(o * (BT * C), BT * C)],
                                 wide[:, bass.ds(o * BT, BT), :].rearrange("p t c -> p (t c)")).then_inc(s_sd, 16)

                sp.wait_ge(s_dig, 4)
                for d in range(2):
                    sp.dma_start(digits_t[d].rearrange("(u r) e -> r u e", r=DT),
                                 digits_s[:, d * 8 * EP:(d + 1) * 8 * EP].rearrange("p (u e) -> p u e", e=EP)
                                 ).then_inc(s_digits, 16)

                def load_digits(n, i, first=False):
                    for s in range(2):
                        if not first:
                            sp.wait_ge(s_masked[n], (2 * i + s) * UN[n] + (RING[n] - UN[n]))
                        at = bass.ds((i * (2 * CT) + (s * CT + CT - PT[n])) * EP, PT[n] * EP)
                        sp.dma_start(lob[n][:, s], digits_t.rearrange("d t e -> d (t e)")[:, at].unsqueeze(0)
                                     .to_broadcast((NP, 2, PT[n] * EP))).then_inc(s_lob[n][s], 16)

                load_starts(0)
                with sp.Fori(0, BLOCKS) as o:
                    store_running(0, o)
                sp.wait_ge(s_rows, 2)
                sp.dma_start(rows_of(table1), nh[:, :, :]).then_inc(s_tab, 16)
                sp.wait_ge(s_digits, 32)
                load_digits(1, 0, first=True)
                load_starts(1)
                with sp.Fori(1, PAIRS) as i:
                    load_digits(1, i)
                sp.wait_ge(s_rows, 3)
                sp.dma_start(rows_of(table2f), ncc[:, :, :]).then_inc(s_tab, 16)
                load_digits(2, 0, first=True)
                with sp.Fori(1, BP + LAG + 1) as i:
                    load_digits(2, i)
                with sp.Fori(0, BLOCKS - 2) as o:
                    store_running(1, o)
                    with sp.Fori(0, BP) as k:
                        load_digits(2, o * BP + k + (BP + LAG + 1))
                store_running(1, BLOCKS - 2)
                with sp.Fori((BLOCKS - 1) * BP + LAG + 1, PAIRS) as i:
                    load_digits(2, i)
                store_running(1, BLOCKS - 1)
                sp.wait_ge(s_rows, 4)
                sp.dma_start(rows_of(table3), rows_3).then_inc(s_tab, 16)
                load_attributes(0)
                load_digits(3, 0, first=True)
                with sp.Fori(1, BP) as k:
                    load_attributes(k)
                    load_digits(3, k)
                with sp.Fori(0, BLOCKS - 1) as o:
                    load_attributes(o * BP + BP)
                    load_digits(3, o * BP + BP)
                    store_running(2, o)
                    with sp.Fori(1, BP) as k:
                        load_attributes(o * BP + BP + k)
                        load_digits(3, o * BP + BP + k)
                store_running(2, BLOCKS - 1)

            sp.wait_ge(s_flag, 1)
            is_sorted = sp.value_load(flag[0:1, 0:1], min_val=0, max_val=1)
            with sp.If(is_sorted):
                sorted_order()
            with sp.Else():
                any_order()
            sp.wait_ge(s_rows, 5)
            sp.dma_start(out_groups, nx[:, 0:FULL, :]).then_inc(s_out, 16)
            sp.dma_start(out_tail, nx[0:TAIL, FULL, :]).then_inc(s_out, 16)
            sp.wait_ge(s_out, 32)
            sp.wait_ge(s_fill, 16)

        @block.gpsimd
        def _(pool):
            pool.memset(identity[:, :], 0.0).then_inc(s_const, 1)
            pool.wait_ge(s_const, 1)
            pool.affine_select(out=identity[:, :], in_=identity[:, :], compare_op=ALU.not_equal, fill=1.0,
                               base=0, pattern=[[-1, 128]], channel_multiplier=1).then_inc(s_const, 1)
            pool.iota(iota_lo_i, [[1, LO]], base=0, channel_multiplier=0).then_inc(s_const, 1)
            pool.iota(iota_kt_i.rearrange("p (k t) -> p k t", t=DC), [[1, NP], [0, DC]], base=0,
                      channel_multiplier=0).then_inc(s_const, 1)
            pool.iota(spare_i[:, :], [[NP, G]], base=E, channel_multiplier=1).then_inc(s_const, 1)
            pool.memset(ones[:, :], 1.0).then_inc(s_const, 1)
            pool.memset(upper[:, :], 1.0).then_inc(s_const, 1)
            pool.wait_ge(s_const, 7)
            pool.affine_select(out=upper[:, :], in_=upper[:, :], compare_op=ALU.is_ge, fill=0.0,
                               base=0, pattern=[[1, NP]], channel_multiplier=-1).then_inc(s_const, 1)
            pool.iota(place_i[:, :], [[NP, B]], base=0, channel_multiplier=1).then_inc(s_const, 1)
            pool.wait_ge(s_in, 80)

            def gather_chunks(n, table, ends_of, row, tiles=CT):
                pool.wait_ge(s_tab, 16 * (n + 1))
                with pool.Fori(0, PAIRS) as i:
                    for s in range(2):
                        pool.wait_ge(s_gfree[n], 2 * i + s + 1)
                        pool.sem_inc(s_pool, 1)
                        pool.tensor_copy(istage[:, s, :, :], ends[:, :, bass.ds(i * (2 * CT) + s * CT, CT)]).then_inc(s_stage, 1)
                        pool.wait_ge(s_stage, 2 * i + s + 1 + n * CHUNKS)
                        pool.sem_inc(s_pool, 1)
                        for t in range(tiles):
                            for d in ends_of:
                                pool.indirect_dma_start(row(s, t, d), None, table,
                                                        bass.IndirectOffsetOnAxis(istage[:, s, d, t:t + 1], 0)
                                                        ).then_inc(s_gat[n][s], 16)

            def any_order():
                gather_chunks(0, table0, (0, 1), lambda s, t, d: gat[:, s, t, d * R0:(d + 1) * R0])
                gather_chunks(1, table1, (0, 1), lambda s, t, d: gat[:, s, t, d * R0:d * R0 + C])
                gather_chunks(2, table2, (0,), lambda s, t, d: gat[:, s, t, 0:C].bitcast(F16))
                gather_chunks(3, table3, (0,), lambda s, t, d: gat[:, s, t, 0:2 * C])

            def sorted_order():
                def put_rows(n, table):
                    pool.wait_ge(s_rows, n + 1)
                    for g in range(G):
                        pool.indirect_dma_start(starts, bass.IndirectOffsetOnAxis(first_edge[:, g:g + 1], 0),
                                                rows0[:, g, :], None).then_inc(s_put, 16)
                    pool.wait_ge(s_tab, 16 * (n + 1))
                    pool.indirect_dma_start(first_rows[:, 0:table.shape[1]], None, table,
                                            bass.IndirectOffsetOnAxis(ends[:, 1, 0:1], 0)).then_inc(s_first, 16)

                def get_last(k):
                    pool.wait_ge(s_sd, 16 * BLOCKS * (k + 1))
                    for g in range(G):
                        pool.indirect_dma_start(last_rows[:, g, :], None, running,
                                                bass.IndirectOffsetOnAxis(last_edge[:, g:g + 1], 0)).then_inc(s_last, 16)

                pool.wait_ge(s_pos, 1)
                pool.wait_ge(s_fill, 16)
                put_rows(0, table0)
                gather_chunks(0, table0, (0,), lambda s, t, d: gat[:, s, t, 0:R0])
                get_last(0)
                put_rows(1, table1)
                gather_chunks(1, table1, (0,), lambda s, t, d: gat[:, s, t, 0:C], CT - PT[1])
                gather_chunks(2, table2f, (0,), lambda s, t, d: gat[:, s, t, 0:C], CT - PT[2])
                get_last(1)
                gather_chunks(3, table3, (0,), lambda s, t, d: gat[:, s, t, 0:2 * C], CT - PT[3])
                get_last(2)

            pool.wait_ge(s_flag, 1)
            is_sorted = pool.value_load(flag[0:1, 0:1], min_val=0, max_val=1)
            with pool.If(is_sorted):
                sorted_order()
            with pool.Else():
                any_order()

        @block.scalar
        def _(act):
            def square_root(k, out_ap, in_ap):
                act.wait_ge(s_sq, k)
                nc.scalar.activation(out_ap, in_ap, ACT.Sqrt).then_inc(s_rt, 1)

            square_root(1, stat[:, 2, :], stat[:, 1, :])
            square_root(2, stat[:, 2, :], stat[:, 1, :])
            square_root(3, stat[:, 2, :], stat[:, 1, :])

            def hidden0(s, i2):
                act.wait_ge(s_xt[0], i2 + 1)
                nc.scalar.activation(xt[:, :, :], p_xt[:, 0:4 * EP].rearrange("p (q e) -> p q e", q=4),
                                     ACT.Copy).then_inc(s_xts[0], 1)
                for j in range(4):
                    act.wait_ge(s_hp[0], i2 * 4 + j + 1)
                    nc.scalar.activation(hid[:, j, :], p_hid[j % 2][:, 0:4 * EP], ACT.Relu,
                                         bias=b1c_0[:, 0:1]).then_inc(s_hs[0], 1)

            def squares0(i2):
                act.wait_ge(s_ab, i2 + 1)
                nc.scalar.activation(prod[:, :, 0:2, :], ab[:, :, :, :], ACT.Square).then_inc(s_squares, 1)

            def parts0(i2, ends_of):
                act.wait_ge(s_msg, i2 + 1)
                for d in ends_of:
                    last = nc.scalar.activation(part_h[:, 0, d].rearrange("p c t -> p t c"), m[:, :, d, :], ACT.Copy)
                last.then_inc(s_p1, 1)

            far = [t.rearrange("p a b c -> p (a b c)").bitcast(F16)[0:EP, 0:2 * LO].rearrange("p (k l) -> p k l", k=2)
                   for t in (ea[:, :, :, :], pr[:, :, :, :])]

            def onehots_s(s, chunk, g):
                act.wait_ge(s_low[1], chunk + 1)
                act.wait_ge(s_ohfree[1], chunk * (CT // OG) + (g + 1))
                for j in range(2):
                    for q in range(2):
                        t = g * OG + 2 * j + q
                        last = nc.scalar.activation(far[j][:, q, :], iota_lo[:, :], ACT.Abs,
                                                    bias=lstage[:, s, 0, t:t + 1], scale=-1.0)
                    last.then_inc(s_far, 1)
                    act.wait_ge(s_far, chunk * (2 * SHARED) + ((g - SG) * 2 + j + 1))
                    for q in range(2):
                        last = nc.scalar.activation(onehot_row(4, g, 0, 2 * j + q), far[j][:, q, :], ACT.Relu,
                                                    bias=ones[0:EP, 0:1], scale=-1.0)
                last.then_inc(s_ohs, 1)

            def layer0(pack, ends_of, blocks_ready=0):
                pack(0, 0)
                hidden0(0, 0)
                pack(0, 1)
                squares0(0)
                hidden0(1, 1)
                if blocks_ready:
                    act.wait_ge(s_xd, blocks_ready)
                with act.Fori(0, PAIRS - 1) as i:
                    parts0(2 * i, ends_of)
                    pack(i + 1, 0)
                    squares0(2 * i + 1)
                    hidden0(0, 2 * i + 2)
                    parts0(2 * i + 1, ends_of)
                    pack(i + 1, 1)
                    squares0(2 * i + 2)
                    hidden0(1, 2 * i + 3)
                parts0(CHUNKS - 2, ends_of)
                squares0(CHUNKS - 1)
                parts0(CHUNKS - 1, ends_of)

            def hidden2(step):
                for q in range(H):
                    act.wait_ge(s_node, step[("hidden", q)])
                    nc.scalar.activation(hidden[:, q * LO:(q + 1) * LO], p_hidden2[q % 2][0:H2, 0:LO], ACT.Relu,
                                         bias=b1c_2[:, 0:1]).then_inc(s_relu, 1)

            def layer3(put_in=lambda s, chunk: None):
                with act.Fori(0, PAIRS) as i:
                    for s in range(2):
                        act.wait_ge(s_xt[3], 2 * i + s + 3)
                        nc.scalar.activation(xt[:, 0:2, :], p_xt[:, 0:2 * EP].rearrange("p (u e) -> p u e", u=2),
                                             ACT.Copy).then_inc(s_xts[3], 1)
                        for j in range(4):
                            act.wait_ge(s_hp[3], (2 * i + s) * 4 + j + 1)
                            nc.scalar.activation(hid[:, j, :], p_hid[j % 2][:, 0:4 * EP], ACT.Relu,
                                                 bias=b1c_3[:, 0:1]).then_inc(s_hs[3], 1)
                        put_in(s, 2 * i + s)

            def any_order():
                def pack(i, s):
                    act.wait_ge(s_gat[0][s], (i + 1) * (2 * CT * 16))
                    nc.scalar.activation(packed[:, s, :, :, :],
                                         gat[:, s, :, :].rearrange("p t (d f) -> p t d f", d=2)[:, :, :, 0:C],
                                         ACT.Copy).then_inc(s_packed, 1)

                layer0(pack, (0, 1))
                square_root(4, stat[:, 2, :], stat[:, 1, :])
                square_root(5, stat[:, 2, :], stat[:, 1, :])
                hidden2(any_step)
                square_root(6, stat[:, 2, :], stat[:, 1, :])
                layer3()

            def sorted_order():
                def pack(i, s):
                    act.wait_ge(s_gat[0][s], (i + 1) * (CT * 16))
                    nc.scalar.activation(packed[:, s, :, 0, :], gat[:, s, :, 0:C], ACT.Copy)
                    nc.scalar.activation(rs[:, s, :], gat[:, s, :, C], ACT.Copy).then_inc(s_gfree[0], 1)
                    nc.scalar.activation(packed[:, s, :, 1, :], wide[:, bass.ds(i * (2 * CT) + s * CT, CT), :],
                                         ACT.Copy).then_inc(s_packed, 1)

                banks = (p_c, p_d, p_e, p_acc)
                for k in range(4):
                    act.wait_ge(s_turned, k + 1)
                    nc.scalar.activation(digits_s[:, k * 4 * EP:(k + 1) * 4 * EP], banks[k][0:DT, 0:4 * EP],
                                         ACT.Copy).then_inc(s_dig, 1)
                act.wait_ge(s_xd, 1)
                layer0(pack, (0,), blocks_ready=BLOCKS)
                square_root(4, stat[:, 2, :], stat[:, 1, :])
                act.sem_inc(s_put_in[1], 2)

                def put_in1(s, chunk):
                    act.wait_ge(s_folded[1], chunk * UN[1] + (UN[1] + RING[1]))
                    act.wait_ge(s_gfree[1], chunk + 1)
                    nc.scalar.activation(gat[:, s, CT - PT[1]:CT, 0:C],
                                         p_folded[s][0:EP, 0:PT[1] * C].rearrange("p (t c) -> p t c", c=C),
                                         ACT.Copy, scale=1.0 / SCALE16).then_inc(s_put_in[1], 1)

                def chunk1(s, chunk, more=True):
                    onehots_s(s, chunk, SG)
                    if more:
                        put_in1(1 - s, chunk + 1)
                    for g in range(SG + 1, CT // OG):
                        onehots_s(s, chunk, g)

                put_in1(0, 0)
                with act.Fori(0, PAIRS - 1) as i:
                    chunk1(0, 2 * i)
                    chunk1(1, 2 * i + 1)
                chunk1(0, CHUNKS - 2)
                chunk1(1, CHUNKS - 1, more=False)
                square_root(5, stat[:, 2, :], stat[:, 1, :])
                act.sem_inc(s_gfree[2], 2)
                act.sem_inc(s_put_in[2], 2)
                with act.Fori(0, PAIRS) as i:
                    for s in range(2):
                        act.wait_ge(s_gat[2][s], (i + 1) * ((CT - PT[2]) * 16))
                        nc.scalar.activation(wide[:, bass.ds(i * (2 * CT) + s * CT, CT - PT[2]), :],
                                             gat[:, s, 0:CT - PT[2], 0:C], ACT.Copy).then_inc(s_gfree[2], 1)
                        act.wait_ge(s_folded[2], (2 * i + s + 1) * UN[2] + RING[2])
                        nc.scalar.activation(wide[:, bass.ds(i * (2 * CT) + (s * CT + CT - PT[2]), PT[2]), :],
                                             p_folded[s][0:EP, 0:PT[2] * C].rearrange("p (t c) -> p t c", c=C),
                                             ACT.Copy, scale=1.0 / SCALE16).then_inc(s_put_in[2], 1)
                hidden2(sorted_step)
                square_root(6, stat[:, 2, :], stat[:, 1, :])

                def put_in3(s, chunk):
                    act.wait_ge(s_folded[3], chunk + 3)
                    act.wait_ge(s_gfree[3], chunk + 1)
                    nc.scalar.activation(gat[:, s, CT - PT[3]:CT, 0:2 * C],
                                         p_folded3.rearrange("p (t c) -> p t c", c=2 * C),
                                         ACT.Copy, scale=1.0 / SCALE16).then_inc(s_put_in[3], 1)

                layer3(put_in3)

            act.wait_ge(s_flag, 1)
            is_sorted = act.value_load(flag[0:1, 0:1], min_val=0, max_val=1)
            with act.If(is_sorted):
                sorted_order()
            with act.Else():
                any_order()

        @block.vector
        def _(dve):
            step = {}
            v = nc.vector
            c = Chain(dve, s_dve)

            v.memset(nx[:, FULL, :], 0.0)
            v.memset(nxt[:, :], NP * G)
            v.memset(zero_rows, 0.0)
            v.memset(w1_0[:, :, :], 0.0)
            v.memset(w2_0[:, :], 0.0)
            v.memset(w1z_3[:, :, :], 0.0)
            v.memset(rows0[:, :, C:R0], 0.0)
            v.memset(zeros[:, :], 0.0)
            v.memset(rows3[:, :, :, :], 0.0).then_inc(s_zero, 1)
            dve.wait_ge(s_zero, 1)

            dve.wait_ge(s_in, 80)
            dve.wait_ge(s_const, 9)
            c.link(v.tensor_copy(iota_lo[:, :], iota_lo_i))
            c.link(v.tensor_copy(n_f[:, :, :], ends[:, :, :]))
            c.link(v.tensor_scalar(t_f[:, :, :], n_f[:, :, :], -(NP - 1) / 2.0, 1.0 / NP, ALU.add, ALU.mult))
            c.link(v.tensor_scalar(t_f[:, :, :], t_f[:, :, :], MAGIC, None, ALU.add))
            c.link(v.tensor_scalar(t_f[:, :, :], t_f[:, :, :], -MAGIC, None, ALU.add))
            v.tensor_copy(group[:, :, :], t_f[:, :, :])
            c.link(v.scalar_tensor_tensor(place[:, :, :], t_f[:, :, :], -float(NP), n_f[:, :, :], ALU.mult, ALU.add))
            c.link(v.tensor_scalar(t_f[:, :, :], n_f[:, :, :], -(LO - 1) / 2.0, 1.0 / LO, ALU.add, ALU.mult))
            c.link(v.tensor_scalar(t_f[:, :, :], t_f[:, :, :], MAGIC, None, ALU.add))
            c.link(v.tensor_scalar(t_f[:, :, :], t_f[:, :, :], -MAGIC, None, ALU.add))
            for d in range(2):
                v.scalar_tensor_tensor(lo[d], t_f[:, d, :], -float(LO), n_f[:, d, :], ALU.mult, ALU.add)
            v.tensor_copy(iota_kt[:, :, :], iota_kt_i.rearrange("p (k t) -> p k t", t=DC))
            v.tensor_copy(dig_l[:, 0:1], place[:, 1, TILES - 1:TILES])
            v.tensor_copy(dig_l[:, 1:2], group[:, 1, TILES - 1:TILES])
            v.memset(same[:, 0:1], 0.0)
            v.tensor_tensor(same[:, 1:TILES], n_f[:, 1, 1:TILES], n_f[:, 1, 0:TILES - 1], ALU.is_equal)
            c.link(v.tensor_copy(nxt_f[:, :], nxt[:, :]))
            v.tensor_tensor(cont[:, :], nxt_f[:, :], n_f[:, 1, TILES - 1:TILES], ALU.is_equal)
            v.tensor_tensor(viol[:, 1:2], nxt_f[:, :], n_f[:, 1, TILES - 1:TILES], ALU.is_lt)
            c.link(v.tensor_tensor(rd[:, 1:TILES], n_f[:, 1, 1:TILES], n_f[:, 1, 0:TILES - 1], ALU.is_lt))
            c.link(v.tensor_reduce(viol[:, 0:1], rd[:, 1:TILES], AX_X, ALU.add))
            c.link(v.tensor_tensor(viol_f[:, :], viol[:, 0:1], viol[:, 1:2], ALU.add))
            dve.sem_inc(s_viol, 1)

            dve.sem_inc(s_cnt_mm, 2)
            with dve.Fori(0, TILES // DC // DU) as i:
                for s in range(DU):
                    dve.wait_ge(s_cnt_mm, DU * i + s + 1)
                    a, b = digits(s % 2)
                    at = bass.ds(i * (DU * DC) + s * DC, DC)
                    for d in range(2):
                        v.tensor_tensor(a[:, d], place[:, d, at].unsqueeze(1).to_broadcast((EP, NP, DC)),
                                        iota_kt[:, :, :], ALU.is_equal)
                        last = v.tensor_tensor(b[:, d], group[:, d, at].unsqueeze(1).to_broadcast((EP, G, DC)),
                                               iota_kt[:, 0:G, :], ALU.is_equal)
                    last.then_inc(s_cnt_oh, 1)

            roots = [0]

            def mask_high(d):
                v.tensor_tensor(hmask[d], t_f[:, d, :].unsqueeze(1).to_broadcast((EP, H, TILES)),
                                iota_lo[0:EP, 0:H].unsqueeze(2).to_broadcast((EP, H, TILES)), ALU.is_equal)

            def inverse_root(out_ap, in_ap):
                c.link(v.tensor_copy(stat[:, 1, :], in_ap))
                roots[0] += 1
                dve.sem_inc(s_sq, 1)
                dve.wait_ge(s_rt, roots[0])
                c.link(v.reciprocal(stat[:, 3, :], stat[:, 2, :]))
                c.link(v.tensor_tensor(stat[:, 2, :], stat[:, 3, :], stat[:, 3, :], ALU.mult))
                c.link(v.scalar_tensor_tensor(stat[:, 2, :], stat[:, 2, :], -0.5, stat[:, 1, :], ALU.mult, ALU.mult))
                c.link(v.scalar_tensor_tensor(out_ap, stat[:, 2, :], 1.5, stat[:, 3, :], ALU.add, ALU.mult))

            def over_channels(ap):
                return ap.unsqueeze(2).to_broadcast((NP, G, C))

            def layernorm_relu():
                c.link(v.tensor_reduce(stat[:, 0, :], nx[:, :, :], AX_X, ALU.add))
                c.link(v.tensor_scalar(stat[:, 0, :], stat[:, 0, :], 1.0 / C, None, ALU.mult))
                c.link(v.tensor_tensor(na[:, :, :], nx[:, :, :], over_channels(stat[:, 0, :]), ALU.subtract))
                c.link(v.tensor_tensor(nb[:, :, :], na[:, :, :], na[:, :, :], ALU.mult))
                c.link(v.tensor_reduce(stat[:, 3, :], nb[:, :, :], AX_X, ALU.add))
                c.link(v.tensor_scalar(stat[:, 3, :], stat[:, 3, :], 1.0 / C, EPS, ALU.mult, ALU.add))
                inverse_root(stat[:, 0, :], stat[:, 3, :])
                c.link(v.tensor_tensor(nb[:, :, :], na[:, :, :], over_channels(stat[:, 0, :]), ALU.mult))
                c.link(v.tensor_scalar(nh[:, :, :], nb[:, :, :], 0.0, None, ALU.max))

            def layer_sums(n, what):
                dve.wait_ge(s_done, n + 1)
                v.tensor_copy(accs[:, :], p_acc[0:NP, 0:LO]).then_inc(s_accs, 1)
                dve.wait_ge(s_node, step[what])
                return p_a[0:NP, 0:G * C].rearrange("p (b h c) -> p h b c", b=B, h=H)

            def by_high(t):
                return t[:, :, :].rearrange("p (h b) c -> p h b c", b=B)

            def sums_to(t, n, what):
                c.link(v.tensor_copy(by_high(t), layer_sums(n, what)))

            def onehots(n, chunk, s, g, og, ring, ends_of):
                dve.wait_ge(s_ohfree[n], chunk * (CT // og) + g + 1)
                for k in range(og):
                    for d in ends_of:
                        last = v.tensor_scalar(onehot_row(ring, g, d, k), iota_lo[0:EP, :],
                                               lstage[:, s, d, g * og + k:g * og + k + 1], None, ALU.is_equal)
                last.then_inc(s_oh[n], 1)

            def onehot_tile(n, chunk, s, t):
                g, k = t // OG, t % OG
                if k == 0:
                    dve.wait_ge(s_ohfree[n], chunk * (CT // OG) + g + 1)
                row = v.tensor_scalar(onehot_row(4, g, 0, k), iota_lo[0:EP, :], lstage[:, s, 0, t:t + 1], None,
                                      ALU.is_equal)
                if k == OG - 1:
                    row.then_inc(s_oh[n], 1)

            def build_onehots(n, chunk, s, ring, ends_of):
                for g in range(CT // OG):
                    onehots(n, chunk, s, g, OG, ring, ends_of)

            def stage_low(i, s, ends_of):
                for d in ends_of:
                    last = v.tensor_scalar(lstage[:, s, d, :], lo[d][:, bass.ds(i * (2 * CT) + s * CT, CT)],
                                           0.0, None, ALU.add)
                return last

            def weigh(out2, part, i, s, d):
                mask = hmask[d][:, :, bass.ds(i * (2 * CT) + s * CT, CT)]
                return v.tensor_tensor(out2.rearrange("p (h c) t -> p h c t", h=H),
                                       part.unsqueeze(1).to_broadcast((EP, H, C, CT)),
                                       mask.unsqueeze(2).to_broadcast((EP, H, C, CT)), ALU.mult)

            def split3(c, msg, meanwhile=lambda k: None):
                parts = [part_b[:, q].rearrange("p c t -> p t c") for q in range(3)]
                c.link(v.tensor_copy(parts[0], msg), lambda: meanwhile(5))
                c.link(v.tensor_tensor(mt[:, :, 0, :], msg, parts[0], ALU.subtract), lambda: meanwhile(6))
                c.link(v.tensor_copy(parts[1], mt[:, :, 0, :]), lambda: meanwhile(7))
                c.link(v.tensor_tensor(parts[2], mt[:, :, 0, :], parts[1], ALU.subtract), lambda: meanwhile(8))

            layernorm_relu()
            dve.wait_ge(s_node, node_step["degrees"])
            c.link(v.tensor_copy(degs[:, :, :], p_a[0:NP, 0:2 * G].rearrange("p (d g) -> p d g", d=2)))
            dve.sem_inc(s_deg, 1)
            c.link(v.tensor_tensor(rdeg[:, :], degs[:, 0, :], degs[:, 1, :], ALU.add))
            c.link(v.tensor_scalar(rdeg[:, :], rdeg[:, :], EPS, None, ALU.max))
            inverse_root(rdeg[:, :], rdeg[:, :])
            c.link(v.tensor_scalar(dis[:, :], degs[:, 1, :], 1.0, None, ALU.add))
            inverse_root(dis[:, :], dis[:, :])
            v.tensor_scalar(rows0[:, :, C], rdeg[:, :], SCALE16, None, ALU.mult)
            v.tensor_copy(rows0[:, :, 0:C], nh[:, :, :]).then_inc(s_rows, 1)

            dve.wait_ge(s_node, node_step["unsorted"])
            v.tensor_scalar(flag[:, :], p_c[0:1, 0:1], 0.5, None, ALU.is_lt).then_inc(s_flag, 1)

            def nodes0():
                c.link(v.tensor_tensor(nb[:, :, :], na[:, :, :], over_channels(rdeg[:, :]), ALU.mult))
                c.link(v.scalar_tensor_tensor(na[:, :, :], nb[:, :, :], 1.0 / SCALE16, nh[:, :, :], ALU.mult, ALU.add))
                c.link(v.scalar_tensor_tensor(nx[:, :, :], na[:, :, :], 0.0, nx[:, :, :], ALU.max, ALU.add))

            def nodes1():
                c.link(v.tensor_tensor(nb[:, :, :], na[:, :, :], nx[:, :, :], ALU.add))
                c.link(v.tensor_scalar(na[:, :, :], nh[:, :, :], -0.2, 1.0, ALU.mult, ALU.add))
                c.link(v.tensor_tensor(ncc[:, :, :], na[:, :, :], nh[:, :, :], ALU.mult))
                c.link(v.scalar_tensor_tensor(na[:, :, :], nh[:, :, :], -1.0, ncc[:, :, :], ALU.add, ALU.mult))
                c.link(v.scalar_tensor_tensor(nx[:, :, :], na[:, :, :], 0.1, nb[:, :, :], ALU.add, ALU.add))

            def nodes2(scale):
                c.link(v.scalar_tensor_tensor(nb[:, :, :], na[:, :, :], scale, ncc[:, :, :], ALU.mult, ALU.add))
                c.link(v.tensor_tensor(na[:, :, :], nb[:, :, :], over_channels(dis[:, :]), ALU.mult))
                dve.sem_inc(s_feat, 1)
                for q in range(H):
                    dve.wait_ge(s_node, step[("turned", q)])
                    v.tensor_copy(turned[:, q * LO:(q + 1) * LO], p_turned[q % 2][0:C, 0:LO]).then_inc(s_feat, 1)
                for q in range(H):
                    dve.wait_ge(s_node, step[("features", q)])
                    v.tensor_copy(features[:, q * LO:(q + 1) * LO], p_features[q % 2][0:PC, 0:LO]).then_inc(s_feat, 1)
                dve.wait_ge(s_node, step["update"])
                c.link(v.tensor_tensor(nb[:, :, :], p_c[0:NP, 0:G * C].rearrange("p (g c) -> p g c", g=G),
                                       b2r_2[:, :].unsqueeze(1).to_broadcast((NP, G, C)), ALU.add))
                c.link(v.tensor_tensor(na[:, :, :], nb[:, :, :], nh[:, :, :], ALU.add))
                c.link(v.tensor_tensor(nx[:, :, :], nx[:, :, :], na[:, :, :], ALU.add))

            def rows_3(more=lambda: None):
                layernorm_relu()
                dve.sem_inc(s_feat, 1)
                more()
                for q in range(H):
                    dve.wait_ge(s_node, step[("turned3", q)])
                    v.tensor_copy(turned[:, q * LO:(q + 1) * LO], p_turned[q % 2][0:C, 0:LO]).then_inc(s_feat, 1)
                for k in range(2):
                    dve.wait_ge(s_node, step[("rooted", k)])
                    both = p_rooted[k][0:NP, 0:G * C].rearrange("p (g r c) -> p g r c", g=G // 2, r=2)
                    half = slice(k * G // 2, (k + 1) * G // 2)
                    v.tensor_copy(rows3[:, half, 1, :], both[:, :, 0, :])
                    v.tensor_copy(ncc[:, half, :], both[:, :, 1, :]).then_inc(s_feat, 1)
                v.tensor_copy(rows3[:, :, 0, :], nh[:, :, :]).then_inc(s_rows, 1)

            def nodes3():
                c.link(v.tensor_tensor(nb[:, :, :], na[:, :, :], ncc[:, :, :], ALU.add))
                c.link(v.tensor_tensor(nx[:, :, :], nx[:, :, :], nb[:, :, :], ALU.add))
                dve.sem_inc(s_rows, 1)

            def messages0(c, s, chunk, xs, xd, rs, rd, to_dst, onehot_tile=lambda t: None):

                def step(ins, *tiles):
                    c.link(ins, lambda: [onehot_tile(t) for t in tiles])

                dve.wait_ge(s_mlp[0], chunk + 1)
                step(v.tensor_tensor(ab[:, :, :, :], p_ab[s][0:EP, :].rearrange("p (t d c) -> p t d c", t=CT, d=2),
                                     b2r_0[:, :, :].unsqueeze(1).to_broadcast((EP, CT, 2, C)), ALU.add), 0)
                dve.sem_inc(s_mfree[0], 1)
                dve.sem_inc(s_ab, 1)
                a, b = ab[:, :, 0, :], ab[:, :, 1, :]
                v.tensor_tensor(prod[:, :, 2, :], a, xs, ALU.mult)
                v.tensor_tensor(prod[:, :, 3, :], b, xd, ALU.mult)
                v.tensor_tensor(prod[:, :, 4, :], a, xd, ALU.mult)
                v.tensor_tensor(prod[:, :, 5, :], b, xs, ALU.mult)
                step(v.tensor_tensor(prod[:, :, 6, :], a, b, ALU.mult), 1, 2)
                dve.wait_ge(s_squares, chunk + 1)
                step(v.tensor_reduce(dots[:, :, :], prod[:, :, :, :], AX_X, ALU.add), 3)
                step(v.tensor_scalar(inv[:, :, :], dots[:, :, 0:2], 1e-24, 0.5, ALU.max, ALU.mult), 4)
                step(v.reciprocal(inv[:, :, :], inv[:, :, :]), 5)
                step(v.tensor_tensor(co[:, :, :], inv[:, :, :], dots[:, :, 2:4], ALU.mult), 6)
                step(v.tensor_tensor(cx[:, :, :], co[:, :, :], dots[:, :, 6:7].to_broadcast((EP, CT, 2)), ALU.mult), 7)
                v.tensor_tensor(ga[:, :, 0], dots[:, :, 4], cx[:, :, 1], ALU.subtract)
                step(v.tensor_tensor(ga[:, :, 1], dots[:, :, 5], cx[:, :, 0], ALU.subtract), 8)
                step(v.tensor_tensor(ga[:, :, :], ga[:, :, :], inv[:, :, :], ALU.mult), 9)
                step(v.tensor_tensor(mt[:, :, :, :], ab[:, :, :, :],
                                     co[:, :, :].unsqueeze(3).to_broadcast((EP, CT, 2, C)), ALU.mult), 10)
                v.tensor_tensor(m[:, :, 0, :], xd, mt[:, :, 1, :], ALU.subtract)
                step(v.tensor_tensor(m[:, :, 1, :], xs, mt[:, :, 0, :], ALU.subtract), 11)
                step(v.tensor_tensor(mt[:, :, :, :], ab[:, :, :, :],
                                     ga[:, :, :].unsqueeze(3).to_broadcast((EP, CT, 2, C)), ALU.mult), 12)
                step(v.tensor_tensor(m[:, :, :, :], m[:, :, :, :], mt[:, :, :, :], ALU.subtract), 13)
                v.tensor_tensor(m[:, :, 0, :], m[:, :, 0, :], rd, ALU.mult)
                step(v.tensor_tensor(to_dst, m[:, :, 1, :], rs, ALU.mult), 14, 15)
                dve.sem_inc(s_msg, 1)

            def messages1(c, i, s, xd, meanwhile=lambda k: None):
                xs = gat[:, s, :, 0:C]
                c.link(v.tensor_scalar(mt[:, :, 0, :], xs, 0.9, 5.0, ALU.mult, ALU.add), lambda: meanwhile(0))
                c.link(v.scalar_tensor_tensor(mt[:, :, 1, :], xd, 0.1, mt[:, :, 0, :], ALU.mult, ALU.add),
                       lambda: meanwhile(1))
                v.reciprocal(mt[:, :, 0, :], mt[:, :, 1, :])
                c.link(v.tensor_tensor(m[:, :, 0, :], xs, xd, ALU.mult), lambda: meanwhile(2))
                dve.sem_inc(s_gfree[1], 1)
                c.link(v.tensor_tensor(m[:, :, 1, :], m[:, :, 0, :], mt[:, :, 0, :], ALU.mult), lambda: meanwhile(3))
                c.link(v.tensor_tensor(m[:, :, 0, :], m[:, :, 1, :],
                                       ew[:, bass.ds(i * (2 * CT) + s * CT, CT)].unsqueeze(2)
                                       .to_broadcast((EP, CT, C)), ALU.mult), lambda: meanwhile(4))

            def use_weights(link, s, chunk, j, banks):
                dve.wait_ge(s_mlp[3], chunk * HALF + j + 1)
                rows = gat[:, s, :, :].rearrange("p (u j) f -> p j u f", u=2)[:, j, :, 0:C]
                link(v.tensor_tensor(pr[:, :, :, :], p_w[j % banks][0:EP, :].rearrange("p (u i o) -> p u i o", u=2, i=C),
                                     rows.unsqueeze(3).to_broadcast((EP, 2, C, C)), ALU.mult))
                dve.sem_inc(s_mfree[3], 1)
                link(v.tensor_reduce(m[:, :, 0, :].rearrange("p (u j) c -> p j u c", u=2)[:, j],
                                     pr[:, :, :, :].rearrange("p u i o -> p u o i"), AX_X, ALU.add))

            def any_order():
                mask_high(0)
                mask_high(1)
                dve.wait_ge(s_w, 16 * W_LOADS)
                dve.sem_inc(s_gfree[0], 2)
                dve.sem_inc(s_ohfree[0], 2)
                dve.sem_inc(s_sfree[0], 2)
                dve.sem_inc(s_mfree[0], 2)
                STEPS0 = 17
                with dve.Fori(0, PAIRS) as i:
                    c0 = Chain(dve, s_chain[0], i * (2 * STEPS0))
                    for s in range(2):
                        dve.wait_ge(s_gat[0][s], (i + 1) * (2 * CT * 16))
                        messages0(c0, s, 2 * i + s, gat[:, s, :, 0:C], gat[:, s, :, R0:R0 + C],
                                  gat[:, s, :, C:C + 1].to_broadcast((EP, CT, C)),
                                  gat[:, s, :, R0 + C:R0 + C + 1].to_broadcast((EP, CT, C)), m[:, :, 1, :])
                        dve.sem_inc(s_gfree[0], 1)
                        dve.wait_ge(s_p1, 2 * i + s + 1)
                        c0.link(v.tensor_tensor(part_h[:, 1].rearrange("p d c t -> p t d c"), m[:, :, :, :],
                                                part_h[:, 0].rearrange("p d c t -> p t d c"), ALU.subtract))
                        dve.wait_ge(s_sfree[0], 2 * i + s + 1)
                        c0.link(stage_low(i, s, (0, 1)))
                        for d in range(2):
                            for q in range(2):
                                last = weigh(stat_h[:, s, 2 * d + q], part_h[:, q, d], i, s, d)
                        c0.link(last)
                        dve.sem_inc(s_stat[0], 1)
                        build_onehots(0, 2 * i + s, s, 2, (0, 1))
                    assert c0.n == 2 * STEPS0, c0.n

                sums_to(na, 0, "sums0")
                nodes0()

                layernorm_relu()
                dve.sem_inc(s_rows, 1)
                dve.sem_inc(s_gfree[1], 2)
                dve.sem_inc(s_ohfree[1], 4)
                dve.sem_inc(s_sfree[1], 2)
                STEPS1 = 11
                with dve.Fori(0, PAIRS) as i:
                    c1 = Chain(dve, s_chain[1], i * (2 * STEPS1))
                    for s in range(2):
                        dve.wait_ge(s_gat[1][s], (i + 1) * (2 * CT * 16))
                        messages1(c1, i, s, gat[:, s, :, R0:R0 + C])
                        split3(c1, m[:, :, 0, :])
                        dve.wait_ge(s_sfree[1], 2 * i + s + 1)
                        c1.link(stage_low(i, s, (0,)))
                        for q in range(3):
                            last = weigh(stat_m[:, s, q], part_b[:, q], i, s, 0)
                        c1.link(last)
                        dve.sem_inc(s_stat[1], 1)
                        build_onehots(1, 2 * i + s, s, 4, (0,))
                    assert c1.n == 2 * STEPS1, c1.n

                sums_to(na, 1, "sums1")
                nodes1()

                layernorm_relu()
                c.link(v.tensor_tensor(ncc[:, :, :], nh[:, :, :], over_channels(dis[:, :]), ALU.mult))
                c.link(v.tensor_scalar(rows2[:, :, 0, :], ncc[:, :, :], SCALE16, None, ALU.mult))
                c.link(v.scalar_tensor_tensor(rows2[:, :, 1, :], ncc[:, :, :], SCALE16, rows2[:, :, 0, :],
                                              ALU.mult, ALU.subtract))
                dve.sem_inc(s_rows, 1)
                dve.sem_inc(s_gfree[2], 2)
                dve.sem_inc(s_ohfree[2], 4)
                dve.sem_inc(s_sfree[2], 2)
                STEPS2 = 2
                with dve.Fori(0, PAIRS) as i:
                    c2 = Chain(dve, s_chain[2], i * (2 * STEPS2))
                    for s in range(2):
                        dve.wait_ge(s_gat[2][s], (i + 1) * (CT * 16))
                        dve.wait_ge(s_sfree[2], 2 * i + s + 1)
                        c2.link(stage_low(i, s, (1,)))
                        halves = gat[:, s, :, 0:C].bitcast(F16)
                        for q in range(2):
                            last = weigh(stat_h[:, s, q], halves[:, :, q * C:(q + 1) * C].rearrange("p t c -> p c t"), i, s, 1)
                        c2.link(last)
                        dve.sem_inc(s_stat[2], 1)
                        dve.sem_inc(s_gfree[2], 1)
                        build_onehots(2, 2 * i + s, s, 4, (1,))
                    assert c2.n == 2 * STEPS2, c2.n

                sums_to(na, 2, "sums2")
                nodes2(1.0 / SCALE16)

                rows_3()
                dve.sem_inc(s_gfree[3], 2)
                dve.sem_inc(s_ohfree[3], 2)
                dve.sem_inc(s_sfree[3], 2)
                dve.sem_inc(s_mfree[3], 2)
                STEPS3 = 2 * HALF + 7

                def weigh_messages(c, i, s, chunk):
                    link = c.link
                    link(v.tensor_tensor(m[:, :, 1, :], m[:, :, 0, :], gat[:, s, :, C:2 * C], ALU.add))
                    dve.sem_inc(s_gfree[3], 1)
                    split3(c, m[:, :, 1, :])
                    dve.wait_ge(s_sfree[3], chunk + 1)
                    link(stage_low(i, s, (1,)))
                    for q in range(3):
                        last = weigh(stat_m[:, s, q], part_b[:, q], i, s, 1)
                    link(last)
                    dve.sem_inc(s_stat[3], 1)

                def finish_and_begin(c, i, s, chunk, i_next):
                    weigh_messages(c, i, s, chunk)
                    dve.wait_ge(s_gat[3][1 - s], (i_next + 1) * (CT * 16))
                    for g in range(HALF):
                        onehots(3, chunk, s, g, 2, 2, (1,))
                        use_weights(c.link, 1 - s, chunk + 1, g, 2)

                dve.wait_ge(s_gat[3][0], CT * 16)
                for j in range(HALF):
                    use_weights(c.link, 0, 0, j, 2)
                with dve.Fori(0, PAIRS - 1) as i:
                    c3 = Chain(dve, s_chain[3], i * (2 * STEPS3))
                    finish_and_begin(c3, i, 0, 2 * i, i)
                    finish_and_begin(c3, i, 1, 2 * i + 1, i + 1)
                    assert c3.n == 2 * STEPS3, c3.n
                finish_and_begin(c, PAIRS - 1, 0, CHUNKS - 2, PAIRS - 1)
                weigh_messages(c, PAIRS - 1, 1, CHUNKS - 1)
                for g in range(HALF):
                    onehots(3, CHUNKS - 1, 1, g, 2, 2, (1,))

                sums_to(na, 3, "sums3")
                nodes3()

            def sorted_order():
                dve.wait_ge(s_node, step["within"])
                c.link(v.tensor_copy(pos[:, 0, :], p_b[0:NP, G:2 * G]))
                c.link(v.tensor_tensor_scan(pos[:, 1, :], ones[0:NP, 0:G], pos[:, 0, :], 0.0, ALU.mult, ALU.add))
                c.link(v.tensor_tensor(pos[:, 1, :], pos[:, 1, :], pos[:, 0, :], ALU.subtract))
                c.link(v.tensor_tensor(pos[:, 0, :], p_b[0:NP, 0:G], pos[:, 1, :], ALU.add))
                c.link(v.tensor_tensor(pos[:, 1, :], pos[:, 0, :], degs[:, 1, :], ALU.subtract))
                v.tensor_scalar(has[:, :], degs[:, 1, :], 0.5, None, ALU.is_gt)
                c.link(v.tensor_copy(spare[:, :], spare_i[:, :]))
                v.tensor_scalar(last_edge[:, :], pos[:, 0, :], -1.0, 0.0, ALU.add, ALU.max)
                c.link(v.tensor_tensor(pos[:, 1, :], pos[:, 1, :], spare[:, :], ALU.subtract))
                c.link(v.tensor_tensor(pos[:, 1, :], pos[:, 1, :], has[:, :], ALU.mult))
                c.link(v.tensor_tensor(first_edge[:, :], pos[:, 1, :], spare[:, :], ALU.add))
                v.tensor_tensor(oh_place[:, :], dig_l[:, 0:1].to_broadcast((EP, NP)), iota_lo[0:EP, 0:NP], ALU.is_equal)
                c.link(v.tensor_tensor(oh_group[:, :], dig_l[:, 1:2].to_broadcast((EP, G)), iota_lo[0:EP, 0:G],
                                       ALU.is_equal))
                dve.sem_inc(s_pos, 1)
                mask_high(0)
                c.link(v.tensor_copy(row_lo[:, :], place_i[:, :]))
                c.link(v.tensor_scalar(row_high[:, :], row_lo[:, 0:1], -(C - 1) / 2.0, 1.0 / C, ALU.add, ALU.mult))
                c.link(v.tensor_scalar(row_high[:, :], row_high[:, :], MAGIC, None, ALU.add))
                c.link(v.tensor_scalar(row_high[:, :], row_high[:, :], -MAGIC, None, ALU.add))
                c.link(v.scalar_tensor_tensor(row_c[:, :], row_high[:, :], -float(C), row_lo[:, 0:1], ALU.mult, ALU.add))
                v.tensor_scalar(fold_z[:, 0:C], iota_lo[0:NP, 0:C], row_c[:, 0:1], None, ALU.is_equal)
                c.link(v.tensor_scalar(fold[:, :], iota_lo[0:NP, 0:C], row_c[:, 0:1], None, ALU.is_equal))

                def split_table(rows):
                    by_lo = rows[:, :, :].rearrange("p (h b) c -> p b h c", b=B)
                    high, low = (tabs[:, :, q, :].rearrange("p b (h c) -> p b h c", c=C) for q in range(2))
                    for b in range(B):
                        last = v.tensor_scalar(high[:, b], by_lo[:, b], SCALE16, None, ALU.mult)
                    c.link(last)
                    for b in range(B):
                        last = v.scalar_tensor_tensor(low[:, b], by_lo[:, b], SCALE16, high[:, b], ALU.mult, ALU.subtract)
                    c.link(last)

                def columns(n, i, s, chunk, blocks):
                    if blocks[0] == 0:
                        dve.wait_ge(s_lob[n][s], (i + 1) * 16)
                        dve.wait_ge(s_picked[n], (chunk + 1) * UN[n])
                    for b in blocks:
                        last = v.tensor_scalar(oht[n][:, s, b, :], lob[n][:, s, 0, :], row_lo[:, b:b + 1], None,
                                               ALU.is_equal)
                    if blocks[-1] == B - 1:
                        last.then_inc(s_oht[n], 1)

                def keep_high(n, s, chunk, u):
                    o, tiles = UNITS[n][u]
                    dve.wait_ge(s_picked[n], chunk * UN[n] + (2 * UN[n] + u + 1))
                    dve.wait_ge(s_folded[n], chunk * UN[n] + (u + 1))
                    v.scalar_tensor_tensor(unit_masked(n, u, s),
                                           lob[n][:, s, 1, o * EP:(o + tiles) * EP].unsqueeze(1)
                                           .to_broadcast((NP, 2, tiles * EP)),
                                           row_high[:, 0:1], unit_picked(n, u, s), ALU.is_equal, ALU.mult
                                           ).then_inc(s_masked[n], 1)

                def free_rings(n):
                    dve.sem_inc(s_picked[n], 2 * UN[n])
                    dve.sem_inc(s_masked[n], RING[n])
                    dve.sem_inc(s_folded[n], RING[n])

                def spread_rows(n, channels):
                    for b in range(BLOCKS):
                        use = n * BLOCKS + b
                        dve.wait_ge(s_z[use % 2], 16 * (use // 2 + 1))
                        if b == 0:
                            dve.wait_ge(s_first, 16 * (n + 1))
                            c.link(v.tensor_copy(zb[0:EP, use % 2, 0, :], first_rows[:, :]))
                        at = slice(b * BT, (b + 1) * BT)
                        for f in range(channels):
                            before = max(b * BT - 1, 0)
                            if f < C:
                                to, start = wide[:, at, f], wide[:, before, f:f + 1]
                            else:
                                to, start = rd[:, at], rd[:, before:before + 1]
                            last = v.tensor_tensor_scan(to, same[:, at], zb[0:EP, use % 2, :, f],
                                                        start if b else 0.0, ALU.mult, ALU.add)
                        c.link(last)
                        dve.sem_inc(s_zfree, 1)
                        if n == 0:
                            dve.sem_inc(s_xd, 1)

                def scan_block(link, o):
                    at = bass.ds(o * BT, BT)
                    for f in range(C):
                        last = v.tensor_tensor_scan(wide[:, at, f], same[:, at], wide[:, at, f],
                                                    tail[:, f:f + 1], ALU.mult, ALU.add)
                    link(last)
                    link(v.tensor_scalar(tail[:, :], wide[:, bass.ds(o * BT + BT - 1, 1), :].rearrange("p a c -> p (a c)"),
                                         0.0, None, ALU.add))
                    dve.sem_inc(s_blk, 1)

                def carried_sums(k, what):
                    c.link(v.tensor_scalar(tail[:, :], tail[:, :], cont[:, 0:1], None, ALU.mult))
                    v.tensor_tensor(crhs[:, :, :], oh_group[:, :].unsqueeze(2).to_broadcast((EP, G, C)),
                                    tail[:, :].unsqueeze(1).to_broadcast((EP, G, C)), ALU.mult).then_inc(s_crhs, 1)
                    dve.wait_ge(s_last, 16 * G * (k + 1))
                    c.link(v.tensor_tensor(na[:, :, :], last_rows[:, :, :], over_channels(has[:, :]), ALU.mult))
                    dve.wait_ge(s_node, step[what])
                    c.link(v.tensor_tensor(nb[:, :, :], na[:, :, :],
                                           p_b[0:NP, 0:G * C].rearrange("p (g c) -> p g c", g=G), ALU.add))

                dve.wait_ge(s_turned, 4)
                dve.sem_inc(s_gfree[0], 2)
                dve.sem_inc(s_ohfree[0], 4)
                dve.sem_inc(s_sfree[0], 2)
                dve.sem_inc(s_mfree[0], 2)
                spread_rows(0, C + 1)
                dve.wait_ge(s_w, 16 * W_LOADS)
                c.link(v.memset(tail[:, :], 0.0))
                STEPS0 = 16
                F0 = BP * 2 * STEPS0 + 2
                with dve.Fori(0, BLOCKS) as o:
                    with dve.Fori(0, BP) as k:
                        i = o * BP + k
                        c0 = Chain(dve, s_chain[0], o * F0 + k * (2 * STEPS0))
                        for s in range(2):
                            at = bass.ds(i * (2 * CT) + s * CT, CT)
                            stage_low(i, s, (0,)).then_inc(s_low[0], 1)
                            dve.wait_ge(s_low[0], 2 * i + s + 1)
                            messages0(c0, s, 2 * i + s, packed[:, s, :, 0, :], packed[:, s, :, 1, :],
                                      rs[:, s, :].unsqueeze(2).to_broadcast((EP, CT, C)),
                                      rd[:, at].unsqueeze(2).to_broadcast((EP, CT, C)), wide[:, at, :],
                                      onehot_tile=lambda t: onehot_tile(0, 2 * i + s, s, t))
                            dve.wait_ge(s_p1, 2 * i + s + 1)
                            c0.link(v.tensor_tensor(part_h[:, 1, 0].rearrange("p c t -> p t c"), m[:, :, 0, :],
                                                    part_h[:, 0, 0].rearrange("p c t -> p t c"), ALU.subtract))
                            dve.wait_ge(s_sfree[0], 2 * i + s + 1)
                            for q in range(2):
                                last = weigh(stat_h[:, s, q], part_h[:, q, 0], i, s, 0)
                            c0.link(last)
                            dve.sem_inc(s_stat[0], 1)
                        assert c0.n == 2 * STEPS0, c0.n
                    cb = Chain(dve, s_chain[0], o * F0 + BP * (2 * STEPS0))
                    scan_block(cb.link, o)
                    assert BP * 2 * STEPS0 + cb.n == F0
                carried_sums(0, "carry0")
                c.link(v.tensor_tensor(by_high(na), layer_sums(0, "sums0"), by_high(nb), ALU.add))
                nodes0()

                layernorm_relu()
                c.link(v.tensor_copy(rows0[:, :, 0:C], nh[:, :, :]))
                split_table(nh)
                dve.sem_inc(s_rows, 1)
                free_rings(1)
                dve.sem_inc(s_gfree[1], 2)
                columns(1, 0, 0, 0, range(B))
                keep_high(1, 0, 0, 0)
                spread_rows(1, C)
                dve.sem_inc(s_ohs, 2 * SHARED)
                dve.sem_inc(s_ohfree[1], 4)
                dve.sem_inc(s_sfree[1], 2)
                STEPS1 = 10

                def chunk1(c, i, s, chunk, i_next, more=True):
                    tiles = {2: (0,), 3: (1,), 4: (2, 3), 5: (4,), 6: (5,), 7: (6,), 8: (7,)}

                    def meanwhile(k):
                        for t in tiles.get(k, ()):
                            onehot_tile(1, chunk, s, t)

                    dve.wait_ge(s_ohs, (chunk + 1) * SHARED)
                    stage_low(i, s, (0,)).then_inc(s_low[1], 1)
                    dve.wait_ge(s_low[1], chunk + 1)
                    if more:
                        columns(1, i_next, 1 - s, chunk + 1, range(B))
                    dve.wait_ge(s_gat[1][s], (i + 1) * ((CT - PT[1]) * 16))
                    dve.wait_ge(s_put_in[1], chunk + 3)
                    messages1(c, i, s, wide[:, bass.ds(i * (2 * CT) + s * CT, CT), :], meanwhile)
                    split3(c, m[:, :, 0, :], meanwhile)
                    if more:
                        keep_high(1, 1 - s, chunk + 1, 0)
                    dve.wait_ge(s_sfree[1], chunk + 1)
                    for q in range(3):
                        last = weigh(stat_m[:, s, q], part_b[:, q], i, s, 0)
                    c.link(last)
                    dve.sem_inc(s_stat[1], 1)

                with dve.Fori(0, PAIRS - 1) as i:
                    c1 = Chain(dve, s_chain[1], i * (2 * STEPS1))
                    chunk1(c1, i, 0, 2 * i, i)
                    chunk1(c1, i, 1, 2 * i + 1, i + 1)
                    assert c1.n == 2 * STEPS1, c1.n
                chunk1(c, PAIRS - 1, 0, CHUNKS - 2, PAIRS - 1)
                chunk1(c, PAIRS - 1, 1, CHUNKS - 1, None, more=False)
                sums_to(na, 1, "sums1")
                nodes1()

                layernorm_relu()
                c.link(v.tensor_tensor(ncc[:, :, :], nh[:, :, :], over_channels(dis[:, :]), ALU.mult))
                c.link(v.memset(tail[:, :], 0.0))
                split_table(ncc)
                dve.sem_inc(s_rows, 1)
                free_rings(2)

                def chunk2(s, chunk, i_next, more=True):
                    keep_high(2, s, chunk, 0)
                    if more:
                        columns(2, i_next, 1 - s, chunk + 1, (0, 1))
                    keep_high(2, s, chunk, 1)
                    if more:
                        columns(2, i_next, 1 - s, chunk + 1, (2, 3))
                    keep_high(2, s, chunk, 2)

                def pair2(i):
                    chunk2(0, 2 * i, i)
                    chunk2(1, 2 * i + 1, i + 1)

                def scan2(o):
                    dve.wait_ge(s_gfree[2], o * (2 * BP) + (2 * BP + 2))
                    dve.wait_ge(s_put_in[2], o * (2 * BP) + (2 * BP + 2))
                    scan_block(Chain(dve, s_chain[2], o * 2).link, o)

                columns(2, 0, 0, 0, range(B))
                with dve.Fori(0, LAG) as i:
                    pair2(i)
                with dve.Fori(0, BLOCKS - 1) as o:
                    with dve.Fori(0, BP) as k:
                        pair2(o * BP + k + LAG)
                    scan2(o)
                with dve.Fori((BLOCKS - 1) * BP + LAG, PAIRS - 1) as i:
                    pair2(i)
                chunk2(0, CHUNKS - 2, PAIRS - 1)
                chunk2(1, CHUNKS - 1, None, more=False)
                scan2(BLOCKS - 1)
                carried_sums(1, "carry2")
                c.link(v.tensor_copy(na[:, :, :], nb[:, :, :]))
                nodes2(1.0)

                rows_3(lambda: split_table(nh))
                c.link(v.memset(tail[:, :], 0.0))
                dve.sem_inc(s_gfree[3], 2)
                dve.sem_inc(s_mfree[3], 4)
                dve.sem_inc(s_picked[3], 2)
                dve.sem_inc(s_masked[3], 1)
                dve.sem_inc(s_folded[3], 2)
                dve.sem_inc(s_put_in[3], 1)
                STEPS3 = 2 * HALF + 1
                F3 = BP * 2 * STEPS3 + 2

                def keep_high3(s, chunk):
                    dve.wait_ge(s_picked[3], chunk + 3)
                    dve.wait_ge(s_folded[3], chunk + 1)
                    v.scalar_tensor_tensor(masked3[:, s, :], lob[3][:, s, 1, :], row_high[:, 0:1],
                                           p_pick[0:NP, 0:PT[3] * EP], ALU.is_equal, ALU.mult).then_inc(s_masked[3], 1)

                def chunk3(c, i, s, chunk, i_next, more=True):
                    weighted = [t.rearrange("p t a c -> p (t a c)").rearrange("p (u i o) -> p u i o", u=2, i=C)
                                for t in (pr[:, :, :, :], ab[:, :, :, :], mt[:, :, :, :])]
                    rows = gat[:, s, :, 0:C].rearrange("p (u j) c -> p j u c", u=2)
                    sums = m[:, :, 0, :].rearrange("p (u j) c -> p j u c", u=2)

                    def multiply(j):
                        dve.wait_ge(s_mlp[3], chunk * HALF + j + 1)
                        if j >= 3:
                            c.wait(back=2)
                        c.mark(v.tensor_tensor(weighted[j % 3],
                                               p_w[j % 4][0:EP, :].rearrange("p (u i o) -> p u i o", u=2, i=C),
                                               rows[:, j].unsqueeze(3).to_broadcast((EP, 2, C, C)), ALU.mult))

                    def add_up(j):
                        dve.sem_inc(s_mfree[3], 1)
                        c.mark(v.tensor_reduce(sums[:, j], weighted[j % 3].rearrange("p u i o -> p u o i"), AX_X, ALU.add))

                    dve.wait_ge(s_gat[3][s], (i + 1) * ((CT - PT[3]) * 16))
                    dve.wait_ge(s_put_in[3], chunk + 2)
                    multiply(0)
                    for j in range(1, HALF):
                        multiply(j)
                        c.wait(back=min(j, 2))
                        add_up(j - 1)
                        if more and j == 1:
                            columns(3, i_next, 1 - s, chunk + 1, range(B))
                        if more and j == HALF // 2:
                            keep_high3(1 - s, chunk + 1)
                    c.wait()
                    add_up(HALF - 1)
                    c.wait()
                    at = bass.ds(i * (2 * CT) + s * CT, CT)
                    c.link(v.tensor_tensor(wide[:, at, :], m[:, :, 0, :], gat[:, s, :, C:2 * C], ALU.add))
                    dve.sem_inc(s_gfree[3], 1)

                columns(3, 0, 0, 0, range(B))
                keep_high3(0, 0)
                with dve.Fori(0, BLOCKS - 1) as o:
                    with dve.Fori(0, BP) as k:
                        i = o * BP + k
                        c3 = Chain(dve, s_chain[3], o * F3 + k * (2 * STEPS3))
                        chunk3(c3, i, 0, 2 * i, i)
                        chunk3(c3, i, 1, 2 * i + 1, i + 1)
                        assert c3.n == 2 * STEPS3, c3.n
                    cb = Chain(dve, s_chain[3], o * F3 + F3 - 2)
                    scan_block(cb.link, o)
                i0 = (BLOCKS - 1) * BP
                with dve.Fori(0, BP - 1) as k:
                    c3 = Chain(dve, s_chain[3], k * (2 * STEPS3) + (BLOCKS - 1) * F3)
                    chunk3(c3, k + i0, 0, 2 * (k + i0), k + i0)
                    chunk3(c3, k + i0, 1, 2 * (k + i0) + 1, k + (i0 + 1))
                chunk3(c, PAIRS - 1, 0, CHUNKS - 2, PAIRS - 1)
                chunk3(c, PAIRS - 1, 1, CHUNKS - 1, None, more=False)
                scan_block(c.link, BLOCKS - 1)
                carried_sums(2, "carry3")
                c.link(v.tensor_copy(na[:, :, :], nb[:, :, :]))
                nodes3()

            steps_before, roots_before = c.n, roots[0]
            dve.wait_ge(s_flag, 1)
            is_sorted = dve.value_load(flag[0:1, 0:1], min_val=0, max_val=1)
            with dve.If(is_sorted):
                step = sorted_step
                sorted_order()
            c.n, roots[0] = steps_before, roots_before
            with dve.Else():
                step = any_step
                any_order()

        @block.tensor
        def _(pe):
            te = nc.tensor
            acc = p_acc[0:NP, 0:LO]

            def clear(last=False):
                return te.matmul(acc, zeros[0:1, 0:NP], zeros[0:1, :], start=not last, stop=last,
                                 skip_group_check=True)

            def turn_sums(n):
                pe.wait_ge(s_accs, n + 1)
                for b in range(B):
                    last = te.transpose(p_a[0:NP, b * NP:(b + 1) * NP], accs[:, b * NP:(b + 1) * NP],
                                        identity[0:NP, 0:NP])
                last.then_inc(s_node, 1)

            def scatter_group(n, chunk, s, g, og, ring, terms, masks, shared=False):
                if shared and g >= SG:
                    pe.wait_ge(s_ohs, chunk * SHARED + (2 * SHARED + g - SG + 1))
                else:
                    pe.wait_ge(s_oh[n], chunk * (SG if shared else CT // og) + g + 1)
                for k in range(og):
                    for d, q in terms:
                        last = te.matmul(acc, masks[:, s, q, :, g * og + k], onehot_row(ring, g, d, k),
                                         start=False, stop=False, skip_group_check=True)
                last.then_inc(s_ohfree[n], 1)

            def masks_used(n):
                te.matmul(acc, zeros[0:1, 0:NP], zeros[0:1, :], start=False, stop=False,
                          skip_group_check=True).then_inc(s_sfree[n], 1)

            def scatter(n, chunk, s, ring, terms, masks, shared=False):
                pe.wait_ge(s_stat[n], chunk + 1)
                for g in range(CT // OG):
                    scatter_group(n, chunk, s, g, OG, ring, terms, masks, shared)
                masks_used(n)

            pe.wait_ge(s_zero, 1)
            te.matmul(p_a[0:NP, 0:2 * G], zeros[0:1, 0:NP], zeros[0:1, 0:2 * G], start=True, stop=False,
                      skip_group_check=True)
            with pe.Fori(0, TILES // DC // DU) as i:
                for s in range(DU):
                    pe.wait_ge(s_cnt_oh, DU * i + s + 1)
                    a, b = digits(s % 2)
                    for d in range(2):
                        for t in range(DC):
                            last = te.matmul(p_a[0:NP, d * G:(d + 1) * G], a[:, d, :, t], b[:, d, :, t],
                                             start=False, stop=False, skip_group_check=True)
                    last.then_inc(s_cnt_mm, 1)
            te.matmul(p_a[0:NP, 0:2 * G], zeros[0:1, 0:NP], zeros[0:1, 0:2 * G], start=False, stop=True,
                      skip_group_check=True).then_inc(s_node, 1)

            pe.wait_ge(s_viol, 1)
            pe.wait_ge(s_const, 9)
            te.matmul(p_c[0:1, 0:1], viol_f[:, :], ones[0:EP, 0:1], start=True, stop=True).then_inc(s_node, 1)
            pe.wait_ge(s_deg, 1)
            te.matmul(p_b[0:NP, 0:G], upper[:, :], degs[:, 1, :], start=True, stop=True)
            te.matmul(p_b[0:NP, G:2 * G], ones[0:NP, :], degs[:, 1, :], start=True, stop=True).then_inc(s_node, 1)

            def mlp0(s, i2):
                pe.wait_ge(s_packed, i2 + 1)
                for q in range(4):
                    last = te.transpose(p_xt[:, q * EP:(q + 1) * EP],
                                        packed[:, s, 4 * q:4 * q + 4, :, :].rearrange("p t d c -> p (t d c)"),
                                        identity[0:EP, 0:EP])
                last.then_inc(s_xt[0], 1)
                pe.wait_ge(s_xts[0], i2 + 1)
                for j in range(4):
                    if j >= 2:
                        pe.wait_ge(s_hs[0], i2 * 4 + j - 1)
                    te.matmul(p_hid[j % 2][:, 0:4 * EP], w1_0[:, j, :],
                              xt[:, :, :].rearrange("p q e -> p (q e)"), start=True, stop=True).then_inc(s_hp[0], 1)
                pe.wait_ge(s_mfree[0], i2 + 1)
                for j in range(4):
                    pe.wait_ge(s_hs[0], i2 * 4 + j + 1)
                    for q in range(4):
                        t = 4 * q + j
                        last = te.matmul(p_ab[s][0:EP, t * 2 * C:(t + 1) * 2 * C], hid[:, j, q * EP:(q + 1) * EP],
                                         w2_0[:, :], start=True, stop=True)
                last.then_inc(s_mlp[0], 1)

            def layer0(ring, terms):
                clear()
                pe.wait_ge(s_w, 16 * W_LOADS)
                mlp0(0, 0)
                mlp0(1, 1)
                with pe.Fori(0, PAIRS - 1) as i:
                    for s in range(2):
                        scatter(0, 2 * i + s, s, ring, terms, stat_h)
                        mlp0(s, 2 * i + s + 2)
                scatter(0, CHUNKS - 2, 0, ring, terms, stat_h)
                scatter(0, CHUNKS - 1, 1, ring, terms, stat_h)
                clear(last=True).then_inc(s_done, 1)

            def scatter_layer(n, ring, terms, masks):
                clear()
                with pe.Fori(0, PAIRS) as i:
                    for s in range(2):
                        scatter(n, 2 * i + s, s, ring, terms, masks)
                clear(last=True).then_inc(s_done, 1)
                turn_sums(n)

            def turn_digits():
                banks = (p_c, p_d, p_e, p_acc)
                for k in range(4):
                    what = lo_s[:, :] if k < 2 else t_f[:, 0, :]
                    for j in range(4):
                        u = (k % 2) * 4 + j
                        last = te.transpose(banks[k][0:DT, j * EP:(j + 1) * EP], what[:, u * DT:(u + 1) * DT],
                                            identity[0:EP, 0:EP])
                    last.then_inc(s_turned, 1)
                pe.wait_ge(s_dig, 4)

            def pick(n, s, chunk, u):
                o, tiles = UNITS[n][u]
                if u == 0:
                    pe.wait_ge(s_oht[n], chunk + 1)
                pe.wait_ge(s_masked[n], chunk * UN[n] + (u + 1))
                for q in range(2):
                    for b in range(B):
                        last = te.matmul(unit_picked(n, u, s)[:, q, :], tabs[:, b, q, :],
                                         oht[n][:, s, b, o * EP:(o + tiles) * EP], start=b == 0, stop=b == B - 1)
                last.then_inc(s_picked[n], 1)

            def fold_unit(n, s, chunk, u):
                o, tiles = UNITS[n][u]
                pe.wait_ge(s_masked[n], chunk * UN[n] + (RING[n] + u + 1))
                if u == 0:
                    pe.wait_ge(s_put_in[n], chunk + 1)
                masked = unit_masked(n, u, s)
                for k in range(tiles):
                    for q in range(2):
                        last = te.matmul(p_folded[s][0:EP, (o + k) * C:(o + k + 1) * C],
                                         masked[:, q, k * EP:(k + 1) * EP], fold[:, :], start=q == 0, stop=q == 1)
                last.then_inc(s_folded[n], 1)

            def layer1():
                clear()
                pe.wait_ge(s_rows, 2)
                for s in range(2):
                    pick(1, s, s, 0)
                    fold_unit(1, s, s, 0)
                terms = ((0, 0), (0, 1), (0, 2))
                with pe.Fori(0, PAIRS - 1) as i:
                    for s in range(2):
                        chunk = 2 * i + s
                        pe.wait_ge(s_stat[1], chunk + 1)
                        for g in range(CT // OG):
                            scatter_group(1, chunk, s, g, OG, 4, terms, stat_m, shared=True)
                            if g == 1:
                                pick(1, s, chunk + 2, 0)
                        masks_used(1)
                        fold_unit(1, s, chunk + 2, 0)
                scatter(1, CHUNKS - 2, 0, 4, terms, stat_m, shared=True)
                scatter(1, CHUNKS - 1, 1, 4, terms, stat_m, shared=True)
                clear(last=True).then_inc(s_done, 1)
                turn_sums(1)

            def layer2():
                pe.wait_ge(s_rows, 3)

                def chunk2(s, chunk, more=True):
                    pick(2, s, chunk, 1)
                    fold_unit(2, s, chunk, 0)
                    pick(2, s, chunk, 2)
                    fold_unit(2, s, chunk, 1)
                    if more:
                        pick(2, 1 - s, chunk + 1, 0)
                    fold_unit(2, s, chunk, 2)

                pick(2, 0, 0, 0)
                with pe.Fori(0, PAIRS - 1) as i:
                    for s in range(2):
                        chunk2(s, 2 * i + s)
                chunk2(0, CHUNKS - 2)
                chunk2(1, CHUNKS - 1, more=False)

            def carry(k):
                pe.wait_ge(s_crhs, k + 1)
                te.matmul(p_b[0:NP, 0:G * C], oh_place[:, :], crhs[:, :, :].rearrange("p g c -> p (g c)"),
                          start=True, stop=True).then_inc(s_node, 1)

            def turn_nodes(rows, before):
                pe.wait_ge(s_feat, before)
                for q in range(H):
                    if q >= 2:
                        pe.wait_ge(s_feat, before + q - 1)
                    for b in range(B):
                        last = te.transpose(p_turned[q % 2][0:C, b * NP:(b + 1) * NP], rows[:, q * B + b, :],
                                            identity[0:NP, 0:NP])
                    last.then_inc(s_node, 1)

            def products2():
                turn_nodes(na, 1)
                for q in range(H):
                    pe.wait_ge(s_feat, max(1 + q + 1, 1 + H + q - 1))
                    te.matmul(p_features[q % 2][0:PC, 0:LO], wg[:, :], turned[:, q * LO:(q + 1) * LO],
                              start=True, stop=True).then_inc(s_node, 1)
                for q in range(H):
                    pe.wait_ge(s_feat, 1 + H + q + 1)
                    if q >= 2:
                        pe.wait_ge(s_relu, q - 1)
                    te.matmul(p_hidden2[q % 2][0:H2, 0:LO], w1_2[:, :], features[:, q * LO:(q + 1) * LO],
                              start=True, stop=True).then_inc(s_node, 1)
                for g in range(G):
                    pe.wait_ge(s_relu, g // B + 1)
                    last = te.matmul(p_c[0:NP, g * C:(g + 1) * C], hidden[:, g * NP:(g + 1) * NP], w2_2[:, :],
                                     start=True, stop=True)
                last.then_inc(s_node, 1)

            def rows_3():
                before = 1 + 2 * H + 1
                turn_nodes(nh, before)
                for g in range(G):
                    pe.wait_ge(s_feat, before + g // B + 1)
                    k = g // (G // 2)
                    at = g % (G // 2) * 2 * C
                    last = te.matmul(p_rooted[k][0:NP, at:at + 2 * C], turned[:, g * NP:(g + 1) * NP],
                                     zr_3[:, :, :].rearrange("i r o -> i (r o)"), start=True, stop=True)
                    if g % (G // 2) == G // 2 - 1:
                        last.then_inc(s_node, 1)
                pe.wait_ge(s_feat, before + H + 2)

            def turn_attributes(i, s):
                pe.wait_ge(s_ea[s], (i + 1) * 16)
                for u in range(2):
                    last = te.transpose(p_xt[:, u * EP:(u + 1) * EP],
                                        ea[:, s, u * HALF:(u + 1) * HALF, :].rearrange("p t c -> p (t c)"),
                                        identity[0:EP, 0:EP])
                last.then_inc(s_xt[3], 1)

            def hidden_sums(jj):
                for k in range(2):
                    last = te.matmul(p_hid[jj % 2][:, k * 2 * EP:(k + 1) * 2 * EP], w1z_3[:, 2 * jj + k, :],
                                     xt[:, 0:2, :].rearrange("p u e -> p (u e)"), start=True, stop=True)
                last.then_inc(s_hp[3], 1)

            def hidden3(i, s, i2):
                turn_attributes(i, s)
                pe.wait_ge(s_xts[3], i2 + 1)
                for jj in range(4):
                    if jj >= 2:
                        pe.wait_ge(s_hs[3], i2 * 4 + jj - 1)
                    hidden_sums(jj)

            def weights3(i2, j, banks):
                pe.wait_ge(s_hs[3], i2 * 4 + j // 2 + 1)
                pe.wait_ge(s_mfree[3], i2 * HALF + j + 1)
                for u in range(2):
                    at = ((j % 2) * 2 + u) * EP
                    last = te.matmul(p_w[j % banks][0:EP, u * OO:(u + 1) * OO], hid[:, j // 2, at:at + EP],
                                     w2s_3[:, :], start=True, stop=True)
                last.then_inc(s_mlp[3], 1)

            def any_order():
                layer0(2, ((0, 0), (0, 1), (1, 2), (1, 3)))
                turn_sums(0)
                scatter_layer(1, 4, ((0, 0), (0, 1), (0, 2)), stat_m)
                scatter_layer(2, 4, ((1, 0), (1, 1)), stat_h)
                products2()
                rows_3()
                clear()

                def scatter_and_weights(chunk, s, i_next):
                    hidden3(i_next, 1 - s, chunk + 1)
                    pe.wait_ge(s_stat[3], chunk + 1)
                    for g in range(HALF):
                        scatter_group(3, chunk, s, g, 2, 2, terms3, stat_m)
                        weights3(chunk + 1, g, 2)
                    masks_used(3)

                terms3 = ((1, 0), (1, 1), (1, 2))
                pe.sem_inc(s_xt[3], 2)
                hidden3(0, 0, 0)
                for j in range(HALF):
                    weights3(0, j, 2)
                with pe.Fori(0, PAIRS - 1) as i:
                    scatter_and_weights(2 * i, 0, i)
                    scatter_and_weights(2 * i + 1, 1, i + 1)
                scatter_and_weights(CHUNKS - 2, 0, PAIRS - 1)
                pe.wait_ge(s_stat[3], CHUNKS)
                for g in range(HALF):
                    scatter_group(3, CHUNKS - 1, 1, g, 2, 2, terms3, stat_m)
                masks_used(3)
                clear(last=True).then_inc(s_done, 1)
                turn_sums(3)

            def pick3(s, chunk):
                pe.wait_ge(s_oht[3], chunk + 1)
                pe.wait_ge(s_masked[3], chunk + 1)
                pe.wait_ge(s_put_in[3], chunk + 1)
                for k in range(2 * B):
                    last = te.matmul(p_pick[0:NP, 0:PT[3] * EP], tabs[:, k % B, k // B, :], oht[3][:, s, k % B, :],
                                     start=k == 0, stop=k == 2 * B - 1)
                last.then_inc(s_picked[3], 1)

            def fold3(s, chunk):
                pe.wait_ge(s_masked[3], chunk + 2)
                for k in range(PT[3]):
                    last = te.matmul(p_folded3[:, k * 2 * C:(k + 1) * 2 * C], masked3[:, s, k * EP:(k + 1) * EP],
                                     fold_z[:, :], start=True, stop=True)
                last.then_inc(s_folded[3], 1)

            def sorted_order():
                turn_digits()
                layer0(4, ((0, 0), (0, 1)))
                carry(0)
                turn_sums(0)
                layer1()
                layer2()
                carry(1)
                products2()
                rows_3()

                def chunk3(chunk, i_next, s_next):
                    turn_attributes(i_next, s_next)
                    for jj in range(4):
                        weights3(chunk, 2 * jj, 4)
                        weights3(chunk, 2 * jj + 1, 4)
                        if jj == 0:
                            pe.wait_ge(s_xts[3], chunk + 2)
                        pe.wait_ge(s_hs[3], chunk * 4 + 4 + jj - 1)
                        hidden_sums(jj)
                        if jj == 1:
                            pick3(s_next, chunk + 1)
                    fold3(s_next, chunk + 1)

                pe.sem_inc(s_xt[3], 2)
                hidden3(0, 0, 0)
                pe.wait_ge(s_rows, 4)
                pick3(0, 0)
                fold3(0, 0)
                with pe.Fori(0, PAIRS - 1) as i:
                    chunk3(2 * i, i, 1)
                    chunk3(2 * i + 1, i + 1, 0)
                chunk3(CHUNKS - 2, PAIRS - 1, 1)
                for j in range(HALF):
                    weights3(CHUNKS - 1, j, 4)
                carry(2)

            pe.wait_ge(s_flag, 1)
            is_sorted = pe.value_load(flag[0:1, 0:1], min_val=0, max_val=1)
            with pe.If(is_sorted):
                sorted_order()
            with pe.Else():
                any_order()


W_LOADS = 1 + 4 * 3 + 2 * 3 + 5 + 8 + 4 + H


_INS = ["x", "src", "dst", "edge_attr_16", "edge_weight", "L0_gnn_W1", "L0_gnn_b1", "L0_gnn_W2", "L0_gnn_b2",
        "L2_gnn_W_gcn", "L2_gnn_W1", "L2_gnn_b1", "L2_gnn_W2", "L2_gnn_b2",
        "L3_gnn_W1", "L3_gnn_b1", "L3_gnn_W2", "L3_gnn_b2", "L3_gnn_root"]
_TURNED = {"L0_gnn_W1", "L0_gnn_W2", "L2_gnn_W_gcn", "L2_gnn_W1", "L2_gnn_W2"}


def kernel(**inputs):
    import numpy as _np
    import concourse.bacc as _bacc
    from concourse import mybir as _mybir
    from concourse.bass_utils import run_bass_kernel_spmd as _run

    nc = _bacc.Bacc("TRN2", target_bir_lowering=False, num_devices=1)
    arrays, args = {}, []
    for name in _INS:
        a = _np.asarray(inputs[name])
        a = _np.ascontiguousarray(a.T if name in _TURNED else a)
        arrays[f"in_{name}_dram"] = a
        args.append(nc.dram_tensor(f"in_{name}_dram", a.shape, _mybir.dt.from_np(a.dtype), kind="ExternalInput").ap())
    args.append(nc.dram_tensor("out_0_dram", (N, C), F32, kind="ExternalOutput").ap())
    gnn_program(nc, *args)
    r = _run(nc, [arrays], core_ids=[0])
    return r.results[0]["out_0_dram"]
```
